# Optimizing a Trainium2 kernel written in Bass

```python
import numpy as np
import jax
import jax.numpy as jnp

def _softmax(x, axis=-1):
    return jax.nn.softmax(x, axis=axis)

def _gelu(x):
    return jax.nn.gelu(x, approximate=True)

def _silu(x):
    return jax.nn.silu(x)

def _sigmoid(x):
    return jax.nn.sigmoid(x)

def _layernorm(x, axis=-1, eps=1e-05):
    m = jnp.mean(x, axis=axis, keepdims=True)
    v = jnp.var(x, axis=axis, keepdims=True)
    return (x - m) / jnp.sqrt(v + eps)

def _scatter_add(tgt, idx, src, axis=0):
    return tgt.at[idx].add(src)

def _segment_sum(src, seg, n):
    return jax.ops.segment_sum(src, seg, n)
kernel_name = 'mk_xattn_seq_d4_seqx_r8_802b1a'

def setup_inputs(seed: int=0):
    np.random.seed(seed)
    _w = jnp.asarray

    def _rec_inputs():
        import jax
        import jax.numpy as jnp
        _rk = jax.random.key(seed)
        x = -0.0003929 + 0.9999 * jax.random.normal(jax.random.fold_in(_rk, 1), (16, 128, 256), jnp.float32)
        _lenS = 128 - jax.random.randint(jax.random.fold_in(_rk, 7), (16,), 0, max(1, 128 // 4) + 1, jnp.int32)
        _lenS2 = 128 - jax.random.randint(jax.random.fold_in(_rk, 8), (16,), 0, max(1, 128 // 4) + 1, jnp.int32)
        _ctx_2048P = jax.random.normal(jax.random.fold_in(_rk, 11), (16, 16, 256), jnp.float32)
        _ctx_2048c = jax.random.dirichlet(jax.random.fold_in(_rk, 511), 0.3 * jnp.ones((16,), jnp.float32), (16, 128))
        _ctx_2048t = jnp.einsum('bsk,bkd->bsd', _ctx_2048c, _ctx_2048P)
        _ctx_2048t = _ctx_2048t * jax.lax.rsqrt(jnp.mean(jnp.square(_ctx_2048t)) + 1e-12) * 0.953939
        ctx_2048 = 2.81802e-05 + 1.00001 * (_ctx_2048t + 0.3 * jax.random.normal(jax.random.fold_in(_rk, 611), (16, 128, 256), jnp.float32))
        _validS = jnp.arange(128)[None, :] < _lenS[:, None]
        _validS2 = jnp.arange(128)[None, :] < _lenS2[:, None]
        _causal = jnp.tril(jnp.ones((128, 128), dtype=bool))
        mask_1x1xSxS2_fc1 = jnp.where(jnp.broadcast_to(_validS2[0:1, None, None, :], (1, 1, 128, 128)), 1.0, 0.0).astype(jnp.float32)
        mask_Bx1xSxS2_ff1 = jnp.where(jnp.ones((16, 1, 128, 128), dtype=bool), 1.0, 0.0).astype(jnp.float32)
        mask_BxS2_ik0 = jnp.where(jnp.broadcast_to(_validS2[:, :], (16, 128)), 0, 1).astype(jnp.int32)
        return (x, ctx_2048, mask_1x1xSxS2_fc1, mask_Bx1xSxS2_ff1, mask_BxS2_ik0)
    x, ctx_2048, mask_1x1xSxS2_fc1, mask_Bx1xSxS2_ff1, mask_BxS2_ik0 = _rec_inputs()

    def _L0_xattn_setup():
        import jax, jax.numpy as jnp
        import numpy as np
        B, C1, C2, N = (8, 128, 128, 256)
        D = C2 // 8
        key = jax.random.key(seed)
        ks = jax.random.split(key, 8)
        s1 = 1.0 / np.sqrt(C1)
        s2 = 1.0 / np.sqrt(C2)
        return {'x1': jax.random.normal(ks[0], (B, C1, N), jnp.float32), 'x2': jax.random.normal(ks[1], (B, C2, N), jnp.float32), 'Wq': jax.random.uniform(ks[2], (D, C1), jnp.float32, -s1, s1), 'bq': jax.random.uniform(ks[3], (D,), jnp.float32, -s1, s1), 'Wk': jax.random.uniform(ks[4], (D, C2), jnp.float32, -s2, s2), 'bk': jax.random.uniform(ks[5], (D,), jnp.float32, -s2, s2), 'Wv': jax.random.uniform(ks[6], (C1, C2), jnp.float32, -s2, s2), 'bv': jax.random.uniform(ks[7], (C1,), jnp.float32, -s2, s2)}
    _L0_xattn_all = _L0_xattn_setup()
    _L0_xattn_in = {k: v for k, v in _L0_xattn_all.items() if k in ('Wq', 'bq', 'Wk', 'bk', 'Wv', 'bv')}
    del _L0_xattn_all

    def _L1_xattn_setup():
        import jax, jax.numpy as jnp
        import numpy as np
        H = 256
        NH = 16
        HD = H // NH
        EPS = 1e-05

        def gelu(x):
            return 0.5 * x * (1.0 + jnp.tanh(0.7978845608028654 * x * (1.0 + 0.044715 * x * x)))

        def layernorm(x, scale, bias):
            m = jnp.mean(x, axis=-1, keepdims=True)
            v = jnp.mean(jnp.square(x - m), axis=-1, keepdims=True)
            return (x - m) * jax.lax.rsqrt(v + EPS) * scale + bias

        def split_heads(x):
            b, s, _ = x.shape
            return x.reshape(b, s, NH, HD).transpose(0, 2, 1, 3)

        def merge_heads(x):
            b, nh, s, hd = x.shape
            return x.transpose(0, 2, 1, 3).reshape(b, s, nh * hd)

        def attention(q, k, v, mask):
            scores = jnp.einsum('bhqd,bhkd->bhqk', q, k) / jnp.sqrt(jnp.float32(HD))
            scores = scores * mask - 10000.0 * (1.0 - mask)
            probs = jax.nn.softmax(scores, axis=-1)
            return jnp.einsum('bhqk,bhkd->bhqd', probs, v)
        key = jax.random.key(seed)
        ks = jax.random.split(key, 16)
        b, s, t = (2, 128, 128)
        w = lambda k, i, o: jax.random.normal(k, (i, o), jnp.float32) * 0.02
        inp = {'hidden_states': jax.random.normal(ks[0], (b, s, H), jnp.float32), 'encoder_states': jax.random.normal(ks[1], (b, t, H), jnp.float32), 'ltor_mask': jnp.tril(jnp.ones((1, 1, s, s), jnp.float32)), 'cross_mask': jnp.ones((b, 1, s, t), jnp.float32), 'ln1_s': jnp.ones((H,), jnp.float32), 'ln1_b': jnp.zeros((H,), jnp.float32), 'w_qkv': w(ks[2], H, 3 * H), 'b_qkv': jnp.zeros((3 * H,), jnp.float32), 'w_ao': w(ks[3], H, H), 'b_ao': jnp.zeros((H,), jnp.float32), 'ln2_s': jnp.ones((H,), jnp.float32), 'ln2_b': jnp.zeros((H,), jnp.float32), 'w_q': w(ks[4], H, H), 'b_q': jnp.zeros((H,), jnp.float32), 'w_kv': w(ks[5], H, 2 * H), 'b_kv': jnp.zeros((2 * H,), jnp.float32), 'w_co': w(ks[6], H, H), 'b_co': jnp.zeros((H,), jnp.float32), 'ln3_s': jnp.ones((H,), jnp.float32), 'ln3_b': jnp.zeros((H,), jnp.float32), 'w1': w(ks[7], H, 4 * H), 'b1': jnp.zeros((4 * H,), jnp.float32), 'w2': w(ks[8], 4 * H, H), 'b2': jnp.zeros((H,), jnp.float32)}
        return inp
    _L1_xattn_all = _L1_xattn_setup()
    _L1_xattn_in = {k: v for k, v in _L1_xattn_all.items() if k in ('ln1_s', 'ln1_b', 'w_qkv', 'b_qkv', 'w_ao', 'b_ao', 'ln2_s', 'ln2_b', 'w_q', 'b_q', 'w_kv', 'b_kv', 'w_co', 'b_co', 'ln3_s', 'ln3_b', 'w1', 'b1', 'w2', 'b2')}
    del _L1_xattn_all

    def _L2_xattn_setup():
        import jax, jax.numpy as jnp
        import numpy as np
        B, P, K, H, NH = (4, 256, 32, 256, 16)
        DH = H // NH
        EPS = 1e-06

        def rmsnorm(x, w):
            var = jnp.mean(jnp.square(x), axis=-1, keepdims=True)
            return x * jax.lax.rsqrt(var + EPS) * w
        key = jax.random.key(seed)
        ks = jax.random.split(key, 12)
        s = 0.02
        return {'x': jax.random.normal(ks[0], (B, P, H), jnp.float32), 'latents': jax.random.normal(ks[1], (B, K, H), jnp.float32), 'attention_mask': jax.random.randint(ks[2], (B, P), 0, 2, jnp.int32), 'q_w': s * jax.random.normal(ks[3], (H, H), jnp.float32), 'q_b': jnp.zeros((H,), jnp.float32), 'kv_w': s * jax.random.normal(ks[4], (H, 2 * H), jnp.float32), 'kv_b': jnp.zeros((2 * H,), jnp.float32), 'out_w': s * jax.random.normal(ks[5], (H, H), jnp.float32), 'out_b': jnp.zeros((H,), jnp.float32), 'postnorm_w': jnp.ones((H,), jnp.float32), 'mlp_w1': s * jax.random.normal(ks[6], (H, 4 * H), jnp.float32), 'mlp_b1': jnp.zeros((4 * H,), jnp.float32), 'mlp_w2': s * jax.random.normal(ks[7], (4 * H, H), jnp.float32), 'mlp_b2': jnp.zeros((H,), jnp.float32)}
    _L2_xattn_all = _L2_xattn_setup()
    _L2_xattn_in = {k: v for k, v in _L2_xattn_all.items() if k in ('q_w', 'q_b', 'kv_w', 'kv_b', 'out_w', 'out_b', 'postnorm_w', 'mlp_w1', 'mlp_b1', 'mlp_w2', 'mlp_b2')}
    del _L2_xattn_all

    def _L3_xattn_setup():
        import jax, jax.numpy as jnp
        import numpy as np
        B, Q, S1, S2 = (4, 32, 256, 256)
        D, H, K, F = (256, 16, 128, 1024)
        LN_EPS = 1e-05

        def _layer_norm(x, scale, offset):
            mu = jnp.mean(x, axis=-1, keepdims=True)
            var = jnp.var(x, axis=-1, keepdims=True)
            return (x - mu) * jax.lax.rsqrt(var + LN_EPS) * scale + offset

        def _cross_attention(q_in, kv_in, wq, bq, wk, bk, wv, bv, wo, bo, bias_k, bias_v):
            b, q_len, _ = q_in.shape
            t = kv_in.shape[1]
            qh = (q_in @ wq + bq).reshape(b, q_len, H, K)
            kh = (kv_in @ wk + bk).reshape(b, t, H, K)
            vh = (kv_in @ wv + bv).reshape(b, t, H, K)
            kh = jnp.concatenate([kh, jnp.broadcast_to(bias_k, (b, 1, H, K))], axis=1)
            vh = jnp.concatenate([vh, jnp.broadcast_to(bias_v, (b, 1, H, K))], axis=1)
            scale = jnp.sqrt(jnp.asarray(K, q_in.dtype))
            logits = jnp.einsum('bqhk,bthk->bhqt', qh, kh) / scale
            weights = jax.nn.softmax(logits, axis=-1)
            ctx = jnp.einsum('bhqt,bthk->bqhk', weights, vh).reshape(b, q_len, H * K)
            return ctx @ wo + bo

        def _forward(x, xf_1, xf_2, ln1_scale, ln1_offset, wq1, bq1, wk1, bk1, wv1, bv1, wo1, bo1, bias_k1, bias_v1, ln2_scale, ln2_offset, wq2, bq2, wk2, bk2, wv2, bv2, wo2, bo2, bias_k2, bias_v2, ln_mlp_scale, ln_mlp_offset, w_fc1, b_fc1, w_fc2, b_fc2):
            res = x
            h = _layer_norm(x, ln1_scale, ln1_offset)
            x = res + _cross_attention(h, xf_1, wq1, bq1, wk1, bk1, wv1, bv1, wo1, bo1, bias_k1, bias_v1)
            res = x
            h = _layer_norm(x, ln2_scale, ln2_offset)
            x = res + _cross_attention(h, xf_2, wq2, bq2, wk2, bk2, wv2, bv2, wo2, bo2, bias_k2, bias_v2)
            h = _layer_norm(x, ln_mlp_scale, ln_mlp_offset)
            h = jax.nn.gelu(h @ w_fc1 + b_fc1, approximate=False) @ w_fc2 + b_fc2
            return x + h
        key = jax.random.key(seed)
        ks = iter(jax.random.split(key, 64))

        def rn(shape, s=0.02):
            return jax.random.normal(next(ks), shape, jnp.float32) * s
        inp = {'x': rn((B, Q, D), 1.0), 'xf_1': rn((B, S1, D), 1.0), 'xf_2': rn((B, S2, D), 1.0)}
        for i in (1, 2):
            inp[f'ln{i}_scale'] = jnp.ones((D,), jnp.float32)
            inp[f'ln{i}_offset'] = jnp.zeros((D,), jnp.float32)
            inp[f'wq{i}'] = rn((D, H * K))
            inp[f'bq{i}'] = jnp.zeros((H * K,), jnp.float32)
            inp[f'wk{i}'] = rn((D, H * K))
            inp[f'bk{i}'] = jnp.zeros((H * K,), jnp.float32)
            inp[f'wv{i}'] = rn((D, H * K))
            inp[f'bv{i}'] = jnp.zeros((H * K,), jnp.float32)
            inp[f'wo{i}'] = rn((H * K, D))
            inp[f'bo{i}'] = jnp.zeros((D,), jnp.float32)
            inp[f'bias_k{i}'] = rn((1, 1, H, K))
            inp[f'bias_v{i}'] = rn((1, 1, H, K))
        inp['ln_mlp_scale'] = jnp.ones((D,), jnp.float32)
        inp['ln_mlp_offset'] = jnp.zeros((D,), jnp.float32)
        inp['w_fc1'] = rn((D, F))
        inp['b_fc1'] = jnp.zeros((F,), jnp.float32)
        inp['w_fc2'] = rn((F, D))
        inp['b_fc2'] = jnp.zeros((D,), jnp.float32)
        return inp
    _L3_xattn_all = _L3_xattn_setup()
    _L3_xattn_in = {k: v for k, v in _L3_xattn_all.items() if k in ('ln1_scale', 'ln1_offset', 'wq1', 'bq1', 'wk1', 'bk1', 'wv1', 'bv1', 'wo1', 'bo1', 'bias_k1', 'bias_v1', 'ln2_scale', 'ln2_offset', 'wq2', 'bq2', 'wk2', 'bk2', 'wv2', 'bv2', 'wo2', 'bo2', 'bias_k2', 'bias_v2', 'ln_mlp_scale', 'ln_mlp_offset', 'w_fc1', 'b_fc1', 'w_fc2', 'b_fc2')}
    del _L3_xattn_all
    return {'x': x, 'ctx_2048': ctx_2048, 'mask_1x1xSxS2_fc1': mask_1x1xSxS2_fc1, 'mask_Bx1xSxS2_ff1': mask_Bx1xSxS2_ff1, 'mask_BxS2_ik0': mask_BxS2_ik0, 'L0_xattn_Wq': _L0_xattn_in['Wq'], 'L0_xattn_bq': _L0_xattn_in['bq'], 'L0_xattn_Wk': _L0_xattn_in['Wk'], 'L0_xattn_bk': _L0_xattn_in['bk'], 'L0_xattn_Wv': _L0_xattn_in['Wv'], 'L0_xattn_bv': _L0_xattn_in['bv'], 'L1_xattn_ln1_s': _L1_xattn_in['ln1_s'], 'L1_xattn_ln1_b': _L1_xattn_in['ln1_b'], 'L1_xattn_w_qkv': _L1_xattn_in['w_qkv'], 'L1_xattn_b_qkv': _L1_xattn_in['b_qkv'], 'L1_xattn_w_ao': _L1_xattn_in['w_ao'], 'L1_xattn_b_ao': _L1_xattn_in['b_ao'], 'L1_xattn_ln2_s': _L1_xattn_in['ln2_s'], 'L1_xattn_ln2_b': _L1_xattn_in['ln2_b'], 'L1_xattn_w_q': _L1_xattn_in['w_q'], 'L1_xattn_b_q': _L1_xattn_in['b_q'], 'L1_xattn_w_kv': _L1_xattn_in['w_kv'], 'L1_xattn_b_kv': _L1_xattn_in['b_kv'], 'L1_xattn_w_co': _L1_xattn_in['w_co'], 'L1_xattn_b_co': _L1_xattn_in['b_co'], 'L1_xattn_ln3_s': _L1_xattn_in['ln3_s'], 'L1_xattn_ln3_b': _L1_xattn_in['ln3_b'], 'L1_xattn_w1': _L1_xattn_in['w1'], 'L1_xattn_b1': _L1_xattn_in['b1'], 'L1_xattn_w2': _L1_xattn_in['w2'], 'L1_xattn_b2': _L1_xattn_in['b2'], 'L2_xattn_q_w': _L2_xattn_in['q_w'], 'L2_xattn_q_b': _L2_xattn_in['q_b'], 'L2_xattn_kv_w': _L2_xattn_in['kv_w'], 'L2_xattn_kv_b': _L2_xattn_in['kv_b'], 'L2_xattn_out_w': _L2_xattn_in['out_w'], 'L2_xattn_out_b': _L2_xattn_in['out_b'], 'L2_xattn_postnorm_w': _L2_xattn_in['postnorm_w'], 'L2_xattn_mlp_w1': _L2_xattn_in['mlp_w1'], 'L2_xattn_mlp_b1': _L2_xattn_in['mlp_b1'], 'L2_xattn_mlp_w2': _L2_xattn_in['mlp_w2'], 'L2_xattn_mlp_b2': _L2_xattn_in['mlp_b2'], 'L3_xattn_ln1_scale': _L3_xattn_in['ln1_scale'], 'L3_xattn_ln1_offset': _L3_xattn_in['ln1_offset'], 'L3_xattn_wq1': _L3_xattn_in['wq1'], 'L3_xattn_bq1': _L3_xattn_in['bq1'], 'L3_xattn_wk1': _L3_xattn_in['wk1'], 'L3_xattn_bk1': _L3_xattn_in['bk1'], 'L3_xattn_wv1': _L3_xattn_in['wv1'], 'L3_xattn_bv1': _L3_xattn_in['bv1'], 'L3_xattn_wo1': _L3_xattn_in['wo1'], 'L3_xattn_bo1': _L3_xattn_in['bo1'], 'L3_xattn_bias_k1': _L3_xattn_in['bias_k1'], 'L3_xattn_bias_v1': _L3_xattn_in['bias_v1'], 'L3_xattn_ln2_scale': _L3_xattn_in['ln2_scale'], 'L3_xattn_ln2_offset': _L3_xattn_in['ln2_offset'], 'L3_xattn_wq2': _L3_xattn_in['wq2'], 'L3_xattn_bq2': _L3_xattn_in['bq2'], 'L3_xattn_wk2': _L3_xattn_in['wk2'], 'L3_xattn_bk2': _L3_xattn_in['bk2'], 'L3_xattn_wv2': _L3_xattn_in['wv2'], 'L3_xattn_bv2': _L3_xattn_in['bv2'], 'L3_xattn_wo2': _L3_xattn_in['wo2'], 'L3_xattn_bo2': _L3_xattn_in['bo2'], 'L3_xattn_bias_k2': _L3_xattn_in['bias_k2'], 'L3_xattn_bias_v2': _L3_xattn_in['bias_v2'], 'L3_xattn_ln_mlp_scale': _L3_xattn_in['ln_mlp_scale'], 'L3_xattn_ln_mlp_offset': _L3_xattn_in['ln_mlp_offset'], 'L3_xattn_w_fc1': _L3_xattn_in['w_fc1'], 'L3_xattn_b_fc1': _L3_xattn_in['b_fc1'], 'L3_xattn_w_fc2': _L3_xattn_in['w_fc2'], 'L3_xattn_b_fc2': _L3_xattn_in['b_fc2']}

def reference(x, ctx_2048, mask_1x1xSxS2_fc1, mask_Bx1xSxS2_ff1, mask_BxS2_ik0, L0_xattn_Wq, L0_xattn_bq, L0_xattn_Wk, L0_xattn_bk, L0_xattn_Wv, L0_xattn_bv, L1_xattn_ln1_s, L1_xattn_ln1_b, L1_xattn_w_qkv, L1_xattn_b_qkv, L1_xattn_w_ao, L1_xattn_b_ao, L1_xattn_ln2_s, L1_xattn_ln2_b, L1_xattn_w_q, L1_xattn_b_q, L1_xattn_w_kv, L1_xattn_b_kv, L1_xattn_w_co, L1_xattn_b_co, L1_xattn_ln3_s, L1_xattn_ln3_b, L1_xattn_w1, L1_xattn_b1, L1_xattn_w2, L1_xattn_b2, L2_xattn_q_w, L2_xattn_q_b, L2_xattn_kv_w, L2_xattn_kv_b, L2_xattn_out_w, L2_xattn_out_b, L2_xattn_postnorm_w, L2_xattn_mlp_w1, L2_xattn_mlp_b1, L2_xattn_mlp_w2, L2_xattn_mlp_b2, L3_xattn_ln1_scale, L3_xattn_ln1_offset, L3_xattn_wq1, L3_xattn_bq1, L3_xattn_wk1, L3_xattn_bk1, L3_xattn_wv1, L3_xattn_bv1, L3_xattn_wo1, L3_xattn_bo1, L3_xattn_bias_k1, L3_xattn_bias_v1, L3_xattn_ln2_scale, L3_xattn_ln2_offset, L3_xattn_wq2, L3_xattn_bq2, L3_xattn_wk2, L3_xattn_bk2, L3_xattn_wv2, L3_xattn_bv2, L3_xattn_wo2, L3_xattn_bo2, L3_xattn_bias_k2, L3_xattn_bias_v2, L3_xattn_ln_mlp_scale, L3_xattn_ln_mlp_offset, L3_xattn_w_fc1, L3_xattn_b_fc1, L3_xattn_w_fc2, L3_xattn_b_fc2):
    import jax
    import jax.numpy as jnp

    def _L0_xattn_ref(x1, x2, Wq, bq, Wk, bk, Wv, bv):
        import jax, jax.numpy as jnp
        import numpy as np
        B, C1, C2, N = (8, 128, 128, 256)
        D = C2 // 8
        q = jnp.einsum('bcn,dc->bnd', x1, Wq) + bq
        k = jnp.einsum('bcn,dc->bdn', x2, Wk) + bk[:, None]
        v = jnp.einsum('bcn,dc->bdn', x2, Wv) + bv[:, None]
        attn = jax.nn.softmax(jnp.einsum('bnd,bdm->bnm', q, k), axis=2)
        attn_out = jnp.einsum('bcm,bnm->bcn', v, attn)
        return attn_out + x1

    def _L1_xattn_ref(hidden_states, encoder_states, ltor_mask, cross_mask, ln1_s, ln1_b, w_qkv, b_qkv, w_ao, b_ao, ln2_s, ln2_b, w_q, b_q, w_kv, b_kv, w_co, b_co, ln3_s, ln3_b, w1, b1, w2, b2):
        import jax, jax.numpy as jnp
        import numpy as np
        H = 256
        NH = 16
        HD = H // NH
        EPS = 1e-05

        def gelu(x):
            return 0.5 * x * (1.0 + jnp.tanh(0.7978845608028654 * x * (1.0 + 0.044715 * x * x)))

        def layernorm(x, scale, bias):
            m = jnp.mean(x, axis=-1, keepdims=True)
            v = jnp.mean(jnp.square(x - m), axis=-1, keepdims=True)
            return (x - m) * jax.lax.rsqrt(v + EPS) * scale + bias

        def split_heads(x):
            b, s, _ = x.shape
            return x.reshape(b, s, NH, HD).transpose(0, 2, 1, 3)

        def merge_heads(x):
            b, nh, s, hd = x.shape
            return x.transpose(0, 2, 1, 3).reshape(b, s, nh * hd)

        def attention(q, k, v, mask):
            scores = jnp.einsum('bhqd,bhkd->bhqk', q, k) / jnp.sqrt(jnp.float32(HD))
            scores = scores * mask - 10000.0 * (1.0 - mask)
            probs = jax.nn.softmax(scores, axis=-1)
            return jnp.einsum('bhqk,bhkd->bhqd', probs, v)
        ln_out = layernorm(hidden_states, ln1_s, ln1_b)
        qkv = ln_out @ w_qkv + b_qkv
        q, k, v = jnp.split(qkv, 3, axis=-1)
        ctx = merge_heads(attention(split_heads(q), split_heads(k), split_heads(v), ltor_mask))
        attn_out = ctx @ w_ao + b_ao
        x = hidden_states + attn_out
        ln_out = layernorm(x, ln2_s, ln2_b)
        q = ln_out @ w_q + b_q
        kv = encoder_states @ w_kv + b_kv
        k, v = jnp.split(kv, 2, axis=-1)
        ctx = merge_heads(attention(split_heads(q), split_heads(k), split_heads(v), cross_mask))
        cross_out = ctx @ w_co + b_co
        x = x + cross_out
        ln_out = layernorm(x, ln3_s, ln3_b)
        mlp_out = gelu(ln_out @ w1 + b1) @ w2 + b2
        return x + mlp_out

    def _L2_xattn_ref(x, latents, attention_mask, q_w, q_b, kv_w, kv_b, out_w, out_b, postnorm_w, mlp_w1, mlp_b1, mlp_w2, mlp_b2):
        import jax, jax.numpy as jnp
        import numpy as np
        B, P, K, H, NH = (4, 256, 32, 256, 16)
        DH = H // NH
        EPS = 1e-06

        def rmsnorm(x, w):
            var = jnp.mean(jnp.square(x), axis=-1, keepdims=True)
            return x * jax.lax.rsqrt(var + EPS) * w
        b, p, _ = x.shape
        k_len = latents.shape[1]
        residual = latents
        h = jnp.concatenate([x, latents], axis=1)
        q = (latents @ q_w + q_b).reshape(b, k_len, NH, DH)
        kv = (h @ kv_w + kv_b).reshape(b, p + k_len, NH, DH, 2)
        kmat, v = (kv[..., 0], kv[..., 1])
        attn = jnp.einsum('bkhd,bnhd->bhkn', q, kmat) / DH
        full_mask = jnp.concatenate([attention_mask.astype(bool), jnp.ones((b, k_len), bool)], axis=-1)
        attn = jnp.where(full_mask[:, None, None, :], attn, -jnp.inf)
        attn = jax.nn.softmax(attn.astype(jnp.float32), axis=-1).astype(q.dtype)
        attn_out = jnp.einsum('bhkn,bnhd->bkhd', attn, v).reshape(b, k_len, H)
        attn_out = attn_out @ out_w + out_b + residual
        out = rmsnorm(attn_out, postnorm_w)
        out = jax.nn.gelu(out @ mlp_w1 + mlp_b1) @ mlp_w2 + mlp_b2
        return out + residual

    def _L3_xattn_ref(x, xf_1, xf_2, ln1_scale, ln1_offset, wq1, bq1, wk1, bk1, wv1, bv1, wo1, bo1, bias_k1, bias_v1, ln2_scale, ln2_offset, wq2, bq2, wk2, bk2, wv2, bv2, wo2, bo2, bias_k2, bias_v2, ln_mlp_scale, ln_mlp_offset, w_fc1, b_fc1, w_fc2, b_fc2):
        import jax, jax.numpy as jnp
        import numpy as np
        B, Q, S1, S2 = (4, 32, 256, 256)
        D, H, K, F = (256, 16, 128, 1024)
        LN_EPS = 1e-05

        def _layer_norm(x, scale, offset):
            mu = jnp.mean(x, axis=-1, keepdims=True)
            var = jnp.var(x, axis=-1, keepdims=True)
            return (x - mu) * jax.lax.rsqrt(var + LN_EPS) * scale + offset

        def _cross_attention(q_in, kv_in, wq, bq, wk, bk, wv, bv, wo, bo, bias_k, bias_v):
            b, q_len, _ = q_in.shape
            t = kv_in.shape[1]
            qh = (q_in @ wq + bq).reshape(b, q_len, H, K)
            kh = (kv_in @ wk + bk).reshape(b, t, H, K)
            vh = (kv_in @ wv + bv).reshape(b, t, H, K)
            kh = jnp.concatenate([kh, jnp.broadcast_to(bias_k, (b, 1, H, K))], axis=1)
            vh = jnp.concatenate([vh, jnp.broadcast_to(bias_v, (b, 1, H, K))], axis=1)
            scale = jnp.sqrt(jnp.asarray(K, q_in.dtype))
            logits = jnp.einsum('bqhk,bthk->bhqt', qh, kh) / scale
            weights = jax.nn.softmax(logits, axis=-1)
            ctx = jnp.einsum('bhqt,bthk->bqhk', weights, vh).reshape(b, q_len, H * K)
            return ctx @ wo + bo

        def _forward(x, xf_1, xf_2, ln1_scale, ln1_offset, wq1, bq1, wk1, bk1, wv1, bv1, wo1, bo1, bias_k1, bias_v1, ln2_scale, ln2_offset, wq2, bq2, wk2, bk2, wv2, bv2, wo2, bo2, bias_k2, bias_v2, ln_mlp_scale, ln_mlp_offset, w_fc1, b_fc1, w_fc2, b_fc2):
            res = x
            h = _layer_norm(x, ln1_scale, ln1_offset)
            x = res + _cross_attention(h, xf_1, wq1, bq1, wk1, bk1, wv1, bv1, wo1, bo1, bias_k1, bias_v1)
            res = x
            h = _layer_norm(x, ln2_scale, ln2_offset)
            x = res + _cross_attention(h, xf_2, wq2, bq2, wk2, bk2, wv2, bv2, wo2, bo2, bias_k2, bias_v2)
            h = _layer_norm(x, ln_mlp_scale, ln_mlp_offset)
            h = jax.nn.gelu(h @ w_fc1 + b_fc1, approximate=False) @ w_fc2 + b_fc2
            return x + h
        return _forward(x, xf_1, xf_2, ln1_scale, ln1_offset, wq1, bq1, wk1, bk1, wv1, bv1, wo1, bo1, bias_k1, bias_v1, ln2_scale, ln2_offset, wq2, bq2, wk2, bk2, wv2, bv2, wo2, bo2, bias_k2, bias_v2, ln_mlp_scale, ln_mlp_offset, w_fc1, b_fc1, w_fc2, b_fc2)
    x = _L0_xattn_ref(x, ctx_2048, L0_xattn_Wq, L0_xattn_bq, L0_xattn_Wk, L0_xattn_bk, L0_xattn_Wv, L0_xattn_bv)
    x = _L1_xattn_ref(x, ctx_2048, mask_1x1xSxS2_fc1, mask_Bx1xSxS2_ff1, L1_xattn_ln1_s, L1_xattn_ln1_b, L1_xattn_w_qkv, L1_xattn_b_qkv, L1_xattn_w_ao, L1_xattn_b_ao, L1_xattn_ln2_s, L1_xattn_ln2_b, L1_xattn_w_q, L1_xattn_b_q, L1_xattn_w_kv, L1_xattn_b_kv, L1_xattn_w_co, L1_xattn_b_co, L1_xattn_ln3_s, L1_xattn_ln3_b, L1_xattn_w1, L1_xattn_b1, L1_xattn_w2, L1_xattn_b2)
    x = _L2_xattn_ref(ctx_2048, x, mask_BxS2_ik0, L2_xattn_q_w, L2_xattn_q_b, L2_xattn_kv_w, L2_xattn_kv_b, L2_xattn_out_w, L2_xattn_out_b, L2_xattn_postnorm_w, L2_xattn_mlp_w1, L2_xattn_mlp_b1, L2_xattn_mlp_w2, L2_xattn_mlp_b2)
    x = _L3_xattn_ref(x, ctx_2048, ctx_2048, L3_xattn_ln1_scale, L3_xattn_ln1_offset, L3_xattn_wq1, L3_xattn_bq1, L3_xattn_wk1, L3_xattn_bk1, L3_xattn_wv1, L3_xattn_bv1, L3_xattn_wo1, L3_xattn_bo1, L3_xattn_bias_k1, L3_xattn_bias_v1, L3_xattn_ln2_scale, L3_xattn_ln2_offset, L3_xattn_wq2, L3_xattn_bq2, L3_xattn_wk2, L3_xattn_bk2, L3_xattn_wv2, L3_xattn_bv2, L3_xattn_wo2, L3_xattn_bo2, L3_xattn_bias_k2, L3_xattn_bias_v2, L3_xattn_ln_mlp_scale, L3_xattn_ln_mlp_offset, L3_xattn_w_fc1, L3_xattn_b_fc1, L3_xattn_w_fc2, L3_xattn_b_fc2)
    return x

_drawn_inputs = setup_inputs


def setup_inputs(seed=0):
    import zlib

    import numpy as np

    out = dict(_drawn_inputs(seed))
    spreads = {'L1_xattn_ln1_s': (1.0, 0.6),
     'L1_xattn_ln1_b': (0.0, 0.8),
     'L1_xattn_b_qkv': (0.0, 0.284),
     'L1_xattn_b_ao': (0.0, 0.1),
     'L1_xattn_ln2_s': (1.0, 0.6),
     'L1_xattn_ln2_b': (0.0, 2.0),
     'L1_xattn_b_q': (0.0, 2.0),
     'L1_xattn_b_kv': (0.0, 0.282),
     'L1_xattn_b_co': (0.0, 0.1),
     'L1_xattn_ln3_s': (1.0, 0.6),
     'L1_xattn_ln3_b': (0.0, 0.8),
     'L1_xattn_b1': (0.0, 0.1),
     'L1_xattn_b2': (0.0, 0.1),
     'L2_xattn_q_b': (0.0, 0.8),
     'L2_xattn_kv_b': (0.0, 0.8),
     'L2_xattn_out_b': (0.0, 2.0),
     'L2_xattn_postnorm_w': (1.0, 0.6),
     'L2_xattn_mlp_b1': (0.0, 0.1),
     'L2_xattn_mlp_b2': (0.0, 0.1),
     'L3_xattn_ln1_scale': (1.0, 0.6),
     'L3_xattn_ln1_offset': (0.0, 0.8),
     'L3_xattn_bq1': (0.0, 0.8),
     'L3_xattn_bk1': (0.0, 2.0),
     'L3_xattn_bv1': (0.0, 0.1),
     'L3_xattn_bo1': (0.0, 0.1),
     'L3_xattn_ln2_scale': (1.0, 0.6),
     'L3_xattn_ln2_offset': (0.0, 0.8),
     'L3_xattn_bq2': (0.0, 0.8),
     'L3_xattn_bk2': (0.0, 2.0),
     'L3_xattn_bv2': (0.0, 0.1),
     'L3_xattn_bo2': (0.0, 0.1),
     'L3_xattn_ln_mlp_scale': (1.0, 0.6),
     'L3_xattn_ln_mlp_offset': (0.0, 0.8),
     'L3_xattn_b_fc1': (0.0, 0.303),
     'L3_xattn_b_fc2': (0.0, 0.1)}
    factors = {'L0_xattn_bq': 2.902,
     'L0_xattn_bk': 64.0,
     'L1_xattn_w_qkv': 4.501,
     'L1_xattn_w_q': 8.0,
     'L2_xattn_q_w': 8.0,
     'L2_xattn_kv_w': 8.0,
     'L2_xattn_out_w': 8.0,
     'L3_xattn_wq1': 8.0,
     'L3_xattn_wk1': 8.0,
     'L3_xattn_bias_k1': 64.0,
     'L3_xattn_bias_v1': 64.0,
     'L3_xattn_wq2': 8.0,
     'L3_xattn_wk2': 8.0,
     'L3_xattn_bias_k2': 64.0,
     'L3_xattn_bias_v2': 64.0}
    for name, (base, spread) in spreads.items():
        noise = np.random.default_rng([zlib.crc32(name.encode()), seed]).standard_normal(out[name].shape)
        drawn = base * np.exp(spread * noise) if base else spread * noise
        out[name] = jnp.asarray(drawn.astype(out[name].dtype))
    for name, factor in factors.items():
        out[name] = (out[name] * factor).astype(out[name].dtype)
    return out
```

```python
import numpy as np

import concourse.bass as bass
from concourse import mybir
from contextlib import ExitStack

F32 = mybir.dt.float32
I32 = mybir.dt.int32
ALU = mybir.AluOpType
ACT = mybir.ActivationFunctionType
AX = mybir.AxisListType

P = 128
B = 16
D = 256
KC = D // P
NB = 4
G = B // NB
R = NB * P
NH = 16
HD = D // NH
HPC = P // HD
F = 1024
FC = F // P
BANK = 512
L0K = 16
W3 = 128
PAIRS = NH // 2

COLS = {}
for _name, _n in [("bq0", 1), ("bk0", 1), ("bv0", 1),
                  ("ln1_s", 2), ("ln1_b", 2), ("ln2_s", 2), ("ln2_b", 2), ("ln3_s", 2), ("ln3_b", 2),
                  ("self_bq", 2), ("self_bk", 2), ("self_bv", 2),
                  ("cross_bq", 2), ("cross_bk", 2), ("cross_bv", 2), ("mlp1_b", FC),
                  ("lat_bq", 2), ("lat_bk", 2), ("lat_bv", 2), ("rms_w", 2), ("mlp2_b", FC),
                  ("lnA_s", 2), ("lnA_b", 2), ("lnB_s", 2), ("lnB_b", 2), ("lnM_s", 2), ("lnM_b", 2),
                  ("mlp3_b", FC), ("head_mask", HPC)]:
    COLS[_name] = (sum(n for _, n in COLS.values()), _n)
NCOLS = sum(n for _, n in COLS.values())

ROWS_A = ["self_bo", "cross_bo", "mlp1_bo", "lat_bo", "mlp2_bo"]
ROWS_B = ["a_bo", "b_bo", "mlp3_bo"]

WEIGHTS_A = [("wq0", 1, P), ("wk0", 1, P), ("wv0", 1, P),
             ("self_q", KC, D), ("self_k", KC, D), ("self_v", KC, D), ("self_o", KC, D),
             ("cross_k", KC, D), ("cross_v", KC, D), ("cross_q", KC, D), ("cross_o", KC, D),
             ("mlp1_up", KC, F), ("mlp1_down", FC, D),
             ("lat_q", KC, D), ("lat_k", KC, D), ("lat_v", KC, D), ("lat_o", KC, D),
             ("mlp2_up", KC, F), ("mlp2_down", FC, D)]

NEG = -1.0e30
RSQRT_MAGIC = 1597463007.0
UNITS = {"chan": NB, "self": 4 * NB, "cross": 4 * NB, "lat": 8 * NB}
FIRST_UNIT = {"chan": 0, "self": 4, "cross": 20, "lat": 36}
NU = sum(UNITS.values())
BATCH_UNITS = {"chan": 1, "self": 4, "cross": 4, "lat": 8}
SCORES_AHEAD = 3

USES_A = ([("chan_q", i) for i in range(2)] + [("chan_k", i) for i in range(2)] + [("chan_v", i) for i in range(2)]
          + [("ln1", c) for c in range(KC)]
          + [("self_q", c) for c in range(KC)] + [("self_k", c) for c in range(KC)]
          + [("self_v", i) for i in range(2)] + [("self_o", b) for b in range(NB)]
          + [("cross_k", c) for c in range(KC)] + [("cross_v", i) for i in range(2)]
          + [("ln2", c) for c in range(KC)] + [("cross_q", c) for c in range(KC)]
          + [("cross_o", b) for b in range(NB)]
          + [("ctx_k", c) for c in range(KC)] + [("ctx_v", i) for i in range(2)]
          + [("ln3", c) for c in range(KC)]
          + [("mlp1_up", f) for f in range(FC)] + [("mlp1_down", i) for i in range(2)]
          + [("lat", c) for c in range(KC)]
          + [("lat_q", c) for c in range(KC)] + [("lat_k", c) for c in range(KC)]
          + [("lat_v", i) for i in range(2)] + [("lat_o", b) for b in range(NB)]
          + [("rms", c) for c in range(KC)]
          + [("mlp2_up", f) for f in range(FC)] + [("mlp2_down", i) for i in range(2)])

NEWTON_STEPS = 3
NORM_STEPS = 2 * NB + 1 + 2 + 3 * NEWTON_STEPS
MASKED_UNITS = UNITS["self"] + UNITS["cross"]
DVE_STEPS_A = 4 * NORM_STEPS + 1


def seed(eng, sems):
    for sem in sems:
        eng.sem_inc(sem, 1)


class Banks:

    def __init__(self, uses, banks, first=0):
        self.at = {key: ((first + i) % banks, (first + i) // banks) for i, key in enumerate(uses)}
        assert len(self.at) == len(uses)
        self.per_loop = [sum(b == k for b, _ in self.at.values()) for k in range(banks)]

    def __getitem__(self, key):
        return self.at[key]


def stages_0_to_2(nc, dram, consts):
    ident, cols = consts["ident"], consts["cols"]

    def col(name, c=0):
        at, n = COLS[name]
        assert c < n
        return cols[:, at + c:at + c + 1]

    with ExitStack() as ctx:
        def sb(name, shape, dt=F32):
            return ctx.enter_context(nc.sbuf_tensor(name, shape, dt))

        def sem(name):
            return ctx.enter_context(nc.semaphore(name))

        total = sum(k * n for _, k, n in WEIGHTS_A)
        weights = sb("weights_a", [P, total])
        w, at = {}, 0
        for name, k, n in WEIGHTS_A:
            w[name] = weights[:, at:at + k * n].rearrange("p (k n) -> p k n", k=k)
            at += k * n
        split = [0, 3 * P, at]
        rows = sb("rows_a", [P, len(ROWS_A), D])
        mask_self = sb("mask_self", [P, P])
        madd_self = sb("madd_self", [P, P])
        mask_cross = sb("mask_cross", [P, NB, P])
        madd_cross = sb("madd_cross", [P, NB, P])
        mask_lat = sb("mask_lat", [P, NB, P], I32)
        madd_lat = sb("madd_lat", [P, NB, 2 * P])

        x_in = sb("x_in", [P, NB, D])
        ctx_in = sb("ctx_in", [P, NB, D])
        ctxT = sb("ctxT", [P, KC, NB, P])
        X = sb("X", [P, NB, D])
        Xb = sb("Xb", [P, NB, D])
        xhat = sb("xhat", [P, NB, D])
        hT = sb("hT", [P, KC, R])
        qT = sb("qT", [P, KC, R])
        big = sb("big", [P, NH * R])
        qm = big[:, :].rearrange("p (h r) -> p h r", h=NH)
        upT = big[:, 0:FC * R].rearrange("p (f r) -> p f r", f=FC)
        q0T = big[:, 0:NB * D]
        k0T = big[:, NB * D:2 * NB * D]
        v0T = big[:, 2 * NB * D:3 * NB * D].rearrange("p (b m c) -> p b m c", b=NB, m=2)
        kT_self = sb("kT_self", [P, KC, R])
        v_self = sb("v_self", [P, NB, NH * 2 * HD])
        kT_lat = sb("kT_lat", [P, KC, NB, 2, P])
        v_lat = sb("v_lat", [P, 2, NB, NH * 2 * HD])
        masked = sb("masked", [P, 2, BANK])
        negated = sb("negated", [P, 3, BANK])
        probs = sb("probs", [P, 4, BANK])
        probsT = sb("probsT", [P, 2, BANK])
        oT = sb("oT", [P, KC, NB, P])
        negmax = sb("negmax", [P, 4, 4])
        sums = sb("sums", [P, 4, 4])
        rsums = sb("rsums", [P, 4, 4])
        stats = sb("stats", [P, NB, 6])
        mv = sb("mv", [P, NB, 2])
        var = sb("var", [P, NB])
        guess = sb("guess", [P, NB], I32)
        rstd = sb("rstd", [P, NB])
        newton = sb("newton", [P, NB])

        def bank(name):
            return ctx.enter_context(nc.psum_tensor(name, [P, BANK], F32))

        scores = [bank(f"scores{i}") for i in range(2)]
        pT_psum = [bank(f"pT_psum{i}") for i in range(2)]
        o_psum = bank("o_psum")
        general = [bank(f"general{i}") for i in range(3)]
        uses = Banks(USES_A, 3)

        s = {n: sem(n) for n in (
            "weights0_loaded", "weights_loaded", "rows_loaded", "mask_self_loaded", "x_loaded", "ctx_loaded",
            "ctxT_loaded", "mask_cross_loaded", "mask_lat_loaded", "mid_stored", "x_released",
            "v_zeroed", "madd_self_ready", "madd_cross_ready", "madd_lat_ready",
            "scores_ready", "scores_free", "max_ready", "exp_done", "rsum_ready", "probs_ready",
            "pT_ready", "pT_copied", "pv_done", "o_copied",
            "xb_ready", "xhat_ready", "qm_dve", "qm_act", "chan_done", "cross_done", "ctx_used", "dve_step", "wait_passed")}
        full = [sem(f"general_full{i}") for i in range(3)]
        free = [sem(f"general_free{i}") for i in range(3)]

        def wait_full(eng, g, key):
            k, n = uses[key]
            eng.wait_ge(full[k], g * uses.per_loop[k] + n + 2)
            return general[k], free[k]

        def wait_free(eng, g, key):
            k, n = uses[key]
            eng.wait_ge(free[k], g * uses.per_loop[k] + n + 1)
            return general[k], full[k]

        def wait_copied(eng, g, key):
            k, n = uses[key]
            eng.wait_ge(free[k], g * uses.per_loop[k] + n + 2)

        def wait_x(eng, g, after):
            if after == "chan":
                eng.wait_ge(s["chan_done"], g * NB + NB + 1)
            elif after.startswith("mlp"):
                for i in range(2):
                    wait_copied(eng, g, (after + "_down", i))
            else:
                for b in range(NB):
                    wait_copied(eng, g, (after + "_o", b))

        def unit_parts(kind, u):
            per = BATCH_UNITS[kind]
            b, i = divmod(u, per)
            return b, i, {"chan": 2, "self": 4, "cross": 4, "lat": 2}[kind]

        XHAT_AFTER = {"ln1": 4, "ln2": 8, "ln3": 12, "rms": 16}
        XB_AFTER = {"self": 1, "cross": 2, "mlp1": 3, "lat": 4, "mlp2": 5}
        ROW_OF = {"self": 0, "cross": 1, "mlp1": 2, "lat": 3, "mlp2": 4}

        with nc.Block() as block:

            @block.sync
            def _(sp):
                sp.dma_start(ident[:, :], dram["ident"]).then_inc(consts["loaded"], 16)
                sp.dma_start(cols[:, :], dram["cols"]).then_inc(consts["loaded"], 16)
                sp.dma_start(weights[:, 0:split[1]], dram["weights_a"][:, 0:split[1]]).then_inc(s["weights0_loaded"], 16)
                with sp.Fori(0, G) as g:
                    sp.wait_ge(s["chan_done"], g * NB + 1)
                    sp.dma_start(x_in[:, :, :], dram["x"][bass.ds(g * NB, NB), :, :].rearrange("b p n -> p b n")).then_inc(s["x_loaded"], 16)
                    sp.dma_start(ctx_in[:, :, :], dram["ctx"][bass.ds(g * NB, NB), :, :].rearrange("b p n -> p b n")).then_inc(s["ctx_loaded"], 16)
                    sp.wait_ge(s["cross_done"], g + 1)
                    sp.dma_start(mask_cross[:, :, :], dram["mask_cross"][bass.ds(g * NB, NB), :, :].rearrange("b p n -> p b n")).then_inc(s["mask_cross_loaded"], 16)
                    sp.wait_ge(s["ctx_used"], g + 1)
                    for c in range(KC):
                        sp.dma_start(ctxT[:, c, :, :], dram["ctxT"][:, c, bass.ds(g * NB, NB), :]).then_inc(s["ctxT_loaded"], 16)
                    sp.wait_ge(s["madd_lat_ready"], g + 1)
                    sp.dma_start(mask_lat[:, :, :], dram["mask_lat"][bass.ds(g * NB, NB), :].partition_broadcast(P)).then_inc(s["mask_lat_loaded"], 16)

            @block.gpsimd
            def _(pool):
                seed(pool, [s["probs_ready"], s["xb_ready"], s["madd_self_ready"], s["madd_cross_ready"], s["madd_lat_ready"],
                            s["v_zeroed"], s["x_released"]])
                nc.gpsimd.memset(v_self[:, :, :], 0.0).then_inc(s["v_zeroed"], 1)
                nc.gpsimd.memset(v_lat[:, :, :, :], 0.0).then_inc(s["v_zeroed"], 1)
                nc.gpsimd.memset(madd_lat[:, :, :], 0.0).then_inc(s["v_zeroed"], 1)
                pool.wait_ge(s["mask_self_loaded"], 16)
                nc.gpsimd.tensor_scalar(madd_self[:, :], mask_self[:, :], -1.0, 10000.0, ALU.add, ALU.mult).then_inc(s["madd_self_ready"], 1)
                with pool.Fori(0, G) as g:

                    def add_bias(name):
                        x_after = {"self": "chan", "cross": "self", "mlp1": "cross", "lat": "mlp1", "mlp2": "mlp1"}[name]
                        wait_x(pool, g, x_after)
                        if name == "mlp2":
                            pool.wait_ge(s["xhat_ready"], g * 16 + XHAT_AFTER["rms"] + 1)
                        nc.gpsimd.tensor_tensor(Xb[:, :, :], X[:, :, :],
                                                rows[:, ROW_OF[name]:ROW_OF[name] + 1, :].broadcast_to([P, NB, D]),
                                                ALU.add).then_inc(s["xb_ready"], 1)

                    def normalise(kind):
                        for u in range(UNITS[kind]):
                            n = FIRST_UNIT[kind] + u
                            segs = unit_parts(kind, u)[2]
                            pr = probs[:, n % 4, :].rearrange("p (s k) -> p s k", s=segs)
                            pool.wait_ge(s["rsum_ready"], g * NU + n + 2)
                            nc.gpsimd.tensor_tensor(pr, pr, rsums[:, n % 4, 0:segs].unsqueeze(2).broadcast_to([P, segs, BANK // segs]),
                                                    ALU.mult).then_inc(s["probs_ready"], 1)

                    normalise("chan")
                    pool.wait_ge(s["rows_loaded"], 16)
                    add_bias("self")
                    pool.wait_ge(s["mask_cross_loaded"], g * 16 + 16)
                    pool.sem_inc(s["wait_passed"], 1)
                    nc.gpsimd.tensor_scalar(madd_cross[:, :, :], mask_cross[:, :, :], -1.0, 10000.0, ALU.add, ALU.mult).then_inc(s["madd_cross_ready"], 1)
                    normalise("self")
                    add_bias("cross")
                    normalise("cross")
                    add_bias("mlp1")
                    pool.wait_ge(s["v_zeroed"], 4)
                    pool.wait_ge(s["mask_lat_loaded"], g * 16 + 16)
                    pool.sem_inc(s["wait_passed"], 1)
                    nc.gpsimd.tensor_scalar(madd_lat[:, :, 0:P], mask_lat[:, :, :], 0.0, NEG, ALU.is_equal, ALU.mult).then_inc(s["madd_lat_ready"], 1)
                    add_bias("lat")
                    normalise("lat")
                    add_bias("mlp2")
                    wait_x(pool, g, "mlp2")
                    pool.dma_start(dram["mid"][:, bass.ds(g * NB, NB), :], X[:, :, :]).then_inc(s["mid_stored"], 16)
                    pool.wait_ge(s["mid_stored"], g * 16 + 16)
                    pool.sem_inc(s["x_released"], 1)

            @block.scalar
            def _(act):
                seed(act, [s["exp_done"], s["pT_copied"], s["o_copied"], s["qm_act"]])
                act.dma_start(weights[:, split[1]:split[2]], dram["weights_a"][:, split[1]:split[2]]).then_inc(s["weights_loaded"], 16)
                act.dma_start(mask_self[:, :], dram["mask_self"]).then_inc(s["mask_self_loaded"], 16)
                act.dma_start(rows[:, :, :], dram["rows_a"].partition_broadcast(P)).then_inc(s["rows_loaded"], 16)
                act.wait_ge(consts["loaded"], 32)
                with act.Fori(0, G) as g:

                    def exps(kind, u):
                        n = FIRST_UNIT[kind] + u
                        segs = unit_parts(kind, u)[2]
                        width = BANK // segs
                        act.wait_ge(s["max_ready"], g * NU + n + 2)
                        act.wait_ge(s["pT_ready"], (g * NU + n - 3 if n >= 4 else g * NU) + 1)
                        for i in range(segs):
                            src = scores[n % 2] if kind == "chan" else negated[:, n % 3, :]
                            last = nc.scalar.activation(probs[:, n % 4, i * width:(i + 1) * width], src[:, i * width:(i + 1) * width],
                                                        ACT.Exp, scale=1.0 if kind == "chan" else -1.0, bias=negmax[:, n % 4, i:i + 1], accum_out=sums[:, n % 4, i:i + 1])
                            if i == segs - 1:
                                last.then_inc(s["exp_done"], 1)

                    def copy_pT(kind, u):
                        n = FIRST_UNIT[kind] + u
                        act.wait_ge(s["pT_ready"], g * NU + n + 2)
                        act.wait_ge(s["pv_done"], (g * NU + n - 1 if n >= 2 else g * NU) + 1)
                        nc.scalar.copy(probsT[:, n % 2, :], pT_psum[n % 2][:, :]).then_inc(s["pT_copied"], 1)

                    def copy_o(kind, b):
                        act.wait_ge(s["pv_done"], g * NU + FIRST_UNIT[kind] + (b + 1) * BATCH_UNITS[kind] + 1)
                        for c in range(KC):
                            nc.scalar.activation(oT[:, c, b, :], o_psum[:, c * P:(c + 1) * P], ACT.Identity,
                                                 bias=col(kind + "_bv", c)).then_inc(s["o_copied"], 1)

                    def attention(kind):
                        n = UNITS[kind]
                        per = BATCH_UNITS[kind]
                        for t in range(n + SCORES_AHEAD + 2):
                            if 0 <= t - SCORES_AHEAD < n:
                                copy_pT(kind, t - SCORES_AHEAD)
                            if t < n:
                                exps(kind, t)
                            done = t - SCORES_AHEAD - 1
                            if kind != "chan" and done >= 0 and done < n and done % per == per - 1:
                                copy_o(kind, done // per)

                    def norm_copy(name):
                        src, freed = wait_full(act, g, (name, 1))
                        if name == "lat":
                            ins = nc.scalar.copy(hT[:, 1, :], src[:, :])
                        elif name == "rms":
                            ins = nc.scalar.activation(hT[:, 1, :], src[:, :], ACT.Copy, scale=col("rms_w", 1))
                        else:
                            ins = nc.scalar.activation(hT[:, 1, :], src[:, :], ACT.Identity, scale=col(name + "_s", 1), bias=col(name + "_b", 1))
                        ins.then_inc(freed, 1)

                    def keys(name, bias, out, split_b):
                        for c in range(KC):
                            src, freed = wait_full(act, g, (name + "_k", c))
                            if split_b:
                                src = src[:, :].rearrange("p (b k) -> p b k", b=NB)
                            else:
                                src = src[:, :]
                            nc.scalar.activation(out[c], src, ACT.Identity, bias=col(bias + "_bk", c)).then_inc(freed, 1)

                    def values(name, out):
                        for i in range(2):
                            src, freed = wait_full(act, g, (name + "_v", i))
                            for j in range(2):
                                dst = out[:, 2 * i + j, :].rearrange("p (t w d) -> p t w d", w=4, d=HD)[:, :, 0:4:3, :]
                                ins = nc.scalar.copy(dst, src[:, j * D:(j + 1) * D].rearrange("p (t w d) -> p t w d", w=2, d=HD))
                            ins.then_inc(freed, 1)

                    def mask_heads(kind):
                        wait_copied(act, g, (kind + "_q", 1))
                        for h in range(HPC):
                            nc.scalar.activation(qm[:, HPC + h, :], qT[:, 1, :], ACT.Copy, scale=col("head_mask", h)).then_inc(s["qm_act"], 1)

                    def gelus(name):
                        for f in range(FC):
                            src, freed = wait_full(act, g, (name + "_up", f))
                            nc.scalar.activation(upT[:, f, :], src[:, :], ACT.Gelu_apprx_tanh, bias=col(name + "_b", f)).then_inc(freed, 1)

                    for i in range(2):
                        src, freed = wait_full(act, g, ("chan_q", i))
                        nc.scalar.activation(q0T[:, i * BANK:(i + 1) * BANK], src[:, :], ACT.Identity, bias=col("bq0")).then_inc(freed, 1)
                    attention("chan")
                    norm_copy("ln1")
                    act.wait_ge(s["v_zeroed"], 3)
                    keys("self", "self", [kT_self[:, c, :] for c in range(KC)], False)
                    values("self", v_self)
                    mask_heads("self")
                    attention("self")
                    kT_ctx = [kT_lat[:, c, :, 0, :] for c in range(KC)]
                    keys("cross", "cross", kT_ctx, True)
                    values("cross", v_lat[:, 0, :, :])
                    norm_copy("ln2")
                    mask_heads("cross")
                    attention("cross")
                    keys("ctx", "lat", kT_ctx, True)
                    values("ctx", v_lat[:, 0, :, :])
                    norm_copy("ln3")
                    gelus("mlp1")
                    norm_copy("lat")
                    keys("lat", "lat", [kT_lat[:, c, :, 1, :] for c in range(KC)], True)
                    values("lat", v_lat[:, 1, :, :])
                    mask_heads("lat")
                    attention("lat")
                    norm_copy("rms")
                    gelus("mlp2")

            @block.vector
            def _(dve):
                seed(dve, [s["max_ready"], s["rsum_ready"], s["chan_done"], s["cross_done"], s["scores_free"], s["qm_dve"],
                           s["xhat_ready"], s["dve_step"]] + free)
                dve.wait_ge(consts["loaded"], 32)
                with dve.Fori(0, G) as g:
                    steps = [0]

                    def step(ins):
                        steps[0] += 1
                        ins.then_inc(s["dve_step"], 1)

                    def wait_step(apart=False):
                        value = g * DVE_STEPS_A + steps[0]
                        if apart:
                            dve.wait_ge(s["dve_step"], value + 1)
                            dve.sem_inc(s["wait_passed"], 1)
                        else:
                            dve.wait_ge(s["dve_step"], value + 1)

                    def front(kind, u):
                        n = FIRST_UNIT[kind] + u
                        b, i, segs = unit_parts(kind, u)
                        dve.wait_ge(s["scores_ready"], g * NU + n + 2)
                        ready = scores[n % 2][:, :].rearrange("p (s k) -> p s k", s=segs)
                        if kind != "chan":
                            m = masked[:, n % 2, :].rearrange("p (s k) -> p s k", s=segs)
                            dve.wait_ge(s["exp_done"], g * NU + n - 1)
                        before = g * NU + n - 3 if n >= 4 else g * NU
                        if kind == "chan":
                            dve.wait_ge(s["exp_done"], before + 1)
                            nc.vector.tensor_reduce(negmax[:, n % 4, 0:segs], ready, axis=AX.X, op=ALU.max, negate=True).then_inc(s["max_ready"], 1)
                            return
                        if kind == "lat":
                            add = madd_lat[:, b, :]
                            dve.wait_ge(s["exp_done"], before + 1)
                            dve.sem_inc(s["wait_passed"], 1)
                        else:
                            mul, add = (mask_self[:, :].unsqueeze(1), madd_self[:, :]) if kind == "self" else (mask_cross[:, b:b + 1, :], madd_cross[:, b, :])
                            nc.vector.tensor_tensor(m, ready, mul.broadcast_to([P, segs, P]), ALU.mult).then_inc(s["scores_free"], 1)
                            dve.wait_ge(s["exp_done"], before + 1)
                            dve.wait_ge(s["scores_free"], g * MASKED_UNITS + n + 1 - FIRST_UNIT["self"] + 1)
                            dve.sem_inc(s["wait_passed"], 1)
                            ready = m
                        for j in range(segs):
                            last = nc.vector.tensor_tensor_reduce(out=negated[:, n % 3, j * (BANK // segs):(j + 1) * (BANK // segs)],
                                                                  in0=ready[:, j, :], in1=add, scale=-1.0, scalar=3.0e38, op0=ALU.add, op1=ALU.min,
                                                                  accum_out=negmax[:, n % 4, j:j + 1])
                        last.then_inc(s["max_ready"], 1)

                    def rsum(kind, u):
                        n = FIRST_UNIT[kind] + u
                        segs = unit_parts(kind, u)[2]
                        dve.wait_ge(s["exp_done"], g * NU + n + 2)
                        dve.wait_ge(s["probs_ready"], (g * NU + n - 3 if n >= 4 else g * NU) + 1)
                        nc.vector.reciprocal(rsums[:, n % 4, 0:segs], sums[:, n % 4, 0:segs]).then_inc(s["rsum_ready"], 1)

                    def residual(kind, b):
                        src, freed = wait_full(dve, g, (kind + "_o", b))
                        dst = Xb if kind == "lat" else X
                        if b == 0:
                            dve.wait_ge(s["xb_ready"], g * 5 + XB_AFTER[kind] + 1)
                        nc.vector.tensor_tensor(dst[:, b, :], src[:, 0:D], Xb[:, b, :], ALU.add).then_inc(freed, 1)

                    def chan_residual(b):
                        dve.wait_ge(s["pv_done"], g * NU + b + 2)
                        if b == 0:
                            dve.wait_ge(s["x_released"], g + 1)
                        nc.vector.scalar_tensor_tensor(out=X[:, b, :], in0=o_psum[:, 0:D], scalar=col("bv0"), in1=x_in[:, b, :],
                                                       op0=ALU.add, op1=ALU.add).then_inc(s["chan_done"], 1)

                    def attention(kind):
                        n = UNITS[kind]
                        per = BATCH_UNITS[kind]
                        for t in range(n + SCORES_AHEAD + 4):
                            if t < n:
                                front(kind, t)
                            if 0 <= t - 1 < n:
                                rsum(kind, t - 1)
                            done = t - SCORES_AHEAD - (2 if kind == "chan" else 3)
                            if 0 <= done < n and done % per == per - 1:
                                b = done // per
                                if kind == "chan":
                                    chan_residual(b)
                                    dve.wait_ge(s["chan_done"], g * NB + b + 2)
                                else:
                                    residual(kind, b)
                                    wait_copied(dve, g, (kind + "_o", b))
                                step(nc.vector.bn_stats(stats[:, b, :], (Xb if kind == "lat" else X)[:, b, :]))

                    def norm(name):
                        src = Xb if name == "rms" else X
                        wait_step(apart=True)
                        for b in range(NB):
                            step(nc.vector.bn_aggr(mv[:, b, :], stats[:, b, :]))
                        wait_step()
                        if name == "rms":
                            step(nc.vector.tensor_tensor(newton[:, :], mv[:, :, 0], mv[:, :, 0], ALU.mult))
                            wait_step()
                            step(nc.vector.scalar_tensor_tensor(out=var[:, :], in0=mv[:, :, 1], scalar=1e-6, in1=newton[:, :], op0=ALU.add, op1=ALU.add))
                        else:
                            step(nc.vector.tensor_scalar(var[:, :], mv[:, :, 1], 1e-5, None, ALU.add))
                        wait_step()
                        inverse_root()
                        for b in range(NB):
                            if name == "rms":
                                ins = nc.vector.tensor_scalar(xhat[:, b, :], src[:, b, :], rstd[:, b:b + 1], None, ALU.mult)
                            else:
                                ins = nc.vector.tensor_scalar(xhat[:, b, :], src[:, b, :], mv[:, b, 0:1], rstd[:, b:b + 1], ALU.subtract, ALU.mult)
                            ins.then_inc(s["xhat_ready"], 1)

                    def inverse_root():
                        step(nc.vector.tensor_single_scalar(guess[:, :], var[:, :].bitcast(I32), 1, ALU.logical_shift_right))
                        wait_step()
                        step(nc.vector.tensor_scalar(guess[:, :], guess[:, :], -1.0, RSQRT_MAGIC, ALU.mult, ALU.add))
                        wait_step()
                        y = guess[:, :].bitcast(F32)
                        for i in range(NEWTON_STEPS):
                            step(nc.vector.scalar_tensor_tensor(out=newton[:, :], in0=y, scalar=-0.5, in1=y, op0=ALU.mult, op1=ALU.mult))
                            wait_step()
                            step(nc.vector.tensor_tensor(newton[:, :], newton[:, :], var[:, :], ALU.mult))
                            wait_step()
                            step(nc.vector.scalar_tensor_tensor(out=rstd[:, :], in0=newton[:, :], scalar=1.5, in1=y, op0=ALU.add, op1=ALU.mult))
                            wait_step()
                            y = rstd[:, :]

                    def norm_copy(name):
                        src, freed = wait_full(dve, g, (name, 0))
                        if name == "lat":
                            ins = nc.vector.tensor_copy(hT[:, 0, :], src[:, :])
                        elif name == "rms":
                            ins = nc.vector.tensor_scalar(hT[:, 0, :], src[:, :], col("rms_w", 0), None, ALU.mult)
                        else:
                            ins = nc.vector.tensor_scalar(hT[:, 0, :], src[:, :], col(name + "_s", 0), col(name + "_b", 0), ALU.mult, ALU.add)
                        ins.then_inc(freed, 1)

                    def queries(i, kind):
                        scale = 1.0 / HD if kind == "lat" else HD ** -0.5
                        for c in range(KC):
                            src, freed = wait_full(dve, g, (kind + "_q", c))
                            if i > 0 and c == 1:
                                dve.wait_ge(s["qm_act"], (g * 3 + i) * HPC + 1)
                            elif c == 1:
                                dve.wait_ge(s["qm_act"], g * 3 * HPC + 1)
                            nc.vector.tensor_scalar(qT[:, c, :], src[:, :], col(kind + "_bq", c), scale, ALU.add, ALU.mult).then_inc(freed, 1)
                        wait_copied(dve, g, (kind + "_q", 0))
                        for h in range(HPC):
                            nc.vector.tensor_scalar(qm[:, h, :], qT[:, 0, :], col("head_mask", h), None, ALU.mult).then_inc(s["qm_dve"], 1)

                    def mlp_residual(name):
                        dve.wait_ge(s["xb_ready"], g * 5 + XB_AFTER[name] + 1)
                        for i in range(2):
                            src, freed = wait_full(dve, g, (name + "_down", i))
                            nc.vector.tensor_tensor(X[:, 2 * i:2 * i + 2, :], src[:, :].rearrange("p (b n) -> p b n", b=2),
                                                    Xb[:, 2 * i:2 * i + 2, :], ALU.add).then_inc(freed, 1)

                    for i in range(2):
                        src, freed = wait_full(dve, g, ("chan_k", i))
                        nc.vector.tensor_scalar(k0T[:, i * BANK:(i + 1) * BANK], src[:, :], col("bk0"), None, ALU.add).then_inc(freed, 1)
                    for i in range(2):
                        src, freed = wait_full(dve, g, ("chan_v", i))
                        nc.vector.tensor_copy(v0T[:, 2 * i:2 * i + 2, :, :], src[:, :].rearrange("p (b m c) -> p b m c", b=2, m=2)).then_inc(freed, 1)
                    attention("chan")
                    norm("ln1")
                    norm_copy("ln1")
                    queries(0, "self")
                    dve.wait_ge(s["madd_self_ready"], 2)
                    attention("self")
                    norm("ln2")
                    norm_copy("ln2")
                    queries(1, "cross")
                    dve.wait_ge(s["madd_cross_ready"], g + 2)
                    attention("cross")
                    norm("ln3")
                    dve.sem_inc(s["cross_done"], 1)
                    norm_copy("ln3")
                    mlp_residual("mlp1")
                    norm_copy("lat")
                    queries(2, "lat")
                    dve.wait_ge(s["madd_lat_ready"], g + 2)
                    attention("lat")
                    norm("rms")
                    norm_copy("rms")
                    mlp_residual("mlp2")
                    assert steps[0] == DVE_STEPS_A, steps

            @block.tensor
            def _(pe):
                seed(pe, [s["scores_ready"], s["pT_ready"], s["pv_done"], s["ctx_used"]] + full)
                pe.wait_ge(consts["loaded"], 32)
                pe.wait_ge(s["weights0_loaded"], 16)
                with pe.Fori(0, G) as g:

                    def transposed(name):
                        src = X if name == "lat" else xhat
                        for c in range(KC):
                            out, filled = wait_free(pe, g, (name, c))
                            for b in range(NB):
                                if name == "lat":
                                    if c == b == 0:
                                        wait_x(pe, g, "mlp1")
                                elif c == 0:
                                    pe.wait_ge(s["xhat_ready"], g * 16 + XHAT_AFTER[name] - NB + b + 2)
                                last = nc.tensor.transpose(out[:, b * P:(b + 1) * P], src[:, b, c * P:(c + 1) * P], ident[:, :])
                            last.then_inc(filled, 1)

                    def project(key, weight, chunk, rhs):
                        out, filled = wait_free(pe, g, key)
                        for c in range(KC):
                            last = nc.tensor.matmul(out[:, :], w[weight][:, c, chunk * P:(chunk + 1) * P], rhs[c], start=(c == 0), stop=(c == KC - 1))
                        last.then_inc(filled, 1)

                    def project_rows(key, weight, i, lhs):
                        out, filled = wait_free(pe, g, key)
                        for j in range(2):
                            for c in range(KC):
                                last = nc.tensor.matmul(out[:, j * D:(j + 1) * D], lhs(c, 2 * i + j), w[weight][:, c, :], start=(c == 0), stop=(c == KC - 1))
                        last.then_inc(filled, 1)

                    def scores_of(kind, u):
                        n = FIRST_UNIT[kind] + u
                        b, i, segs = unit_parts(kind, u)
                        old = n - 2
                        if old < FIRST_UNIT["self"] and old >= 0:
                            pe.wait_ge(s["exp_done"], g * NU + old + 2)
                        elif 0 <= old < FIRST_UNIT["lat"]:
                            pe.wait_ge(s["scores_free"], g * MASKED_UNITS + old + 1 - FIRST_UNIT["self"] + 1)
                        else:
                            pe.wait_ge(s["max_ready"], g * NU + max(old + 1, 0) + 1)
                        out = scores[n % 2]
                        if kind != "chan" and b == 0:
                            nth = {"self": 0, "cross": 1, "lat": 2}[kind]
                            heads = NH // BATCH_UNITS[kind] * (i + 1)
                            if heads <= HPC:
                                pe.wait_ge(s["qm_dve"], (g * 3 + nth) * HPC + heads + 1)
                            else:
                                pe.wait_ge(s["qm_act"], (g * 3 + nth) * HPC + heads - HPC + 1)
                        for j in range(segs):
                            if kind == "chan":
                                last = nc.tensor.matmul(out[:, j * D:(j + 1) * D], q0T[:, b * D + j * P:b * D + (j + 1) * P], k0T[:, b * D:(b + 1) * D], start=True, stop=True)
                            elif kind == "lat":
                                h = 2 * i + j
                                last = nc.tensor.matmul(out[:, j * D:(j + 1) * D], qm[:, h, b * P:(b + 1) * P],
                                                        kT_lat[:, h // HPC, b, :, :], start=True, stop=True)
                            else:
                                h = 4 * i + j
                                key = kT_self[:, h // HPC, b * P:(b + 1) * P] if kind == "self" else kT_lat[:, h // HPC, b, 0, :]
                                last = nc.tensor.matmul(out[:, j * P:(j + 1) * P], qm[:, h, b * P:(b + 1) * P], key, start=True, stop=True)
                        last.then_inc(s["scores_ready"], 1)

                    def transpose_probs(kind, u):
                        n = FIRST_UNIT[kind] + u
                        pe.wait_ge(s["probs_ready"], g * NU + n + 2)
                        pe.wait_ge(s["pT_copied"], (g * NU + n - 1 if n >= 2 else g * NU) + 1)
                        for j in range(4):
                            at = (j % 2) * 2 + j // 2 if kind == "chan" else j
                            last = nc.tensor.transpose(pT_psum[n % 2][:, at * P:(at + 1) * P], probs[:, n % 4, j * P:(j + 1) * P], ident[:, :])
                        last.then_inc(s["pT_ready"], 1)

                    def weigh_values(kind, u):
                        n = FIRST_UNIT[kind] + u
                        b, i, segs = unit_parts(kind, u)
                        pe.wait_ge(s["pT_copied"], g * NU + n + 2)
                        if i == 0:
                            if b > 0 and kind == "chan":
                                pe.wait_ge(s["chan_done"], g * NB + b + 1)
                            elif b == 0 and kind == "self":
                                pe.wait_ge(s["chan_done"], g * NB + NB + 1)
                            else:
                                nth = {"chan": 0, "self": 0, "cross": NB, "lat": 2 * NB}[kind] + b
                                pe.wait_ge(s["o_copied"], (g * 3 * NB + nth) * KC + 1)
                        pT = probsT[:, n % 2, :]
                        if kind == "chan":
                            for m in range(2):
                                last = nc.tensor.matmul(o_psum[:, 0:D], v0T[:, b, m, :], pT[:, m * D:(m + 1) * D], start=(m == 0), stop=(m == 1))
                        elif kind == "lat":
                            for j in range(2):
                                h = 2 * i + j
                                row, c = 32 * (i % 4), i // 4
                                for m in range(2):
                                    last = nc.tensor.matmul(o_psum[row:row + 32, c * P:(c + 1) * P], v_lat[:, m, b, 32 * h:32 * h + 32],
                                                            pT[:, (2 * j + m) * P:(2 * j + m + 1) * P], start=(j == 0 and m == 0), stop=(j == 1 and m == 1))
                        else:
                            for j in range(4):
                                h = 4 * i + j
                                row, c = 32 * (h // 2 % 4), h // 8
                                v = v_self[:, b, 32 * h:32 * h + 32] if kind == "self" else v_lat[:, 0, b, 32 * h:32 * h + 32]
                                last = nc.tensor.matmul(o_psum[row:row + 32, c * P:(c + 1) * P], v, pT[:, j * P:(j + 1) * P], start=(j % 2 == 0), stop=(j % 2 == 1))
                        last.then_inc(s["pv_done"], 1)

                    def output(kind, b):
                        nth = {"self": 0, "cross": NB, "lat": 2 * NB}[kind] + b
                        pe.wait_ge(s["o_copied"], (g * 3 * NB + nth + 1) * KC + 1)
                        out, filled = wait_free(pe, g, (kind + "_o", b))
                        for c in range(KC):
                            last = nc.tensor.matmul(out[:, 0:D], oT[:, c, b, :], w[kind + "_o"][:, c, :], start=(c == 0), stop=(c == KC - 1))
                        last.then_inc(filled, 1)

                    def attention(kind):
                        n = UNITS[kind]
                        per = BATCH_UNITS[kind]
                        for t in range(n + SCORES_AHEAD + 3):
                            if t < n:
                                scores_of(kind, t)
                            if 0 <= t - SCORES_AHEAD < n:
                                transpose_probs(kind, t - SCORES_AHEAD)
                            if 0 <= t - SCORES_AHEAD - 1 < n:
                                weigh_values(kind, t - SCORES_AHEAD - 1)
                            done = t - SCORES_AHEAD - 2
                            if kind != "chan" and 0 <= done < n and done % per == per - 1:
                                output(kind, done // per)

                    def mlp(name):
                        for f in range(FC):
                            project((name + "_up", f), name + "_up", f, [hT[:, c, :] for c in range(KC)])
                        for i in range(2):
                            out, filled = wait_free(pe, g, (name + "_down", i))
                            for j in range(2):
                                b = 2 * i + j
                                for f in range(FC):
                                    if i == j == 0:
                                        wait_copied(pe, g, (name + "_up", f))
                                    last = nc.tensor.matmul(out[:, j * D:(j + 1) * D], upT[:, f, b * P:(b + 1) * P], w[name + "_down"][:, f, :], start=(f == 0), stop=(f == FC - 1))
                            last.then_inc(filled, 1)

                    hT_chunks = [hT[:, c, :] for c in range(KC)]
                    ctxT_chunks = [ctxT[:, c, :, :] for c in range(KC)]

                    def hT_rows(c, b):
                        return hT[:, c, b * P:(b + 1) * P]

                    def ctxT_rows(c, b):
                        return ctxT[:, c, b, :]

                    pe.wait_ge(s["x_loaded"], g * 16 + 16)
                    for i in range(2):
                        out, filled = wait_free(pe, g, ("chan_q", i))
                        nc.tensor.matmul(out[:, :], w["wq0"][:, 0, :], x_in[:, 2 * i:2 * i + 2, :], start=True, stop=True).then_inc(filled, 1)
                    pe.wait_ge(s["ctx_loaded"], g * 16 + 16)
                    for i in range(2):
                        out, filled = wait_free(pe, g, ("chan_k", i))
                        nc.tensor.matmul(out[:, :], w["wk0"][:, 0, :], ctx_in[:, 2 * i:2 * i + 2, :], start=True, stop=True).then_inc(filled, 1)
                    for i in range(2):
                        out, filled = wait_free(pe, g, ("chan_v", i))
                        for j in range(4):
                            b, m = 2 * i + j // 2, j % 2
                            last = nc.tensor.matmul(out[:, j * P:(j + 1) * P], ctx_in[:, b, m * P:(m + 1) * P], w["wv0"][:, 0, :], start=True, stop=True)
                        last.then_inc(filled, 1)
                    for i in range(2):
                        for name in ("chan_q", "chan_k", "chan_v"):
                            wait_copied(pe, g, (name, i))
                    attention("chan")

                    pe.wait_ge(s["weights_loaded"], 16)
                    transposed("ln1")
                    for c in range(KC):
                        wait_copied(pe, g, ("ln1", c))
                    for c in range(KC):
                        project(("self_q", c), "self_q", c, hT_chunks)
                    for c in range(KC):
                        project(("self_k", c), "self_k", c, hT_chunks)
                    for i in range(2):
                        project_rows(("self_v", i), "self_v", i, hT_rows)
                    for i in range(2):
                        wait_copied(pe, g, ("self_k", i))
                        wait_copied(pe, g, ("self_v", i))
                    attention("self")

                    pe.wait_ge(s["ctxT_loaded"], g * 32 + 32)
                    for c in range(KC):
                        project(("cross_k", c), "cross_k", c, ctxT_chunks)
                    for i in range(2):
                        project_rows(("cross_v", i), "cross_v", i, ctxT_rows)
                    transposed("ln2")
                    for c in range(KC):
                        wait_copied(pe, g, ("ln2", c))
                    for c in range(KC):
                        project(("cross_q", c), "cross_q", c, hT_chunks)
                    for i in range(2):
                        wait_copied(pe, g, ("cross_k", i))
                        wait_copied(pe, g, ("cross_v", i))
                    attention("cross")

                    for c in range(KC):
                        project(("ctx_k", c), "lat_k", c, ctxT_chunks)
                    for i in range(2):
                        project_rows(("ctx_v", i), "lat_v", i, ctxT_rows)
                    for i in range(2):
                        wait_copied(pe, g, ("ctx_v", i))
                    pe.sem_inc(s["ctx_used"], 1)
                    transposed("ln3")
                    for c in range(KC):
                        wait_copied(pe, g, ("ln3", c))
                    mlp("mlp1")

                    transposed("lat")
                    for c in range(KC):
                        wait_copied(pe, g, ("lat", c))
                    for c in range(KC):
                        project(("lat_q", c), "lat_q", c, hT_chunks)
                    for c in range(KC):
                        project(("lat_k", c), "lat_k", c, hT_chunks)
                    for i in range(2):
                        project_rows(("lat_v", i), "lat_v", i, hT_rows)
                    for i in range(2):
                        for name in ("ctx_k", "lat_k", "lat_v"):
                            wait_copied(pe, g, (name, i))
                    attention("lat")
                    transposed("rms")
                    for c in range(KC):
                        wait_copied(pe, g, ("rms", c))
                    mlp("mlp2")


STEPS = 2 * G
PRE_USES = [(n, i) for i in range(G) for n in ("q", "k")]


def pair_uses(last):
    uses = []
    for t in range(STEPS):
        if not (last and t >= G):
            uses += [("q", t), ("k", t)]
        uses.append(("v", t))
        done = t - G - 1
        if done >= 0:
            uses += [("out", done, 0), ("out", done, 1)]
    return uses + [("out", G - 1, 0), ("out", G - 1, 1)]


MLP3_USES = [("ln", c) for c in (1, 0)] + [("up", f) for f in range(FC)] + [("down", i) for i in range(2)]
SCALE3 = W3 ** -0.5
HCOLS = 4
ATT_UNITS = PAIRS * STEPS


def stage_3(nc, dram, consts):
    ident, cols = consts["ident"], consts["cols"]

    with ExitStack() as ctx:
        def sb(name, shape, dt=F32):
            return ctx.enter_context(nc.sbuf_tensor(name, shape, dt))

        def sem(name):
            return ctx.enter_context(nc.semaphore(name))

        X = sb("X3", [P, B, D])
        hT = sb("hT3", [P, KC, B * P])
        ctxT = sb("ctxT3", [P, KC, B * P])
        xhat = sb("xhat3", [P, NB, D])
        qT = sb("qT3", [P, 2, B * P])
        kT = sb("kT3", [P, 2, B * P])
        v = sb("v3", [P, 2, B, P])
        oT = sb("oT3", [P, 2, B * P])
        probs = sb("probs3", [P, 2, BANK])
        probsT = sb("probsT3", [P, BANK])
        rawmax = sb("rawmax3", [P, 2, NB])
        negmax = sb("negmax3", [P, 2, NB])
        sums = sb("sums3", [P, 2, NB])
        learned = sb("learned3", [P, 2, NB])
        totals = sb("totals3", [P, 2, NB])
        rsums = sb("rsums3", [P, 2, NB])
        w_qk = sb("w_qk3", [P, 2, 2, KC, P])
        w_v = sb("w_v3", [P, 2, KC, P])
        w_o = sb("w_o3", [P, 2, D])
        hcols = sb("hcols3", [P, 2 * NH * HCOLS])
        vrows = sb("vrows3", [P, 2, 2 * NH * P])
        rows = sb("rows_b", [P, len(ROWS_B), D])
        w_up = sb("w_up3", [P, KC, F])
        w_down = sb("w_down3", [P, FC, D])
        upT = sb("upT3", [P, FC, R])
        stats = sb("stats3", [P, NB, 6])
        mv = sb("mv3", [P, NB, 2])
        var = sb("var3", [P, NB])
        guess = sb("guess3", [P, NB], I32)
        rstd = sb("rstd3", [P, NB])
        newton = sb("newton3", [P, NB])

        def bank(name):
            return ctx.enter_context(nc.psum_tensor(name, [P, BANK], F32))

        NGEN = 4
        scores = [bank(f"scores3_{i}") for i in range(2)]
        pT_psum = bank("pT_psum3")
        o_psum = bank("o_psum3")
        general = [bank(f"general3_{i}") for i in range(NGEN)]

        s = {n: sem(n + "3") for n in (
            "x_loaded", "ctxT_loaded", "w_qk0_loaded", "w_a_loaded", "w_b_loaded", "vectors_loaded", "mlp_loaded", "stored",
            "vrows_ready", "xb_ready", "xhat_ready",
            "scores_ready", "max_ready", "exp_done", "rsum_ready", "probs_ready", "pT_ready", "pT_copied",
            "o_ready", "o_copied", "dve_step", "wait_passed")}
        full = [sem(f"general_full3_{i}") for i in range(NGEN)]
        free = [sem(f"general_free3_{i}") for i in range(NGEN)]

        sections = {"ln": Banks([("ln", 1), ("ln", 0)], NGEN), "pre": Banks(PRE_USES, NGEN),
                    "pair": Banks(pair_uses(False), NGEN), "last": Banks(pair_uses(True), NGEN), "mlp": Banks(MLP3_USES, NGEN)}
        times = {"ln": G, "pre": 1, "pair": PAIRS - 1, "last": 1}
        before = {}
        for k in range(NGEN):
            total = 0
            for name in ("ln", "pre", "pair", "last"):
                before[name, k] = total
                total += times[name] * sections[name].per_loop[k]
            before["mlp", k] = 2 * total
            before["attention", k] = total

        def use(section, a, i, key):
            k, n = sections[section][key]
            count = before[section, k] + n + i * sections[section].per_loop[k]
            if section != "mlp":
                count = count + a * before["attention", k]
            return k, count

        def wait_full(eng, *at):
            k, n = use(*at)
            eng.wait_ge(full[k], n + 2)
            return general[k], free[k]

        def wait_full_apart(eng, *at):
            k, n = use(*at)
            eng.wait_ge(full[k], n + 2)
            eng.sem_inc(s["wait_passed"], 1)
            return general[k], free[k]

        def wait_free(eng, *at):
            k, n = use(*at)
            eng.wait_ge(free[k], n + 1)
            return general[k], full[k]

        def wait_copied(eng, *at):
            k, n = use(*at)
            eng.wait_ge(free[k], n + 2)

        def pair_section(last):
            return "last" if last else "pair"

        with nc.Block() as block:

            @block.sync
            def _(sp):
                def load_qk0(pair):
                    sp.dma_start(w_qk[:, 0, :, :, :], dram["w_qk"][bass.ds(pair, 1), :, 0, :].rearrange("a p (w c n) -> p (a w) c n", w=2, c=KC)).then_inc(s["w_qk0_loaded"], 16)

                def load_a(pair):
                    sp.dma_start(w_qk[:, 1, :, :, :], dram["w_qk"][bass.ds(pair, 1), :, 1, :].rearrange("a p (w c n) -> p (a w) c n", w=2, c=KC)).then_inc(s["w_a_loaded"], 16)
                    sp.dma_start(w_v[:, 0, :, :], dram["w_v"][bass.ds(pair, 1), :, 0, :].rearrange("a p (c n) -> p (a c) n", c=KC)).then_inc(s["w_a_loaded"], 16)

                def load_b(pair):
                    sp.dma_start(w_v[:, 1, :, :], dram["w_v"][bass.ds(pair, 1), :, 1, :].rearrange("a p (c n) -> p (a c) n", c=KC)).then_inc(s["w_b_loaded"], 16)
                    sp.dma_start(w_o[:, :, :], dram["w_o"][bass.ds(pair, 1), :, :].rearrange("a p (h n) -> p (a h) n", h=2)).then_inc(s["w_b_loaded"], 16)

                for i in range(G):
                    sp.dma_start(X[:, NB * i:NB * i + NB, :], dram["mid"][:, NB * i:NB * i + NB, :]).then_inc(s["x_loaded"], 16)
                for c in range(KC):
                    sp.dma_start(ctxT[:, c, :], dram["ctxT"][:, c, :, :].rearrange("p b k -> p (b k)")).then_inc(s["ctxT_loaded"], 16)
                with sp.Fori(0, 2) as a:
                    for load, section, i, key in ((load_qk0, "pair", PAIRS - 2, ("k", STEPS - 1)), (load_a, "last", 0, ("v", G - 1)),
                                                  (load_b, "last", 0, ("out", G - 1, 1))):
                        k, n = use(section, 0, i, key)
                        sp.wait_ge(full[k], a * (n + 1) + 1)
                        load(a * PAIRS)
                    wait_full(sp, "pre", a, 0, ("k", G - 1))
                    load_qk0(a * PAIRS + 1)

                    def next_weights(i, more):
                        wait_full(sp, "pair", a, i, ("v", G - 1))
                        load_a(a * PAIRS + i + 1)
                        if more:
                            wait_full(sp, "pair", a, i, ("k", STEPS - 1))
                            load_qk0(a * PAIRS + i + 2)
                        wait_full(sp, "pair", a, i, ("out", G - 1, 1))
                        load_b(a * PAIRS + i + 1)

                    with sp.Fori(0, PAIRS - 2) as i:
                        next_weights(i, True)
                    next_weights(PAIRS - 2, False)

            @block.gpsimd
            def _(pool):
                seed(pool, [s["vrows_ready"], s["xb_ready"], s["probs_ready"]])
                pool.wait_ge(s["vectors_loaded"], 64)
                nc.gpsimd.tensor_tensor(vrows[:, 0, :], vrows[:, 0, :], vrows[:, 1, :], ALU.subtract).then_inc(s["vrows_ready"], 1)
                with pool.Fori(0, 2) as a:
                    pool.wait_ge(s["xhat_ready"], a * B + B + 1)
                    nc.gpsimd.tensor_tensor(X[:, :, :], X[:, :, :], rows[:, bass.ds(a, 1), :].broadcast_to([P, B, D]), ALU.add).then_inc(s["xb_ready"], 1)
                    with pool.Fori(0, PAIRS) as i:
                        for t in range(STEPS):
                            n = a * ATT_UNITS + i * STEPS + t
                            pr = probs[:, t % 2, :].rearrange("p (b k) -> p b k", b=NB)
                            pool.wait_ge(s["rsum_ready"], n + 2)
                            nc.gpsimd.tensor_tensor(pr, pr, rsums[:, t % 2, :].unsqueeze(2).broadcast_to([P, NB, P]), ALU.mult).then_inc(s["probs_ready"], 1)
                with pool.Fori(0, G) as g:
                    x = X[:, bass.ds(g * NB, NB), :]
                    pool.wait_ge(s["xhat_ready"], 2 * B + g * NB + NB + 1)
                    nc.gpsimd.tensor_tensor(x, x, rows[:, 2:3, :].broadcast_to([P, NB, D]), ALU.add).then_inc(s["xb_ready"], 1)
                    for j in range(2):
                        wait_copied(pool, "mlp", 0, g, ("down", j))
                    pool.dma_start(dram["out"][bass.ds(g * NB, NB), :, :].rearrange("b p n -> p b n"), X[:, bass.ds(g * NB, NB), :]).then_inc(s["stored"], 16)
                pool.wait_ge(s["stored"], 16 * G)

            @block.scalar
            def _(act):
                seed(act, [s["exp_done"], s["pT_copied"], s["o_copied"]])
                act.dma_start(hcols[:, :], dram["hcols"]).then_inc(s["vectors_loaded"], 16)
                act.dma_start(rows[:, :, :], dram["rows_b"].partition_broadcast(P)).then_inc(s["vectors_loaded"], 16)
                for j in range(2):
                    act.dma_start(vrows[:, j, :], dram["vrows"][j, :].partition_broadcast(P)).then_inc(s["vectors_loaded"], 16)
                act.dma_start(w_up[:, :, :], dram["w_up"].rearrange("p (c n) -> p c n", c=KC)).then_inc(s["mlp_loaded"], 16)
                act.dma_start(w_down[:, :, :], dram["w_down"].rearrange("p (c n) -> p c n", c=FC)).then_inc(s["mlp_loaded"], 16)
                act.wait_ge(s["vectors_loaded"], 64)

                def copy_q(a, i, section, t, head):
                    src, freed = wait_full_apart(act, section, a, i, ("q", t))
                    pair = i if section == "pre" or t < G else i + 1
                    at = a * (NH * HCOLS) + pair * (2 * HCOLS) + head * HCOLS
                    row = (t % G) * R
                    nc.scalar.activation(qT[:, head, row:row + R], src[:, :], ACT.Identity, bias=hcols[:, bass.ds(at, 1)]).then_inc(freed, 1)

                def exps(n, t):
                    act.wait_ge(s["max_ready"], n + 2)
                    act.wait_ge(s["pT_ready"], (n - 1 if t >= 2 else n - t) + 1)
                    for b in range(NB):
                        nc.scalar.activation(probs[:, t % 2, b * P:(b + 1) * P], scores[t % 2][:, b * P:(b + 1) * P], ACT.Exp,
                                             bias=negmax[:, t % 2, b:b + 1], scale=SCALE3, accum_out=sums[:, t % 2, b:b + 1])
                    nc.scalar.activation(learned[:, t % 2, :], negmax[:, t % 2, :], ACT.Exp).then_inc(s["exp_done"], 1)

                def copy_pT(n):
                    act.wait_ge(s["pT_ready"], n + 2)
                    act.wait_ge(s["o_ready"], n + 1)
                    nc.scalar.copy(probsT[:, :], pT_psum[:, :]).then_inc(s["pT_copied"], 1)

                def copy_o(a, i, n, t):
                    head = t // G
                    at = a * (NH * HCOLS) + i * (2 * HCOLS) + head * HCOLS + 3
                    act.wait_ge(s["o_ready"], n + 2)
                    act.sem_inc(s["wait_passed"], 1)
                    row = (t % G) * R
                    nc.scalar.activation(oT[:, head, row:row + R], o_psum[:, :], ACT.Identity, bias=hcols[:, bass.ds(at, 1)]).then_inc(s["o_copied"], 1)

                def pair(a, i, last):
                    for t in range(STEPS):
                        n = a * ATT_UNITS + i * STEPS + t
                        exps(n, t)
                        if t > 0:
                            copy_o(a, i, n - 1, t - 1)
                        if not (last and t >= G):
                            section = pair_section(last)
                            src, freed = wait_full_apart(act, section, a, 0 if last else i, ("q", t))
                            head = 1 - t // G
                            at = a * (NH * HCOLS) + i * (2 * HCOLS) + (HCOLS if t < G else 2 * HCOLS)
                            row = (t % G) * R
                            nc.scalar.activation(qT[:, head, row:row + R], src[:, :], ACT.Identity, bias=hcols[:, bass.ds(at, 1)]).then_inc(freed, 1)
                        copy_pT(n)
                    copy_o(a, i, n, STEPS - 1)

                def norm_copy(section, a, g, dst, scale, shift):
                    src, freed = wait_full_apart(act, section, a, g, ("ln", 1))
                    nc.scalar.activation(dst, src[:, :], ACT.Identity, scale=scale, bias=shift).then_inc(freed, 1)

                with act.Fori(0, 2) as a:
                    at = COLS["lnA_s"][0] + a * 4 + 1
                    with act.Fori(0, G) as g:
                        norm_copy("ln", a, g, hT[:, 1, bass.ds(g * R, R)], cols[:, bass.ds(at, 1)], cols[:, bass.ds(at + 2, 1)])
                    for t in range(G):
                        copy_q(a, 0, "pre", t, 0)
                    with act.Fori(0, PAIRS - 1) as i:
                        pair(a, i, False)
                    pair(a, PAIRS - 1, True)
                with act.Fori(0, G) as g:
                    at = COLS["lnM_s"][0] + 1
                    norm_copy("mlp", 0, g, hT[:, 1, 0:R], cols[:, at:at + 1], cols[:, at + 2:at + 3])
                    for f in range(FC):
                        src, freed = wait_full(act, "mlp", 0, g, ("up", f))
                        at = COLS["mlp3_b"][0] + f
                        nc.scalar.activation(upT[:, f, :], src[:, :], ACT.Gelu, bias=cols[:, at:at + 1]).then_inc(freed, 1)

            @block.vector
            def _(dve):
                seed(dve, [s["xhat_ready"], s["max_ready"], s["rsum_ready"], s["dve_step"]] + free)
                dve.wait_ge(s["x_loaded"], 16 * G)
                dve.wait_ge(s["vectors_loaded"], 64)

                def copy_k(a, i, section, loop, t, head, pair):
                    src, freed = wait_full(dve, section, a, loop, ("k", t))
                    at = a * (NH * HCOLS) + pair * (2 * HCOLS) + head * HCOLS
                    row = (t % G) * R
                    nc.vector.tensor_scalar(kT[:, head, row:row + R], src[:, :], hcols[:, bass.ds(at + 1, 1)], hcols[:, bass.ds(at + 2, 1)],
                                            ALU.add, ALU.subtract).then_inc(freed, 1)

                def copy_v(a, i, section, loop, t):
                    src, freed = wait_full(dve, section, a, loop, ("v", t))
                    head = t // G
                    at = a * (NH * P) + i * (2 * P) + head * P
                    b = (t % G) * NB
                    nc.vector.tensor_tensor(v[:, head, b:b + NB, :], src[:, :].rearrange("p (b k) -> p b k", b=NB),
                                            vrows[:, 0, bass.ds(at, P)].unsqueeze(1).broadcast_to([P, NB, P]), ALU.add).then_inc(freed, 1)

                def front(n, t):
                    dve.wait_ge(s["scores_ready"], n + 2)
                    nc.vector.tensor_reduce(rawmax[:, t % 2, :], scores[t % 2][:, :].rearrange("p (b k) -> p b k", b=NB),
                                            axis=AX.X, op=ALU.max, negate=True).then_inc(s["dve_step"], 1)
                    dve.wait_ge(s["dve_step"], steps(n) + 2)
                    nc.vector.tensor_scalar(negmax[:, t % 2, :], rawmax[:, t % 2, :], 0.0, SCALE3, ALU.min, ALU.mult).then_inc(s["max_ready"], 1)

                def rsum(n, t):
                    dve.wait_ge(s["exp_done"], n + 2)
                    dve.wait_ge(s["probs_ready"], (n - 1 if t >= 2 else n - t) + 1)
                    nc.vector.tensor_tensor(totals[:, t % 2, :], sums[:, t % 2, :], learned[:, t % 2, :], ALU.add).then_inc(s["dve_step"], 1)
                    dve.wait_ge(s["dve_step"], steps(n) + 3)
                    nc.vector.reciprocal(rsums[:, t % 2, :], totals[:, t % 2, :]).then_inc(s["rsum_ready"], 1)

                def steps(n):
                    return n * 2 + norms_before[0]

                norms_before = [0]

                def add_out(a, i, section, loop, quarter):
                    for j in range(2):
                        src, freed = wait_full(dve, section, a, loop, ("out", quarter, j))
                        x = X[:, NB * quarter + 2 * j:NB * quarter + 2 * j + 2, :]
                        nc.vector.tensor_tensor(x, src[:, :].rearrange("p (b n) -> p b n", b=2), x, ALU.add).then_inc(freed, 1)

                def pair(a, i, last):
                    section, loop = pair_section(last), 0 if last else i
                    for t in range(STEPS):
                        n = a * ATT_UNITS + i * STEPS + t
                        front(n, t)
                        rsum(n, t)
                        if t < G:
                            copy_k(a, i, section, loop, t, 1, i)
                        elif not last:
                            copy_k(a, i, section, loop, t, 0, i + 1)
                        copy_v(a, i, section, loop, t)
                        if t == G:
                            dve.wait_ge(s["xb_ready"], a + 2)
                        if t > G:
                            add_out(a, i, section, loop, t - G - 1)
                    add_out(a, i, section, loop, G - 1)

                def norm(base, g):
                    count = [0]

                    def step(ins):
                        count[0] += 1
                        ins.then_inc(s["dve_step"], 1)

                    def wait_step(apart=False):
                        if apart:
                            dve.wait_ge(s["dve_step"], base + count[0] + 1)
                            dve.sem_inc(s["wait_passed"], 1)
                        else:
                            dve.wait_ge(s["dve_step"], base + count[0] + 1)

                    for b in range(NB):
                        step(nc.vector.bn_stats(stats[:, b, :], X[:, bass.ds(g * NB + b, 1), :].rearrange("p a n -> p (a n)")))
                    wait_step(apart=True)
                    for b in range(NB):
                        step(nc.vector.bn_aggr(mv[:, b, :], stats[:, b, :]))
                    wait_step()
                    step(nc.vector.tensor_scalar(var[:, :], mv[:, :, 1], 1e-5, None, ALU.add))
                    wait_step()
                    step(nc.vector.tensor_single_scalar(guess[:, :], var[:, :].bitcast(I32), 1, ALU.logical_shift_right))
                    wait_step()
                    step(nc.vector.tensor_scalar(guess[:, :], guess[:, :], -1.0, RSQRT_MAGIC, ALU.mult, ALU.add))
                    wait_step()
                    y = guess[:, :].bitcast(F32)
                    for i in range(NEWTON_STEPS):
                        step(nc.vector.scalar_tensor_tensor(out=newton[:, :], in0=y, scalar=-0.5, in1=y, op0=ALU.mult, op1=ALU.mult))
                        wait_step()
                        step(nc.vector.tensor_tensor(newton[:, :], newton[:, :], var[:, :], ALU.mult))
                        wait_step()
                        step(nc.vector.scalar_tensor_tensor(out=rstd[:, :], in0=newton[:, :], scalar=1.5, in1=y, op0=ALU.add, op1=ALU.mult))
                        wait_step()
                        y = rstd[:, :]
                    assert count[0] == NORM_STEPS
                    for b in range(NB):
                        nc.vector.tensor_scalar(xhat[:, b, :], X[:, bass.ds(g * NB + b, 1), :].rearrange("p a n -> p (a n)"),
                                                mv[:, b, 0:1], rstd[:, b:b + 1], ALU.subtract, ALU.mult).then_inc(s["xhat_ready"], 1)

                def norm_copy(section, a, g, dst, scale, shift):
                    src, freed = wait_full(dve, section, a, g, ("ln", 0))
                    nc.vector.tensor_scalar(dst, src[:, :], scale, shift, ALU.mult, ALU.add).then_inc(freed, 1)

                per_attention = G * NORM_STEPS + 2 * ATT_UNITS
                with dve.Fori(0, 2) as a:
                    at = COLS["lnA_s"][0] + a * 4
                    with dve.Fori(0, G) as g:
                        norm(a * per_attention + g * NORM_STEPS, g)
                        norm_copy("ln", a, g, hT[:, 0, bass.ds(g * R, R)], cols[:, bass.ds(at, 1)], cols[:, bass.ds(at + 2, 1)])
                    norms_before[0] = (a + 1) * (G * NORM_STEPS)
                    for t in range(G):
                        copy_k(a, 0, "pre", 0, t, 0, 0)
                    dve.wait_ge(s["vrows_ready"], 2)
                    with dve.Fori(0, PAIRS - 1) as i:
                        pair(a, i, False)
                    pair(a, PAIRS - 1, True)
                with dve.Fori(0, G) as g:
                    norm(2 * per_attention + g * NORM_STEPS, g)
                    at = COLS["lnM_s"][0]
                    norm_copy("mlp", 0, g, hT[:, 0, 0:R], cols[:, at:at + 1], cols[:, at + 2:at + 3])
                    dve.wait_ge(s["xb_ready"], 2 + g + 2)
                    for j in range(2):
                        src, freed = wait_full(dve, "mlp", 0, g, ("down", j))
                        x = X[:, bass.ds(g * NB + 2 * j, 2), :]
                        nc.vector.tensor_tensor(x, src[:, :].rearrange("p (b n) -> p b n", b=2), x, ALU.add).then_inc(freed, 1)

            @block.tensor
            def _(pe):
                seed(pe, [s["scores_ready"], s["pT_ready"], s["o_ready"]] + full)
                def transposed(section, a, g, first):
                    for c in (1, 0):
                        out, filled = wait_free(pe, section, a, g, ("ln", c))
                        for b in range(NB):
                            if c == 1:
                                pe.wait_ge(s["xhat_ready"], first + b + 2)
                            last = nc.tensor.transpose(out[:, b * P:(b + 1) * P], xhat[:, b, c * P:(c + 1) * P], ident[:, :])
                        last.then_inc(filled, 1)

                def project(at, weight, src, quarter):
                    out, filled = wait_free(pe, *at)
                    for c in range(KC):
                        last = nc.tensor.matmul(out[:, :], weight(c), src[:, c, quarter * R:(quarter + 1) * R], start=(c == 0), stop=(c == KC - 1))
                    last.then_inc(filled, 1)

                def queries_keys(section, a, i, t, head):
                    project((section, a, i, ("q", t)), lambda c: w_qk[:, head, 0, c, :], hT, t % G)
                    project((section, a, i, ("k", t)), lambda c: w_qk[:, head, 1, c, :], ctxT, t % G)

                def values(section, a, i, t):
                    head = t // G
                    out, filled = wait_free(pe, section, a, i, ("v", t))
                    for j in range(NB):
                        b = (t % G) * NB + j
                        for c in range(KC):
                            last = nc.tensor.matmul(out[:, j * P:(j + 1) * P], ctxT[:, c, b * P:(b + 1) * P], w_v[:, head, c, :], start=(c == 0), stop=(c == KC - 1))
                    last.then_inc(filled, 1)

                def weigh_values(n, t, a, section, loop):
                    head = t // G
                    pe.wait_ge(s["pT_copied"], n + 2)
                    wait_copied(pe, section, a, loop, ("v", t))
                    pe.wait_ge(s["o_copied"], n + 1)
                    for j in range(NB):
                        last = nc.tensor.matmul(o_psum[:, j * P:(j + 1) * P], v[:, head, (t % G) * NB + j, :], probsT[:, j * P:(j + 1) * P], start=True, stop=True)
                    last.then_inc(s["o_ready"], 1)

                def output(n, a, section, loop, quarter):
                    pe.wait_ge(s["o_copied"], n + 2)
                    for half in range(2):
                        out, filled = wait_free(pe, section, a, loop, ("out", quarter, half))
                        for j in range(2):
                            b = quarter * NB + 2 * half + j
                            for head in range(2):
                                last = nc.tensor.matmul(out[:, j * D:(j + 1) * D], oT[:, head, b * P:(b + 1) * P], w_o[:, head, :], start=(head == 0), stop=(head == 1))
                        last.then_inc(filled, 1)

                def pair(a, i, last_pair):
                    section, loop = pair_section(last_pair), 0 if last_pair else i
                    first = a * ATT_UNITS + i * STEPS
                    pe.wait_ge(s["w_a_loaded"], (a * PAIRS + i + 1) * 32)
                    for t in range(STEPS):
                        n = first + t
                        head = t // G
                        if t == 0:
                            wait_ready(a, i, last_pair)
                        if t >= G:
                            for name in ("q", "k"):
                                wait_copied(pe, section, a, loop, (name, t - G))
                        pe.wait_ge(s["exp_done"], (n - 1 if t >= 2 else n - t) + 1)
                        for j in range(NB):
                            b = (t % G) * NB + j
                            last = nc.tensor.matmul(scores[t % 2][:, j * P:(j + 1) * P], qT[:, head, b * P:(b + 1) * P], kT[:, head, b * P:(b + 1) * P], start=True, stop=True)
                        last.then_inc(s["scores_ready"], 1)
                        if t > 0:
                            weigh_values(n - 1, t - 1, a, section, loop)
                        if t == G:
                            pe.wait_ge(s["w_b_loaded"], (a * PAIRS + i + 1) * 32)
                            if not last_pair:
                                pe.wait_ge(s["w_qk0_loaded"], (a * PAIRS + i + 2) * 16)
                        if not (last_pair and t >= G):
                            queries_keys(section, a, loop, t, 1 - head)
                        if t < STEPS - 1:
                            values(section, a, loop, t)
                            if t > G:
                                output(n - 1, a, section, loop, t - G - 1)
                        pe.wait_ge(s["probs_ready"], n + 2)
                        pe.wait_ge(s["pT_copied"], n + 1)
                        for j in range(NB):
                            last = nc.tensor.transpose(pT_psum[:, j * P:(j + 1) * P], probs[:, t % 2, j * P:(j + 1) * P], ident[:, :])
                        last.then_inc(s["pT_ready"], 1)
                    values(section, a, loop, t)
                    output(n - 1, a, section, loop, G - 2)
                    weigh_values(n, t, a, section, loop)
                    output(n, a, section, loop, G - 1)

                def wait_ready(a, i, last_pair):
                    for k in range(NGEN):
                        count = before["pair", k] + a * before["attention", k] + i * sections["pair"].per_loop[k]
                        pe.wait_ge(free[k], count + 1)

                pe.wait_ge(s["ctxT_loaded"], 32)
                with pe.Fori(0, 2) as a:
                    with pe.Fori(0, G) as g:
                        transposed("ln", a, g, a * B + g * NB)
                    for c in range(KC):
                        wait_copied(pe, "ln", a, G - 1, ("ln", c))
                    pe.wait_ge(s["w_qk0_loaded"], a * (16 * PAIRS) + 16)
                    for t in range(G):
                        queries_keys("pre", a, 0, t, 0)
                    with pe.Fori(0, PAIRS - 1) as i:
                        pair(a, i, False)
                    pair(a, PAIRS - 1, True)
                pe.wait_ge(s["mlp_loaded"], 32)
                with pe.Fori(0, G) as g:
                    transposed("mlp", 0, g, 2 * B + g * NB)
                    for c in range(KC):
                        wait_copied(pe, "mlp", 0, g, ("ln", c))
                    for f in range(FC):
                        out, filled = wait_free(pe, "mlp", 0, g, ("up", f))
                        for c in range(KC):
                            last = nc.tensor.matmul(out[:, :], w_up[:, c, f * P:(f + 1) * P], hT[:, c, 0:R], start=(c == 0), stop=(c == KC - 1))
                        last.then_inc(filled, 1)
                    for i in range(2):
                        out, filled = wait_free(pe, "mlp", 0, g, ("down", i))
                        for j in range(2):
                            for f in range(FC):
                                if i == j == 0:
                                    wait_copied(pe, "mlp", 0, g, ("up", f))
                                last = nc.tensor.matmul(out[:, j * D:(j + 1) * D], upT[:, f, (2 * i + j) * P:(2 * i + j + 1) * P], w_down[:, f, :], start=(f == 0), stop=(f == FC - 1))
                        last.then_inc(filled, 1)


def chunked(w):
    k, n = w.shape
    return w.reshape(k // P, P, n).transpose(1, 0, 2).reshape(P, -1)


def columns(v):
    return v.reshape(-1, P).T


def by_pair(*matrices):
    stacked = np.stack([m.reshape(KC, P, PAIRS, 2, W3) for m in matrices])
    return stacked.transpose(3, 2, 4, 0, 1, 5).reshape(PAIRS, P, 2, -1)


def laid_out(x, ctx_2048, mask_1x1xSxS2_fc1, mask_Bx1xSxS2_ff1, mask_BxS2_ik0, **w):
    def padded(a, axis):
        widths = [(0, 0)] * a.ndim
        widths[axis] = (0, P - a.shape[axis])
        return np.pad(a, widths)

    l0, l1, l2, l3 = ("L0_xattn_", "L1_xattn_", "L2_xattn_", "L3_xattn_")
    qkv, b_qkv = w[l1 + "w_qkv"], w[l1 + "b_qkv"]
    kv, b_kv = w[l1 + "w_kv"], w[l1 + "b_kv"]
    lat_kv, b_lat_kv = w[l2 + "kv_w"], w[l2 + "kv_b"]
    weights = {
        "wq0": padded(w[l0 + "Wq"].T, 1), "wk0": padded(w[l0 + "Wk"].T, 1), "wv0": w[l0 + "Wv"].T,
        "self_q": qkv[:, 0:D], "self_k": qkv[:, D:2 * D], "self_v": qkv[:, 2 * D:3 * D], "self_o": w[l1 + "w_ao"],
        "cross_k": kv[:, 0:D], "cross_v": kv[:, D:2 * D], "cross_q": w[l1 + "w_q"], "cross_o": w[l1 + "w_co"],
        "mlp1_up": w[l1 + "w1"], "mlp1_down": w[l1 + "w2"],
        "lat_q": w[l2 + "q_w"], "lat_k": lat_kv[:, 0::2], "lat_v": lat_kv[:, 1::2], "lat_o": w[l2 + "out_w"],
        "mlp2_up": w[l2 + "mlp_w1"], "mlp2_down": w[l2 + "mlp_w2"],
    }
    vectors = {
        "bq0": padded(w[l0 + "bq"], 0), "bk0": padded(w[l0 + "bk"], 0), "bv0": w[l0 + "bv"],
        "ln1_s": w[l1 + "ln1_s"], "ln1_b": w[l1 + "ln1_b"], "ln2_s": w[l1 + "ln2_s"], "ln2_b": w[l1 + "ln2_b"],
        "ln3_s": w[l1 + "ln3_s"], "ln3_b": w[l1 + "ln3_b"],
        "self_bq": b_qkv[0:D], "self_bk": b_qkv[D:2 * D], "self_bv": b_qkv[2 * D:3 * D],
        "cross_bq": w[l1 + "b_q"], "cross_bk": b_kv[0:D], "cross_bv": b_kv[D:2 * D], "mlp1_b": w[l1 + "b1"],
        "lat_bq": w[l2 + "q_b"], "lat_bk": b_lat_kv[0::2], "lat_bv": b_lat_kv[1::2], "rms_w": w[l2 + "postnorm_w"],
        "mlp2_b": w[l2 + "mlp_b1"],
        "lnA_s": w[l3 + "ln1_scale"], "lnA_b": w[l3 + "ln1_offset"], "lnB_s": w[l3 + "ln2_scale"], "lnB_b": w[l3 + "ln2_offset"],
        "lnM_s": w[l3 + "ln_mlp_scale"], "lnM_b": w[l3 + "ln_mlp_offset"], "mlp3_b": w[l3 + "b_fc1"],
    }
    head_mask = np.repeat(np.eye(HPC, dtype=np.float32), HD, axis=0)
    return {
        "x": x, "ctx": ctx_2048,
        "ctxT": np.ascontiguousarray(ctx_2048.reshape(B, P, KC, P).transpose(3, 2, 0, 1)),
        "mask_self": mask_1x1xSxS2_fc1[0, 0], "mask_cross": mask_Bx1xSxS2_ff1[:, 0], "mask_lat": mask_BxS2_ik0,
        "ident": np.eye(P, dtype=np.float32),
        "cols": np.concatenate([columns(vectors[n]) if n in vectors else head_mask for n in COLS], axis=1),
        "weights_a": np.concatenate([chunked(weights[n]) for n, _, _ in WEIGHTS_A], axis=1),
        "rows_a": np.stack([w[l1 + "b_ao"], w[l1 + "b_co"], w[l1 + "b2"], w[l2 + "out_b"], w[l2 + "mlp_b2"]]),
        "rows_b": np.stack([w[l3 + "bo1"], w[l3 + "bo2"], w[l3 + "b_fc2"]]),
        "w_qk": np.concatenate([by_pair(w[l3 + f"wq{a}"], w[l3 + f"wk{a}"]) for a in (1, 2)]),
        "w_v": np.concatenate([by_pair(w[l3 + f"wv{a}"]) for a in (1, 2)]),
        "w_o": np.concatenate([w[l3 + f"wo{a}"].reshape(PAIRS, 2, P, D).transpose(0, 2, 1, 3).reshape(PAIRS, P, 2 * D) for a in (1, 2)]),
        "hcols": np.concatenate([np.stack([w[l3 + f"{n}{a}"].reshape(NH, P) for n in ("bq", "bk", "bias_k", "bias_v")], axis=1)
                                 for a in (1, 2)]).reshape(2 * NH * HCOLS, P).T,
        "vrows": np.stack([np.concatenate([w[l3 + f"{n}{a}"].reshape(-1) for a in (1, 2)]) for n in ("bv", "bias_v")]),
        "w_up": chunked(w[l3 + "w_fc1"]), "w_down": chunked(w[l3 + "w_fc2"]),
    }


def build(nc, dram):
    with ExitStack() as ctx:
        consts = {
            "ident": ctx.enter_context(nc.sbuf_tensor("ident", [P, P], F32)),
            "cols": ctx.enter_context(nc.sbuf_tensor("cols", [P, NCOLS], F32)),
            "loaded": ctx.enter_context(nc.semaphore("consts_loaded")),
        }
        stages_0_to_2(nc, dram, consts)
        stage_3(nc, dram, consts)


def kernel(**inputs):
    import concourse.bacc as bacc
    from concourse.bass_utils import run_bass_kernel_spmd

    arrays = laid_out(**{name: np.asarray(a) for name, a in inputs.items()})
    arrays = {name: np.ascontiguousarray(a) for name, a in arrays.items()}
    nc = bacc.Bacc("TRN2", target_bir_lowering=False, num_devices=1)
    dram = {name: nc.dram_tensor(name + "_dram", a.shape, mybir.dt.from_np(a.dtype), kind="ExternalInput").ap()
            for name, a in arrays.items()}
    dram["mid"] = nc.dram_tensor("mid_dram", (P, B, D), F32, kind="Internal").ap()
    dram["out"] = nc.dram_tensor("out_dram", (B, P, D), F32, kind="ExternalOutput").ap()
    build(nc, dram)
    result = run_bass_kernel_spmd(nc, [{name + "_dram": a for name, a in arrays.items()}], core_ids=[0])
    return result.results[0]["out_dram"]
```

```python
import numpy as np

import concourse.bass as bass
from concourse import mybir
from contextlib import ExitStack

F32 = mybir.dt.float32
I32 = mybir.dt.int32
F32R = mybir.dt.float32r
ALU = mybir.AluOpType
ACT = mybir.ActivationFunctionType
AX = mybir.AxisListType

P = 128
B = 16
D = 256
KC = D // P
NB = 4
G = B // NB
R = NB * P
NH = 16
HD = D // NH
HPC = P // HD
F = 1024
FC = F // P
BANK = 512
L0K = 16
W3 = 128
PAIRS = NH // 2

COLS = {}
for _name, _n in [("bq0", 1), ("bk0", 1), ("bv0", 1),
                  ("ln1_s", 2), ("ln1_b", 2), ("ln2_s", 2), ("ln2_b", 2), ("ln3_s", 2), ("ln3_b", 2),
                  ("self_bq", 2), ("self_bk", 2), ("self_bv", 2),
                  ("cross_bq", 2), ("cross_bk", 2), ("cross_bv", 2), ("mlp1_b", FC),
                  ("lat_bq", 2), ("lat_bk", 2), ("lat_bv", 2), ("rms_w", 2), ("mlp2_b", FC),
                  ("lnA_s", 2), ("lnA_b", 2), ("lnB_s", 2), ("lnB_b", 2), ("lnM_s", 2), ("lnM_b", 2),
                  ("mlp3_b", FC), ("head_mask", HPC)]:
    COLS[_name] = (sum(n for _, n in COLS.values()), _n)
NCOLS = sum(n for _, n in COLS.values())

ROWS_A = ["self_bo", "cross_bo", "mlp1_bo", "lat_bo", "mlp2_bo"]
ROWS_B = ["a_bo", "b_bo", "mlp3_bo"]

WEIGHTS_A = [("wq0", 1, P), ("wk0", 1, P), ("wv0", 1, P),
             ("self_q", KC, D), ("self_k", KC, D), ("self_v", KC, D), ("self_o", KC, D),
             ("cross_k", KC, D), ("cross_v", KC, D), ("cross_q", KC, D), ("cross_o", KC, D),
             ("mlp1_up", KC, F), ("mlp1_down", FC, D),
             ("lat_q", KC, D), ("lat_k", KC, D), ("lat_v", KC, D), ("lat_o", KC, D),
             ("mlp2_up", KC, F), ("mlp2_down", FC, D)]

NEG = -1.0e30
RSQRT_MAGIC = 1597463007.0
UNITS = {"chan": NB, "self": 4 * NB, "cross": 4 * NB, "lat": 8 * NB}
FIRST_UNIT = {"chan": 0, "self": 4, "cross": 20, "lat": 36}
NU = sum(UNITS.values())
BLOCK_UNITS = {"chan": 1, "self": 2, "cross": 2, "lat": 4}
BLOCKS = KC * NB
SCORES_AHEAD = 3

def qkv_uses(name):
    return [(name + "_q", 0), (name + "_k", 0), (name + "_v", 0), (name + "_v", 1), (name + "_q", 1), (name + "_k", 1)]


USES_A = ([("chan_q", i) for i in range(2)] + [("chan_k", i) for i in range(2)] + [("chan_v", i) for i in range(2)]
          + [("ln1", c) for c in range(KC)]
          + qkv_uses("self") + [("self_o", b) for b in range(NB)]
          + [("cross_k", c) for c in range(KC)] + [("cross_v", i) for i in range(2)]
          + [("ln2", c) for c in range(KC)] + [("cross_q", c) for c in range(KC)]
          + [("cross_o", b) for b in range(NB)]
          + [("ctx_k", c) for c in range(KC)] + [("ctx_v", i) for i in range(2)]
          + [("ln3", c) for c in range(KC)]
          + [("mlp1_up", f) for f in range(FC)] + [("mlp1_down", i) for i in range(2)]
          + [("lat", c) for c in range(KC)]
          + qkv_uses("lat") + [("lat_o", b) for b in range(NB)]
          + [("rms", c) for c in range(KC)]
          + [("mlp2_up", f) for f in range(FC)] + [("mlp2_down", i) for i in range(2)])
NBANKS_A = 2

NEWTON_STEPS = 3
NORM_STEPS = 2 * NB + 1 + 2 + 3 * NEWTON_STEPS
MASKED_UNITS = UNITS["self"] + UNITS["cross"]
DVE_STEPS_A = 4 * NORM_STEPS + 1


def seed(eng, sems):
    for sem in sems:
        eng.sem_inc(sem, 1)


class Banks:

    def __init__(self, uses, banks, first=0):
        self.at = {key: ((first + i) % banks, (first + i) // banks) for i, key in enumerate(uses)}
        assert len(self.at) == len(uses)
        self.per_loop = [sum(b == k for b, _ in self.at.values()) for k in range(banks)]

    def __getitem__(self, key):
        return self.at[key]


def stages_0_to_2(nc, dram, consts):
    ident, cols = consts["ident"], consts["cols"]

    def col(name, c=0):
        at, n = COLS[name]
        assert c < n
        return cols[:, at + c:at + c + 1]

    with ExitStack() as ctx:
        def sb(name, shape, dt=F32):
            return ctx.enter_context(nc.sbuf_tensor(name, shape, dt))

        def sem(name):
            return ctx.enter_context(nc.semaphore(name))

        total = sum(k * n for _, k, n in WEIGHTS_A)
        weights = sb("weights_a", [P, total])
        w, at = {}, 0
        for name, k, n in WEIGHTS_A:
            w[name] = weights[:, at:at + k * n].rearrange("p (k n) -> p k n", k=k)
            at += k * n
        split = [0, 3 * P, at]
        rows = sb("rows_a", [P, len(ROWS_A), D])
        mask_self = sb("mask_self", [P, P])
        madd_self = sb("madd_self", [P, P])
        mask_cross = sb("mask_cross", [P, NB, P])
        madd_cross = sb("madd_cross", [P, NB, P])
        mask_lat = sb("mask_lat", [P, NB, P], I32)
        madd_lat = sb("madd_lat", [P, NB, 2 * P])

        x_in = sb("x_in", [P, NB, D])
        ctx_in = sb("ctx_in", [P, NB, D])
        ctxT = sb("ctxT", [P, KC, NB, P])
        X = sb("X", [P, NB, D])
        Xb = sb("Xb", [P, NB, D])
        xhat = sb("xhat", [P, NB, D])
        hT = sb("hT", [P, KC, R])
        qT = sb("qT", [P, KC, R])
        big = sb("big", [P, NH * R])
        qm = big[:, :].rearrange("p (h r) -> p h r", h=NH)
        upT = big[:, 0:FC * R].rearrange("p (f r) -> p f r", f=FC)
        q0T = big[:, 0:NB * D]
        k0T = big[:, NB * D:2 * NB * D]
        v0T = big[:, 2 * NB * D:3 * NB * D].rearrange("p (b m c) -> p b m c", b=NB, m=2)
        kT_self = sb("kT_self", [P, KC, R])
        v_self = sb("v_self", [P, NB, NH * 2 * HD])
        kT_lat = sb("kT_lat", [P, KC, NB, 2, P])
        v_lat = sb("v_lat", [P, 2, NB, NH * 2 * HD])
        masked = sb("masked", [P, 2, BANK])
        negated = sb("negated", [P, 3, BANK])
        probs = sb("probs", [P, 4, BANK])
        probsT = sb("probsT", [P, 2, BANK])
        oT = sb("oT", [P, KC, NB, P])
        negmax = sb("negmax", [P, 4, 4])
        sums = sb("sums", [P, 4, 4])
        rsums = sb("rsums", [P, 4, 4])
        stats = sb("stats", [P, NB, 6])
        mv = sb("mv", [P, NB, 2])
        var = sb("var", [P, NB])
        guess = sb("guess", [P, NB], I32)
        rstd = sb("rstd", [P, NB])
        newton = sb("newton", [P, NB])

        def bank(name):
            return ctx.enter_context(nc.psum_tensor(name, [P, BANK], F32))

        scores = [bank(f"scores{i}") for i in range(2)]
        pT_psum = [bank(f"pT_psum{i}") for i in range(2)]
        o_psum = [bank(f"o_psum{i}") for i in range(2)]
        general = [bank(f"general{i}") for i in range(NBANKS_A)]
        uses = Banks(USES_A, NBANKS_A)

        s = {n: sem(n) for n in (
            "weights0_loaded", "weights_loaded", "rows_loaded", "mask_self_loaded", "x_loaded", "ctx_loaded",
            "ctxT_loaded", "mask_cross_loaded", "mask_lat_loaded", "mid_stored", "x_released",
            "v_zeroed", "madd_self_ready", "madd_cross_ready", "madd_lat_ready",
            "scores_ready", "scores_free", "max_ready", "exp_done", "rsum_ready", "probs_ready",
            "pT_ready", "pT_copied", "pv_done", "o_copied",
            "xb_ready", "xhat_ready", "qm_dve", "qm_pool", "chan_done", "cross_done", "ctx_used", "dve_step", "wait_passed")}
        full = [sem(f"general_full{i}") for i in range(NBANKS_A)]
        free = [sem(f"general_free{i}") for i in range(NBANKS_A)]

        def wait_full(eng, g, key):
            k, n = uses[key]
            eng.wait_ge(full[k], g * uses.per_loop[k] + n + 2)
            return general[k], free[k]

        def wait_free(eng, g, key):
            k, n = uses[key]
            eng.wait_ge(free[k], g * uses.per_loop[k] + n + 1)
            return general[k], full[k]

        def wait_copied(eng, g, key):
            k, n = uses[key]
            eng.wait_ge(free[k], g * uses.per_loop[k] + n + 2)

        def wait_x(eng, g, after):
            if after == "chan":
                eng.wait_ge(s["chan_done"], g * NB + NB + 1)
            elif after.startswith("mlp"):
                for i in range(2):
                    wait_copied(eng, g, (after + "_down", i))
            else:
                for b in range(NB):
                    wait_copied(eng, g, (after + "_o", b))

        def unit_parts(kind, u):
            block, i = divmod(u, BLOCK_UNITS[kind])
            c, b = divmod(block, NB)
            return c, b, i, {"chan": 2, "self": 4, "cross": 4, "lat": 2}[kind]

        NTH = {"self": 0, "cross": 1, "lat": 2}
        XHAT_AFTER = {"ln1": 4, "ln2": 8, "ln3": 12, "rms": 16}
        XB_AFTER = {"self": 1, "cross": 2, "mlp1": 3, "lat": 4, "mlp2": 5}
        ROW_OF = {"self": 0, "cross": 1, "mlp1": 2, "lat": 3, "mlp2": 4}

        with nc.Block() as block:

            @block.sync
            def _(sp):
                sp.dma_start(ident[:, :], dram["ident"]).then_inc(consts["loaded"], 16)
                sp.dma_start(cols[:, :], dram["cols"]).then_inc(consts["loaded"], 16)
                sp.dma_start(weights[:, 0:split[1]], dram["weights_a"][:, 0:split[1]]).then_inc(s["weights0_loaded"], 16)
                with sp.Fori(0, G) as g:
                    sp.wait_ge(s["chan_done"], g * NB + 1)
                    sp.dma_start(x_in[:, :, :], dram["x"][bass.ds(g * NB, NB), :, :].rearrange("b p n -> p b n")).then_inc(s["x_loaded"], 16)
                    sp.dma_start(ctx_in[:, :, :], dram["ctx"][bass.ds(g * NB, NB), :, :].rearrange("b p n -> p b n")).then_inc(s["ctx_loaded"], 16)
                    sp.wait_ge(s["cross_done"], g + 1)
                    sp.dma_start(mask_cross[:, :, :], dram["mask_cross"][bass.ds(g * NB, NB), :, :].rearrange("b p n -> p b n")).then_inc(s["mask_cross_loaded"], 16)
                    sp.wait_ge(s["ctx_used"], g + 1)
                    for c in range(KC):
                        sp.dma_start(ctxT[:, c, :, :], dram["ctxT"][:, c, bass.ds(g * NB, NB), :]).then_inc(s["ctxT_loaded"], 16)
                    sp.wait_ge(s["madd_lat_ready"], g + 1)
                    sp.dma_start(mask_lat[:, :, :], dram["mask_lat"][bass.ds(g * NB, NB), :].partition_broadcast(P)).then_inc(s["mask_lat_loaded"], 16)

            @block.gpsimd
            def _(pool):
                seed(pool, [s["probs_ready"], s["qm_pool"], s["xb_ready"], s["madd_self_ready"], s["madd_cross_ready"], s["madd_lat_ready"],
                            s["v_zeroed"], s["x_released"]])
                nc.gpsimd.memset(v_self[:, :, :], 0.0).then_inc(s["v_zeroed"], 1)
                nc.gpsimd.memset(v_lat[:, :, :, :], 0.0).then_inc(s["v_zeroed"], 1)
                nc.gpsimd.memset(madd_lat[:, :, :], 0.0).then_inc(s["v_zeroed"], 1)
                pool.wait_ge(s["mask_self_loaded"], 16)
                nc.gpsimd.tensor_scalar(madd_self[:, :], mask_self[:, :], -1.0, 10000.0, ALU.add, ALU.mult).then_inc(s["madd_self_ready"], 1)
                with pool.Fori(0, G) as g:

                    def add_bias(name):
                        x_after = {"self": "chan", "cross": "self", "mlp1": "cross", "lat": "mlp1", "mlp2": "mlp1"}[name]
                        wait_x(pool, g, x_after)
                        if name == "mlp2":
                            pool.wait_ge(s["xhat_ready"], g * 16 + XHAT_AFTER["rms"] + 1)
                        nc.gpsimd.tensor_tensor(Xb[:, :, :], X[:, :, :],
                                                rows[:, ROW_OF[name]:ROW_OF[name] + 1, :].broadcast_to([P, NB, D]),
                                                ALU.add).then_inc(s["xb_ready"], 1)

                    def normalise(kind):
                        for u in range(UNITS[kind]):
                            n = FIRST_UNIT[kind] + u
                            segs = unit_parts(kind, u)[3]
                            pr = probs[:, n % 4, :].rearrange("p (s k) -> p s k", s=segs)
                            pool.wait_ge(s["rsum_ready"], g * NU + n + 2)
                            nc.gpsimd.tensor_tensor(pr, pr, rsums[:, n % 4, 0:segs].unsqueeze(2).broadcast_to([P, segs, BANK // segs]),
                                                    ALU.mult).then_inc(s["probs_ready"], 1)
                            if kind != "chan" and u < HPC - 1:
                                for h in range(2) if u == 0 else [u + 1]:
                                    mask_head(kind, h)

                    def mask_head(kind, h):
                        wait_copied(pool, g, (kind + "_q", 1))
                        mask = COLS["head_mask"][0] + h
                        nc.gpsimd.tensor_tensor(qm[:, HPC + h, :], qT[:, 1, :], cols[:, mask:mask + 1].broadcast_to([P, R]), ALU.mult).then_inc(s["qm_pool"], 1)

                    normalise("chan")
                    pool.wait_ge(s["rows_loaded"], 16)
                    add_bias("self")
                    pool.wait_ge(s["mask_cross_loaded"], g * 16 + 16)
                    pool.sem_inc(s["wait_passed"], 1)
                    nc.gpsimd.tensor_scalar(madd_cross[:, :, :], mask_cross[:, :, :], -1.0, 10000.0, ALU.add, ALU.mult).then_inc(s["madd_cross_ready"], 1)
                    normalise("self")
                    add_bias("cross")
                    normalise("cross")
                    add_bias("mlp1")
                    pool.wait_ge(s["v_zeroed"], 4)
                    pool.wait_ge(s["mask_lat_loaded"], g * 16 + 16)
                    pool.sem_inc(s["wait_passed"], 1)
                    nc.gpsimd.tensor_scalar(madd_lat[:, :, 0:P], mask_lat[:, :, :], 0.0, NEG, ALU.is_equal, ALU.mult).then_inc(s["madd_lat_ready"], 1)
                    add_bias("lat")
                    normalise("lat")
                    add_bias("mlp2")
                    wait_x(pool, g, "mlp2")
                    pool.dma_start(dram["mid"][:, bass.ds(g * NB, NB), :], X[:, :, :]).then_inc(s["mid_stored"], 16)
                    pool.wait_ge(s["mid_stored"], g * 16 + 16)
                    pool.sem_inc(s["x_released"], 1)

            @block.scalar
            def _(act):
                seed(act, [s["exp_done"], s["pT_copied"], s["o_copied"]])
                act.dma_start(weights[:, split[1]:split[2]], dram["weights_a"][:, split[1]:split[2]]).then_inc(s["weights_loaded"], 16)
                act.dma_start(mask_self[:, :], dram["mask_self"]).then_inc(s["mask_self_loaded"], 16)
                act.dma_start(rows[:, :, :], dram["rows_a"].partition_broadcast(P)).then_inc(s["rows_loaded"], 16)
                act.wait_ge(consts["loaded"], 32)
                with act.Fori(0, G) as g:

                    def exps(kind, u):
                        n = FIRST_UNIT[kind] + u
                        segs = unit_parts(kind, u)[3]
                        width = BANK // segs
                        act.wait_ge(s["max_ready"], g * NU + n + 2)
                        act.wait_ge(s["pT_ready"], (g * NU + n - 3 if n >= 4 else g * NU) + 1)
                        for i in range(segs):
                            src = scores[n % 2] if kind == "chan" else negated[:, n % 3, :]
                            last = nc.scalar.activation(probs[:, n % 4, i * width:(i + 1) * width], src[:, i * width:(i + 1) * width],
                                                        ACT.Exp, scale=1.0 if kind == "chan" else -1.0, bias=negmax[:, n % 4, i:i + 1], accum_out=sums[:, n % 4, i:i + 1])
                            if i == segs - 1:
                                last.then_inc(s["exp_done"], 1)

                    def copy_pT(kind, u):
                        n = FIRST_UNIT[kind] + u
                        act.wait_ge(s["pT_ready"], g * NU + n + 2)
                        act.wait_ge(s["pv_done"], (g * NU + n - 1 if n >= 2 else g * NU) + 1)
                        nc.scalar.copy(probsT[:, n % 2, :], pT_psum[n % 2][:, :]).then_inc(s["pT_copied"], 1)

                    def copy_o(kind, block):
                        act.wait_ge(s["pv_done"], g * NU + FIRST_UNIT[kind] + (block + 1) * BLOCK_UNITS[kind] + 1)
                        c, b = divmod(block, NB)
                        nc.scalar.activation(oT[:, c, b, :], o_psum[block % 2][:, 0:P], ACT.Identity,
                                             bias=col(kind + "_bv", c)).then_inc(s["o_copied"], 1)

                    def attention(kind, meanwhile={}):
                        n = UNITS[kind]
                        per = BLOCK_UNITS[kind]
                        for t in range(n + SCORES_AHEAD + 2):
                            if 0 <= t - SCORES_AHEAD < n:
                                copy_pT(kind, t - SCORES_AHEAD)
                            if t < n:
                                exps(kind, t)
                            if t in meanwhile:
                                meanwhile[t]()
                            done = t - SCORES_AHEAD - 1
                            if kind != "chan" and 0 <= done < n and done % per == per - 1:
                                copy_o(kind, done // per)

                    def norm_copy(name):
                        src, freed = wait_full(act, g, (name, 1))
                        if name == "lat":
                            ins = nc.scalar.copy(hT[:, 1, :], src[:, :])
                        elif name == "rms":
                            ins = nc.scalar.activation(hT[:, 1, :], src[:, :], ACT.Copy, scale=col("rms_w", 1))
                        else:
                            ins = nc.scalar.activation(hT[:, 1, :], src[:, :], ACT.Identity, scale=col(name + "_s", 1), bias=col(name + "_b", 1))
                        ins.then_inc(freed, 1)

                    def keys(name, bias, out, split_b, chunks=range(KC)):
                        for c in chunks:
                            src, freed = wait_full(act, g, (name + "_k", c))
                            if split_b:
                                src = src[:, :].rearrange("p (b k) -> p b k", b=NB)
                            else:
                                src = src[:, :]
                            nc.scalar.activation(out[c], src, ACT.Identity, bias=col(bias + "_bk", c)).then_inc(freed, 1)

                    def values(name, out, halves=range(2)):
                        for i in halves:
                            src, freed = wait_full(act, g, (name + "_v", i))
                            for j in range(2):
                                dst = out[:, 2 * i + j, :].rearrange("p (t w d) -> p t w d", w=4, d=HD)[:, :, 0:4:3, :]
                                ins = nc.scalar.copy(dst, src[:, j * D:(j + 1) * D].rearrange("p (t w d) -> p t w d", w=2, d=HD))
                            ins.then_inc(freed, 1)

                    def gelus(name):
                        for f in range(FC):
                            src, freed = wait_full(act, g, (name + "_up", f))
                            nc.scalar.activation(upT[:, f, :], src[:, :], ACT.Gelu_apprx_tanh, bias=col(name + "_b", f)).then_inc(freed, 1)

                    for i in range(2):
                        src, freed = wait_full(act, g, ("chan_q", i))
                        nc.scalar.activation(q0T[:, i * BANK:(i + 1) * BANK], src[:, :], ACT.Identity, bias=col("bq0")).then_inc(freed, 1)
                    attention("chan")
                    norm_copy("ln1")
                    act.wait_ge(s["v_zeroed"], 3)
                    kT = [kT_self[:, c, :] for c in range(KC)]
                    keys("self", "self", kT, False, [0])
                    attention("self", {0: lambda: values("self", v_self, [0]), 1: lambda: values("self", v_self, [1]),
                                       3: lambda: keys("self", "self", kT, False, [1])})
                    kT_ctx = [kT_lat[:, c, :, 0, :] for c in range(KC)]
                    keys("cross", "cross", kT_ctx, True)
                    values("cross", v_lat[:, 0, :, :])
                    norm_copy("ln2")
                    attention("cross")
                    keys("ctx", "lat", kT_ctx, True)
                    values("ctx", v_lat[:, 0, :, :])
                    norm_copy("ln3")
                    gelus("mlp1")
                    norm_copy("lat")
                    kT_own, v_own = [kT_lat[:, c, :, 1, :] for c in range(KC)], v_lat[:, 1, :, :]
                    keys("lat", "lat", kT_own, True, [0])
                    attention("lat", {0: lambda: values("lat", v_own, [0]), 1: lambda: values("lat", v_own, [1]),
                                      3: lambda: keys("lat", "lat", kT_own, True, [1])})
                    norm_copy("rms")
                    gelus("mlp2")

            @block.vector
            def _(dve):
                seed(dve, [s["max_ready"], s["rsum_ready"], s["chan_done"], s["cross_done"], s["scores_free"], s["qm_dve"],
                           s["xhat_ready"], s["dve_step"]] + free)
                dve.wait_ge(consts["loaded"], 32)
                with dve.Fori(0, G) as g:
                    steps = [0]

                    def step(ins):
                        steps[0] += 1
                        ins.then_inc(s["dve_step"], 1)

                    def wait_step(apart=False):
                        value = g * DVE_STEPS_A + steps[0]
                        if apart:
                            dve.wait_ge(s["dve_step"], value + 1)
                            dve.sem_inc(s["wait_passed"], 1)
                        else:
                            dve.wait_ge(s["dve_step"], value + 1)

                    def front(kind, u):
                        n = FIRST_UNIT[kind] + u
                        c, b, i, segs = unit_parts(kind, u)
                        dve.wait_ge(s["scores_ready"], g * NU + n + 2)
                        ready = scores[n % 2][:, :].rearrange("p (s k) -> p s k", s=segs)
                        if kind != "chan":
                            m = masked[:, n % 2, :].rearrange("p (s k) -> p s k", s=segs)
                            dve.wait_ge(s["exp_done"], g * NU + n - 1)
                        before = g * NU + n - 3 if n >= 4 else g * NU
                        if kind == "chan":
                            dve.wait_ge(s["exp_done"], before + 1)
                            nc.vector.tensor_reduce(negmax[:, n % 4, 0:segs], ready, axis=AX.X, op=ALU.max, negate=True).then_inc(s["max_ready"], 1)
                            return
                        if kind == "lat":
                            add = madd_lat[:, b, :]
                            dve.wait_ge(s["exp_done"], before + 1)
                            dve.sem_inc(s["wait_passed"], 1)
                        else:
                            mul, add = (mask_self[:, :].unsqueeze(1), madd_self[:, :]) if kind == "self" else (mask_cross[:, b:b + 1, :], madd_cross[:, b, :])
                            nc.vector.tensor_tensor(m, ready, mul.broadcast_to([P, segs, P]), ALU.mult).then_inc(s["scores_free"], 1)
                            dve.wait_ge(s["exp_done"], before + 1)
                            dve.wait_ge(s["scores_free"], g * MASKED_UNITS + n + 1 - FIRST_UNIT["self"] + 1)
                            dve.sem_inc(s["wait_passed"], 1)
                            ready = m
                        for j in range(segs):
                            last = nc.vector.tensor_tensor_reduce(out=negated[:, n % 3, j * (BANK // segs):(j + 1) * (BANK // segs)],
                                                                  in0=ready[:, j, :], in1=add, scale=-1.0, scalar=3.0e38, op0=ALU.add, op1=ALU.min,
                                                                  accum_out=negmax[:, n % 4, j:j + 1])
                        last.then_inc(s["max_ready"], 1)

                    def rsum(kind, u):
                        n = FIRST_UNIT[kind] + u
                        segs = unit_parts(kind, u)[3]
                        dve.wait_ge(s["exp_done"], g * NU + n + 2)
                        dve.wait_ge(s["probs_ready"], (g * NU + n - 3 if n >= 4 else g * NU) + 1)
                        nc.vector.reciprocal(rsums[:, n % 4, 0:segs], sums[:, n % 4, 0:segs]).then_inc(s["rsum_ready"], 1)

                    def residual(kind, b):
                        src, freed = wait_full(dve, g, (kind + "_o", b))
                        dst = Xb if kind == "lat" else X
                        if b == 0:
                            dve.wait_ge(s["xb_ready"], g * 5 + XB_AFTER[kind] + 1)
                        nc.vector.tensor_tensor(dst[:, b, :], src[:, 0:D], Xb[:, b, :], ALU.add).then_inc(freed, 1)

                    def chan_residual(b):
                        dve.wait_ge(s["pv_done"], g * NU + b + 2)
                        if b == 0:
                            dve.wait_ge(s["x_released"], g + 1)
                        nc.vector.scalar_tensor_tensor(out=X[:, b, :], in0=o_psum[b % 2][:, 0:D], scalar=col("bv0"), in1=x_in[:, b, :],
                                                       op0=ALU.add, op1=ALU.add).then_inc(s["chan_done"], 1)

                    def attention(kind, meanwhile={}):
                        n = UNITS[kind]
                        per = BLOCK_UNITS[kind]
                        for t in range(n + SCORES_AHEAD + 4):
                            if t < n:
                                front(kind, t)
                            if 0 <= t - 1 < n:
                                rsum(kind, t - 1)
                            if t in meanwhile:
                                meanwhile[t]()
                            done = t - SCORES_AHEAD - (2 if kind == "chan" else 3)
                            if 0 <= done < n and done % per == per - 1 and (kind == "chan" or done // per >= NB):
                                b = done // per % NB
                                if kind == "chan":
                                    chan_residual(b)
                                    dve.wait_ge(s["chan_done"], g * NB + b + 2)
                                else:
                                    residual(kind, b)
                                    wait_copied(dve, g, (kind + "_o", b))
                                step(nc.vector.bn_stats(stats[:, b, :], (Xb if kind == "lat" else X)[:, b, :]))

                    def norm(name):
                        src = Xb if name == "rms" else X
                        wait_step(apart=True)
                        for b in range(NB):
                            step(nc.vector.bn_aggr(mv[:, b, :], stats[:, b, :]))
                        wait_step()
                        if name == "rms":
                            step(nc.vector.tensor_tensor(newton[:, :], mv[:, :, 0], mv[:, :, 0], ALU.mult))
                            wait_step()
                            step(nc.vector.scalar_tensor_tensor(out=var[:, :], in0=mv[:, :, 1], scalar=1e-6, in1=newton[:, :], op0=ALU.add, op1=ALU.add))
                        else:
                            step(nc.vector.tensor_scalar(var[:, :], mv[:, :, 1], 1e-5, None, ALU.add))
                        wait_step()
                        inverse_root()
                        for b in range(NB):
                            if name == "rms":
                                ins = nc.vector.tensor_scalar(xhat[:, b, :], src[:, b, :], rstd[:, b:b + 1], None, ALU.mult)
                            else:
                                ins = nc.vector.tensor_scalar(xhat[:, b, :], src[:, b, :], mv[:, b, 0:1], rstd[:, b:b + 1], ALU.subtract, ALU.mult)
                            ins.then_inc(s["xhat_ready"], 1)

                    def inverse_root():
                        step(nc.vector.tensor_single_scalar(guess[:, :], var[:, :].bitcast(I32), 1, ALU.logical_shift_right))
                        wait_step()
                        step(nc.vector.tensor_scalar(guess[:, :], guess[:, :], -1.0, RSQRT_MAGIC, ALU.mult, ALU.add))
                        wait_step()
                        y = guess[:, :].bitcast(F32)
                        for i in range(NEWTON_STEPS):
                            step(nc.vector.scalar_tensor_tensor(out=newton[:, :], in0=y, scalar=-0.5, in1=y, op0=ALU.mult, op1=ALU.mult))
                            wait_step()
                            step(nc.vector.tensor_tensor(newton[:, :], newton[:, :], var[:, :], ALU.mult))
                            wait_step()
                            step(nc.vector.scalar_tensor_tensor(out=rstd[:, :], in0=newton[:, :], scalar=1.5, in1=y, op0=ALU.add, op1=ALU.mult))
                            wait_step()
                            y = rstd[:, :]

                    def norm_copy(name):
                        src, freed = wait_full(dve, g, (name, 0))
                        if name == "lat":
                            ins = nc.vector.tensor_copy(hT[:, 0, :], src[:, :])
                        elif name == "rms":
                            ins = nc.vector.tensor_scalar(hT[:, 0, :], src[:, :], col("rms_w", 0), None, ALU.mult)
                        else:
                            ins = nc.vector.tensor_scalar(hT[:, 0, :], src[:, :], col(name + "_s", 0), col(name + "_b", 0), ALU.mult, ALU.add)
                        ins.then_inc(freed, 1)

                    def queries(i, kind, chunks):
                        scale = 1.0 / HD if kind == "lat" else HD ** -0.5
                        for c in chunks:
                            src, freed = wait_full(dve, g, (kind + "_q", c))
                            if c == 1:
                                dve.wait_ge(s["qm_pool"], (g * 3 + i) * HPC + 1)
                            nc.vector.tensor_scalar(qT[:, c, :], src[:, :], col(kind + "_bq", c), scale, ALU.add, ALU.mult).then_inc(freed, 1)
                        if 0 not in chunks:
                            return
                        wait_copied(dve, g, (kind + "_q", 0))
                        for h in range(HPC):
                            nc.vector.tensor_scalar(qm[:, h, :], qT[:, 0, :], col("head_mask", h), None, ALU.mult).then_inc(s["qm_dve"], 1)

                    def mlp_residual(name):
                        dve.wait_ge(s["xb_ready"], g * 5 + XB_AFTER[name] + 1)
                        for i in range(2):
                            src, freed = wait_full(dve, g, (name + "_down", i))
                            nc.vector.tensor_tensor(X[:, 2 * i:2 * i + 2, :], src[:, :].rearrange("p (b n) -> p b n", b=2),
                                                    Xb[:, 2 * i:2 * i + 2, :], ALU.add).then_inc(freed, 1)

                    for i in range(2):
                        src, freed = wait_full(dve, g, ("chan_k", i))
                        nc.vector.tensor_scalar(k0T[:, i * BANK:(i + 1) * BANK], src[:, :], col("bk0"), None, ALU.add).then_inc(freed, 1)
                    for i in range(2):
                        src, freed = wait_full(dve, g, ("chan_v", i))
                        nc.vector.tensor_copy(v0T[:, 2 * i:2 * i + 2, :, :], src[:, :].rearrange("p (b m c) -> p b m c", b=2, m=2)).then_inc(freed, 1)
                    attention("chan")
                    norm("ln1")
                    norm_copy("ln1")
                    queries(0, "self", [0])
                    dve.wait_ge(s["madd_self_ready"], 2)
                    attention("self", {2: lambda: queries(0, "self", [1])})
                    norm("ln2")
                    norm_copy("ln2")
                    queries(1, "cross", [0])
                    dve.wait_ge(s["madd_cross_ready"], g + 2)
                    attention("cross", {2: lambda: queries(1, "cross", [1])})
                    norm("ln3")
                    dve.sem_inc(s["cross_done"], 1)
                    norm_copy("ln3")
                    mlp_residual("mlp1")
                    norm_copy("lat")
                    queries(2, "lat", [0])
                    dve.wait_ge(s["madd_lat_ready"], g + 2)
                    attention("lat", {2: lambda: queries(2, "lat", [1])})
                    norm("rms")
                    norm_copy("rms")
                    mlp_residual("mlp2")
                    assert steps[0] == DVE_STEPS_A, steps

            @block.tensor
            def _(pe):
                seed(pe, [s["scores_ready"], s["pT_ready"], s["pv_done"], s["ctx_used"]] + full)
                pe.wait_ge(consts["loaded"], 32)
                pe.wait_ge(s["weights0_loaded"], 16)
                with pe.Fori(0, G) as g:

                    def transposed(name):
                        src = X if name == "lat" else xhat
                        for c in range(KC):
                            out, filled = wait_free(pe, g, (name, c))
                            for b in range(NB):
                                if name == "lat":
                                    if c == b == 0:
                                        wait_x(pe, g, "mlp1")
                                elif c == 0:
                                    pe.wait_ge(s["xhat_ready"], g * 16 + XHAT_AFTER[name] - NB + b + 2)
                                last = nc.tensor.transpose(out[:, b * P:(b + 1) * P], src[:, b, c * P:(c + 1) * P], ident[:, :])
                            last.then_inc(filled, 1)

                    def project(key, weight, chunk, rhs):
                        out, filled = wait_free(pe, g, key)
                        for c in range(KC):
                            last = nc.tensor.matmul(out[:, :], w[weight][:, c, chunk * P:(chunk + 1) * P], rhs[c], start=(c == 0), stop=(c == KC - 1))
                        last.then_inc(filled, 1)

                    def project_rows(key, weight, i, lhs):
                        out, filled = wait_free(pe, g, key)
                        for j in range(2):
                            for c in range(KC):
                                last = nc.tensor.matmul(out[:, j * D:(j + 1) * D], lhs(c, 2 * i + j), w[weight][:, c, :], start=(c == 0), stop=(c == KC - 1))
                        last.then_inc(filled, 1)

                    def scores_of(kind, u):
                        n = FIRST_UNIT[kind] + u
                        c, b, i, segs = unit_parts(kind, u)
                        old = n - 2
                        if old < FIRST_UNIT["self"] and old >= 0:
                            pe.wait_ge(s["exp_done"], g * NU + old + 2)
                        elif 0 <= old < FIRST_UNIT["lat"]:
                            pe.wait_ge(s["scores_free"], g * MASKED_UNITS + old + 1 - FIRST_UNIT["self"] + 1)
                        else:
                            pe.wait_ge(s["max_ready"], g * NU + max(old + 1, 0) + 1)
                        out = scores[n % 2]
                        if kind != "chan" and b == 0:
                            nth = NTH[kind]
                            pe.wait_ge(s["qm_pool" if c else "qm_dve"], (g * 3 + nth) * HPC + segs * (i + 1) + 1)
                            if i == 0:
                                wait_copied(pe, g, (kind + "_k", c))
                        for j in range(segs):
                            if kind == "chan":
                                last = nc.tensor.matmul(out[:, j * D:(j + 1) * D], q0T[:, b * D + j * P:b * D + (j + 1) * P], k0T[:, b * D:(b + 1) * D], start=True, stop=True)
                            elif kind == "lat":
                                h = c * HPC + 2 * i + j
                                last = nc.tensor.matmul(out[:, j * D:(j + 1) * D], qm[:, h, b * P:(b + 1) * P],
                                                        kT_lat[:, c, b, :, :], start=True, stop=True)
                            else:
                                h = c * HPC + 4 * i + j
                                key = kT_self[:, c, b * P:(b + 1) * P] if kind == "self" else kT_lat[:, c, b, 0, :]
                                last = nc.tensor.matmul(out[:, j * P:(j + 1) * P], qm[:, h, b * P:(b + 1) * P], key, start=True, stop=True)
                        last.then_inc(s["scores_ready"], 1)

                    def transpose_probs(kind, u):
                        n = FIRST_UNIT[kind] + u
                        pe.wait_ge(s["probs_ready"], g * NU + n + 2)
                        pe.wait_ge(s["pT_copied"], (g * NU + n - 1 if n >= 2 else g * NU) + 1)
                        for j in range(4):
                            at = (j % 2) * 2 + j // 2 if kind == "chan" else j
                            last = nc.tensor.transpose(pT_psum[n % 2][:, at * P:(at + 1) * P], probs[:, n % 4, j * P:(j + 1) * P], ident[:, :])
                        last.then_inc(s["pT_ready"], 1)

                    def weigh_values(kind, u):
                        n = FIRST_UNIT[kind] + u
                        c, b, i, segs = unit_parts(kind, u)
                        pe.wait_ge(s["pT_copied"], g * NU + n + 2)
                        block = c * NB + b
                        if i == 0:
                            if kind == "chan":
                                if b >= 2:
                                    pe.wait_ge(s["chan_done"], g * NB + b)
                                else:
                                    pe.wait_ge(s["o_copied"], g * 3 * BLOCKS + 1)
                            elif kind == "self" and block < 2:
                                pe.wait_ge(s["chan_done"], g * NB + NB - 1 + block + 1)
                            else:
                                pe.wait_ge(s["o_copied"], g * 3 * BLOCKS + BLOCKS * NTH[kind] + block)
                            if kind != "chan" and block == 0:
                                for half in range(2):
                                    wait_copied(pe, g, (kind + "_v", half))
                        pT = probsT[:, n % 2, :]
                        out = o_psum[block % 2]
                        if kind == "chan":
                            for m in range(2):
                                last = nc.tensor.matmul(out[:, 0:D], v0T[:, b, m, :], pT[:, m * D:(m + 1) * D], start=(m == 0), stop=(m == 1))
                        elif kind == "lat":
                            for j in range(2):
                                h = c * HPC + 2 * i + j
                                for m in range(2):
                                    last = nc.tensor.matmul(out[32 * i:32 * i + 32, 0:P], v_lat[:, m, b, 32 * h:32 * h + 32],
                                                            pT[:, (2 * j + m) * P:(2 * j + m + 1) * P], start=(j == 0 and m == 0), stop=(j == 1 and m == 1))
                        else:
                            for j in range(4):
                                h = c * HPC + 4 * i + j
                                row = 32 * (h // 2 % 4)
                                v = v_self[:, b, 32 * h:32 * h + 32] if kind == "self" else v_lat[:, 0, b, 32 * h:32 * h + 32]
                                last = nc.tensor.matmul(out[row:row + 32, 0:P], v, pT[:, j * P:(j + 1) * P], start=(j % 2 == 0), stop=(j % 2 == 1))
                        last.then_inc(s["pv_done"], 1)

                    def output(kind, b):
                        pe.wait_ge(s["o_copied"], g * 3 * BLOCKS + BLOCKS * NTH[kind] + NB + b + 2)
                        out, filled = wait_free(pe, g, (kind + "_o", b))
                        for c in range(KC):
                            last = nc.tensor.matmul(out[:, 0:D], oT[:, c, b, :], w[kind + "_o"][:, c, :], start=(c == 0), stop=(c == KC - 1))
                        last.then_inc(filled, 1)

                    def attention(kind, meanwhile={}):
                        n = UNITS[kind]
                        per = BLOCK_UNITS[kind]
                        for t in range(n + SCORES_AHEAD + 3):
                            if t < n:
                                scores_of(kind, t)
                            if t in meanwhile:
                                meanwhile[t]()
                            if 0 <= t - SCORES_AHEAD < n:
                                transpose_probs(kind, t - SCORES_AHEAD)
                            if 0 <= t - SCORES_AHEAD - 1 < n:
                                weigh_values(kind, t - SCORES_AHEAD - 1)
                            done = t - SCORES_AHEAD - 2
                            if kind != "chan" and NB * per <= done < n and done % per == per - 1:
                                output(kind, done // per - NB)

                    def mlp(name):
                        for f in range(FC):
                            project((name + "_up", f), name + "_up", f, [hT[:, c, :] for c in range(KC)])
                        for i in range(2):
                            out, filled = wait_free(pe, g, (name + "_down", i))
                            for j in range(2):
                                b = 2 * i + j
                                for f in range(FC):
                                    if i == j == 0:
                                        wait_copied(pe, g, (name + "_up", f))
                                    last = nc.tensor.matmul(out[:, j * D:(j + 1) * D], upT[:, f, b * P:(b + 1) * P], w[name + "_down"][:, f, :], start=(f == 0), stop=(f == FC - 1))
                            last.then_inc(filled, 1)

                    hT_chunks = [hT[:, c, :] for c in range(KC)]
                    ctxT_chunks = [ctxT[:, c, :, :] for c in range(KC)]

                    def hT_rows(c, b):
                        return hT[:, c, b * P:(b + 1) * P]

                    def ctxT_rows(c, b):
                        return ctxT[:, c, b, :]

                    def own_attention(name):
                        project((name + "_q", 0), name + "_q", 0, hT_chunks)
                        project((name + "_k", 0), name + "_k", 0, hT_chunks)
                        attention(name, {0: lambda: project_rows((name + "_v", 0), name + "_v", 0, hT_rows),
                                         1: lambda: project_rows((name + "_v", 1), name + "_v", 1, hT_rows),
                                         2: lambda: project((name + "_q", 1), name + "_q", 1, hT_chunks),
                                         3: lambda: project((name + "_k", 1), name + "_k", 1, hT_chunks)})

                    pe.wait_ge(s["x_loaded"], g * 16 + 16)
                    for i in range(2):
                        out, filled = wait_free(pe, g, ("chan_q", i))
                        nc.tensor.matmul(out[:, :], w["wq0"][:, 0, :], x_in[:, 2 * i:2 * i + 2, :], start=True, stop=True).then_inc(filled, 1)
                    pe.wait_ge(s["ctx_loaded"], g * 16 + 16)
                    for i in range(2):
                        out, filled = wait_free(pe, g, ("chan_k", i))
                        nc.tensor.matmul(out[:, :], w["wk0"][:, 0, :], ctx_in[:, 2 * i:2 * i + 2, :], start=True, stop=True).then_inc(filled, 1)
                    for i in range(2):
                        out, filled = wait_free(pe, g, ("chan_v", i))
                        for j in range(4):
                            b, m = 2 * i + j // 2, j % 2
                            last = nc.tensor.matmul(out[:, j * P:(j + 1) * P], ctx_in[:, b, m * P:(m + 1) * P], w["wv0"][:, 0, :], start=True, stop=True)
                        last.then_inc(filled, 1)
                    for i in range(2):
                        wait_copied(pe, g, ("chan_v", i))
                    attention("chan")

                    pe.wait_ge(s["weights_loaded"], 16)
                    transposed("ln1")
                    for c in range(KC):
                        wait_copied(pe, g, ("ln1", c))
                    own_attention("self")

                    pe.wait_ge(s["ctxT_loaded"], g * 32 + 32)
                    for c in range(KC):
                        project(("cross_k", c), "cross_k", c, ctxT_chunks)
                    for i in range(2):
                        project_rows(("cross_v", i), "cross_v", i, ctxT_rows)
                    transposed("ln2")
                    for c in range(KC):
                        wait_copied(pe, g, ("ln2", c))
                    project(("cross_q", 0), "cross_q", 0, hT_chunks)
                    attention("cross", {0: lambda: project(("cross_q", 1), "cross_q", 1, hT_chunks)})

                    for c in range(KC):
                        project(("ctx_k", c), "lat_k", c, ctxT_chunks)
                    for i in range(2):
                        project_rows(("ctx_v", i), "lat_v", i, ctxT_rows)
                    for i in range(2):
                        wait_copied(pe, g, ("ctx_v", i))
                    pe.sem_inc(s["ctx_used"], 1)
                    transposed("ln3")
                    for c in range(KC):
                        wait_copied(pe, g, ("ln3", c))
                    mlp("mlp1")

                    transposed("lat")
                    for c in range(KC):
                        wait_copied(pe, g, ("lat", c))
                    own_attention("lat")
                    transposed("rms")
                    for c in range(KC):
                        wait_copied(pe, g, ("rms", c))
                    mlp("mlp2")


STEPS = 2 * G
ATT_UNITS = PAIRS * STEPS
SCALE3 = W3 ** -0.5
HCOLS = 4
NGEN = 4
NORM_STEPS3 = 2 * B + 2 + 3 * NEWTON_STEPS

HI, LO = 0, 1
PASSES = [(HI, HI), (LO, HI), (HI, LO)]


def pair_uses(last):
    uses = []
    for t in range(STEPS):
        if not (last and t >= G):
            uses.append(("q", t))
        uses.append(("k", t))
        if t < G:
            uses += [("v", t, 0), ("v", t, 1)]
        elif t > G:
            uses += [("out", t - G - 1, 0), ("out", t - G - 1, 1)]
    return uses + [("out", G - 1, 0), ("out", G - 1, 1)]


LN_USES = [("ln", g, c) for g in range(2) for c in range(KC)]
for _g in range(G):
    LN_USES.append(("q", _g))
    if _g + 2 < G:
        LN_USES += [("ln", _g + 2, c) for c in range(KC)]
SECTIONS = {"start": Banks([("k", t) for t in range(G)], NGEN),
            "ln": Banks(LN_USES, NGEN), "pair": Banks(pair_uses(False), NGEN), "last": Banks(pair_uses(True), NGEN),
            "mlp_ln": Banks([("ln", g, c) for g in range(G) for c in range(KC)], NGEN),
            "mlp": Banks([("up", f) for f in range(FC)] + [("down", i) for i in range(2)], NGEN)}


def bank_count(section, a, i, key):
    k, n = SECTIONS[section][key]
    per = {name: SECTIONS[name].per_loop[k] for name in SECTIONS}
    attention = per["ln"] + (PAIRS - 1) * per["pair"] + per["last"]
    if section == "start":
        return k, n
    if section in ("mlp_ln", "mlp"):
        n += per["start"] + 2 * attention
        return k, n if section == "mlp_ln" else i * per["mlp"] + (n + per["mlp_ln"])
    n += per["start"] + {"ln": 0, "pair": per["ln"], "last": per["ln"] + (PAIRS - 1) * per["pair"]}[section]
    return k, a * attention + i * per[section] + n


def stage_3(nc, dram, consts):
    ident, cols = consts["ident"], consts["cols"]

    with ExitStack() as ctx:
        def sb(name, shape, dt=F32):
            return ctx.enter_context(nc.sbuf_tensor(name, shape, dt))

        def sem(name):
            return ctx.enter_context(nc.semaphore(name))

        X = sb("X3", [P, B, D])
        hT = sb("hT3", [P, 2, KC, B * P], F32R)
        ctxT = sb("ctxT3", [P, 2, KC, B * P], F32R)
        qT = sb("qT3", [P, 2, B * P])
        kT = sb("kT3", [P, 2, B * P])
        v = sb("v3", [P, 2, B, P])
        oT = sb("oT3", [P, 2, 2, B * P], F32R)
        probs = sb("probs3", [P, 2, BANK])
        probsT = sb("probsT3", [P, BANK])
        rawmax = sb("rawmax3", [P, 2, NB])
        negmax = sb("negmax3", [P, 2, NB])
        sums = sb("sums3", [P, 2, NB])
        learned = sb("learned3", [P, 2, NB])
        totals = sb("totals3", [P, 2, NB])
        rsums = sb("rsums3", [P, 2, NB])
        raw_qk = sb("raw_qk3", [P, 2, 2 * KC * P])
        raw_v = sb("raw_v3", [P, KC * 2 * P])
        raw_o = sb("raw_o3", [P, 2 * D])
        w_qk = sb("w_qk3", [P, 2, 2, 2 * KC * P], F32R)
        w_v = sb("w_v3", [P, 2, KC * 2 * P], F32R)
        w_o = sb("w_o3", [P, 2, 2 * D], F32R)
        raw_vrows = sb("raw_vrows3", [P, 2, 2 * P])
        vrow = sb("vrow3", [P, 2 * P])
        hcols = sb("hcols3", [P, (2 * NH + 1) * HCOLS])
        rows = sb("rows_b", [P, len(ROWS_B), D])
        stats = sb("stats3", [P, B, 6])
        mv = sb("mv3", [P, B, 2])
        var = sb("var3", [P, B])
        guess = sb("guess3", [P, B], I32)
        rstd = sb("rstd3", [P, B])
        shift = sb("shift3", [P, B])
        newton = sb("newton3", [P, B])

        xhat = qT[:, :, :].rearrange("p h r -> p (h r)").rearrange("p (b n) -> p b n", b=B)
        raw_hT = kT[:, 1, :].rearrange("p (i c r) -> p i c r", i=2, c=KC)
        raw_ctxT = v[:, :, :, :].rearrange("p h b k -> p h (b k)")
        raw_up = v[:, 0, :, :].rearrange("p b k -> p (b k)")
        raw_down = v[:, 1, :, :].rearrange("p b k -> p (b k)")
        w_up = ctxT[:, :, 0, :].rearrange("p s (c n) -> p s c n", c=KC)
        w_down = ctxT[:, :, 1, :].rearrange("p s (f n) -> p s f n", f=FC)
        gelu = qT[:, :, :].rearrange("p h r -> p (h r)").rearrange("p (f r) -> p f r", f=FC)
        upT = oT[:, :, :, :].rearrange("p s h r -> p s (h r)").rearrange("p s (f r) -> p s f r", f=FC)

        def bank(name):
            return ctx.enter_context(nc.psum_tensor(name, [P, BANK], F32))

        scores = [bank(f"scores3_{i}") for i in range(2)]
        pT_psum = bank("pT_psum3")
        o_psum = bank("o_psum3")
        general = [bank(f"general3_{i}") for i in range(NGEN)]

        s = {n: sem(n + "3") for n in (
            "raw_qk0_loaded", "raw_qk1_loaded", "raw_v_loaded", "raw_o_loaded", "raw_up_loaded", "raw_down_loaded",
            "vectors_loaded", "stored",
            "hi_done", "vrow_ready", "qk0_ready", "qk1_ready", "wv_ready", "wo_ready", "w_up_ready", "w_down_hi", "w_down_ready",
            "ctxT_hi", "ctxT_ready", "xb_ready", "norm_step", "norm_ready", "xhat_dve", "xhat_act",
            "hT_hi", "hT_ready",
            "scores_ready", "max_step", "max_ready", "exp_done", "rsum_step", "rsum_ready", "probs_ready", "pT_ready", "pT_copied",
            "o_ready", "o_hi", "o_lo", "upT_hi", "upT_ready", "wait_passed")}
        x_loaded = [sem(f"x_loaded3_{g}") for g in range(G)]
        ctxT_loaded = [sem(f"ctxT_loaded3_{g}") for g in range(G)]
        full = [sem(f"general_full3_{i}") for i in range(NGEN)]
        free = [sem(f"general_free3_{i}") for i in range(NGEN)]

        def wait_full(eng, *at):
            k, n = bank_count(*at)
            eng.wait_ge(full[k], n + 2)
            return general[k], free[k]

        def wait_full_apart(eng, *at):
            k, n = bank_count(*at)
            eng.wait_ge(full[k], n + 2)
            eng.sem_inc(s["wait_passed"], 1)
            return general[k], free[k]

        def wait_free(eng, *at):
            k, n = bank_count(*at)
            eng.wait_ge(free[k], n + 1)
            return general[k], full[k]

        def wait_copied(eng, *at):
            k, n = bank_count(*at)
            eng.wait_ge(free[k], n + 2)

        def pair_section(last):
            return "last" if last else "pair"

        def quarter(g):
            return slice(g * R, (g + 1) * R)

        def qk_parts(head):
            return lambda part: w_qk[:, head, part, :]

        def v_parts(part):
            return w_v[:, part, :]

        def o_parts(part):
            return w_o[:, part, :]

        with nc.Block() as block:

            @block.sync
            def _(sp):
                def load_qk(pair, head):
                    sp.dma_start(raw_qk[:, head, :], dram["w_qk"][bass.ds(pair, 1), :, head, :].rearrange("a p n -> p (a n)")).then_inc(s[f"raw_qk{head}_loaded"], 16)

                def load_v(pair):
                    sp.dma_start(raw_v[:, :], dram["w_v"][bass.ds(pair, 1), :, :].rearrange("a p n -> p (a n)")).then_inc(s["raw_v_loaded"], 16)
                    sp.dma_start(raw_vrows[:, :, :].rearrange("p j n -> p (j n)"), dram["vrows"][bass.ds(pair, 1), :].rearrange("a n -> (a n)").partition_broadcast(P)).then_inc(s["raw_v_loaded"], 16)

                def load_o(pair):
                    sp.dma_start(raw_o[:, :], dram["w_o"][bass.ds(pair, 1), :, :].rearrange("a p n -> p (a n)")).then_inc(s["raw_o_loaded"], 16)

                load_qk(0, 0)
                for g in range(G):
                    sp.dma_start(X[:, NB * g:NB * g + NB, :], dram["mid"][:, NB * g:NB * g + NB, :]).then_inc(x_loaded[g], 16)
                load_qk(0, 1)
                load_v(0)
                load_o(0)

                def next_weights(pair, following, more):
                    sp.wait_ge(s["qk0_ready"], pair + 2)
                    load_qk(following, 0)
                    sp.wait_ge(s["wv_ready"], pair + 2)
                    sp.wait_ge(s["vrow_ready"], pair + 2)
                    load_v(following)
                    sp.wait_ge(s["qk1_ready"], pair + 2)
                    load_qk(following, 1)
                    if more:
                        sp.wait_ge(s["wo_ready"], pair + 2)
                        load_o(following)

                with sp.Fori(0, 2 * PAIRS - 1) as i:
                    next_weights(i, i + 1, True)
                next_weights(2 * PAIRS - 1, 0, False)
                sp.wait_ge(s["o_ready"], 2 * ATT_UNITS - STEPS + G + 1)
                sp.dma_start(raw_up, dram["w_up"]).then_inc(s["raw_up_loaded"], 16)
                sp.wait_ge(s["o_ready"], 2 * ATT_UNITS + 1)
                sp.dma_start(raw_down, dram["w_down"]).then_inc(s["raw_down_loaded"], 16)

            @block.gpsimd
            def _(pool):
                seed(pool, [s["vrow_ready"], s["qk0_ready"], s["qk1_ready"], s["wv_ready"], s["wo_ready"],
                            s["xb_ready"], s["probs_ready"], s["hT_ready"], s["upT_ready"]])

                def split_lo(parts, raw, his, ready):
                    pool.wait_ge(s["hi_done"], his + 1)
                    nc.gpsimd.tensor_tensor(parts(LO), raw, parts(HI), ALU.subtract).then_inc(s[ready], 1)

                def value_rows(loads):
                    pool.wait_ge(s["raw_v_loaded"], loads)
                    nc.gpsimd.tensor_tensor(vrow[:, :], raw_vrows[:, 0, :], raw_vrows[:, 1, :], ALU.subtract).then_inc(s["vrow_ready"], 1)

                split_lo(qk_parts(0), raw_qk[:, 0, :], 1, "qk0_ready")
                value_rows(32)
                split_lo(v_parts, raw_v[:, :], 2, "wv_ready")
                split_lo(qk_parts(1), raw_qk[:, 1, :], 3, "qk1_ready")

                def split_h(a, g):
                    pool.wait_ge(s["hT_hi"], a * G + g + 2)
                    nc.gpsimd.tensor_tensor(hT[:, LO, :, quarter(g)], raw_hT[:, g % 2, :, :], hT[:, HI, :, quarter(g)], ALU.subtract).then_inc(s["hT_ready"], 1)

                def pair(a, i, last):
                    pair_index = a * PAIRS + i
                    his = pair_index * 4 + 3
                    for t in range(STEPS):
                        n = a * ATT_UNITS + i * STEPS + t
                        pr = probs[:, t % 2, :].rearrange("p (b k) -> p b k", b=NB)
                        pool.wait_ge(s["rsum_ready"], n + 2)
                        nc.gpsimd.tensor_tensor(pr, pr, rsums[:, t % 2, :].unsqueeze(2).broadcast_to([P, NB, P]), ALU.mult).then_inc(s["probs_ready"], 1)
                        if t == 0:
                            split_lo(qk_parts(0), raw_qk[:, 0, :], his + 1, "qk0_ready")
                        elif t == 1:
                            split_lo(o_parts, raw_o[:, :], his + 2, "wo_ready")
                        elif t == G:
                            value_rows(pair_index * 32 + 64)
                            split_lo(v_parts, raw_v[:, :], his + 3, "wv_ready")
                        elif t == G + 1:
                            split_lo(qk_parts(1), raw_qk[:, 1, :], his + 4, "qk1_ready")
                        if last and t < G:
                            for j in range(2):
                                wait_copied(pool, "pair", a, PAIRS - 2, ("out", t, j))
                            pool.sem_inc(s["wait_passed"], 1)
                            x = X[:, NB * t:NB * t + NB, :]
                            nc.gpsimd.tensor_tensor(x, x, rows[:, bass.ds(a, 1), :].broadcast_to([P, NB, D]), ALU.add).then_inc(s["xb_ready"], 1)

                with pool.Fori(0, 2) as a:
                    for g in range(G):
                        split_h(a, g)
                    with pool.Fori(0, PAIRS - 1) as i:
                        pair(a, i, False)
                    pair(a, PAIRS - 1, True)
                pool.wait_ge(s["hi_done"], 2 * PAIRS * 4 + 5)
                nc.gpsimd.tensor_tensor(w_up[:, LO, :, :].rearrange("p c n -> p (c n)"), raw_up, w_up[:, HI, :, :].rearrange("p c n -> p (c n)"), ALU.subtract).then_inc(s["w_up_ready"], 1)
                for g in range(G):
                    split_h(2, g)
                with pool.Fori(0, G) as g:
                    for f in range(FC):
                        pool.wait_ge(s["upT_hi"], g * FC + f + 2)
                        nc.gpsimd.tensor_tensor(upT[:, LO, f, :], gelu[:, f, :], upT[:, HI, f, :], ALU.subtract).then_inc(s["upT_ready"], 1)
                        if f == 0:
                            x = X[:, bass.ds(g * NB, NB), :]
                            nc.gpsimd.tensor_tensor(x, x, rows[:, 2:3, :].broadcast_to([P, NB, D]), ALU.add).then_inc(s["xb_ready"], 1)
                    for j in range(2):
                        wait_copied(pool, "mlp", 0, g, ("down", j))
                        x = bass.ds(g * NB + 2 * j, 2)
                        pool.dma_start(dram["out"][x, :, :].rearrange("b p n -> p b n"), X[:, x, :]).then_inc(s["stored"], 16)
                pool.wait_ge(s["stored"], 2 * 16 * G)

            @block.scalar
            def _(act):
                seed(act, [s["exp_done"], s["pT_copied"], s["o_hi"], s["hi_done"], s["xhat_act"], s["hT_hi"]])
                for g in range(G):
                    act.dma_start(raw_ctxT[:, :, quarter(g)], dram["ctxT"][:, :, NB * g:NB * g + NB, :].rearrange("p c b k -> p c (b k)")).then_inc(ctxT_loaded[g], 16)
                act.dma_start(hcols[:, :], dram["hcols"]).then_inc(s["vectors_loaded"], 16)
                act.dma_start(rows[:, :, :], dram["rows_b"].partition_broadcast(P)).then_inc(s["vectors_loaded"], 16)

                def split_hi(name, loads, parts, raw):
                    act.wait_ge(s[name], loads)
                    nc.scalar.copy(parts(HI), raw).then_inc(s["hi_done"], 1)

                split_hi("raw_qk0_loaded", 16, qk_parts(0), raw_qk[:, 0, :])
                for g in range(G):
                    act.wait_ge(ctxT_loaded[g], 16)
                    nc.scalar.copy(ctxT[:, HI, :, quarter(g)], raw_ctxT[:, :, quarter(g)]).then_inc(s["ctxT_hi"], 1)
                split_hi("raw_v_loaded", 32, v_parts, raw_v[:, :])
                split_hi("raw_qk1_loaded", 16, qk_parts(1), raw_qk[:, 1, :])
                act.wait_ge(s["vectors_loaded"], 32)

                def xhat_rows(a, g):
                    act.wait_ge(s["norm_ready"], a * 2 + 3)
                    act.sem_inc(s["wait_passed"], 1)
                    for b in (NB * g + 1, NB * g + 3):
                        nc.scalar.activation(xhat[:, b, :], X[:, b, :], ACT.Identity, scale=rstd[:, b:b + 1], bias=shift[:, b:b + 1]).then_inc(s["xhat_act"], 1)

                def norm_copies(section, a, g, at):
                    if g >= 2:
                        act.wait_ge(s["hT_ready"], a * G + g)
                    src, freed = wait_full_apart(act, section, a, 0, ("ln", g, 1))
                    nc.scalar.activation(raw_hT[:, g % 2, 1, :], src[:, :], ACT.Identity, scale=cols[:, bass.ds(at + 1, 1)], bias=cols[:, bass.ds(at + 3, 1)]).then_inc(freed, 1)
                    for c in range(KC):
                        wait_copied(act, section, a, 0, ("ln", g, c))
                    nc.scalar.copy(hT[:, HI, :, quarter(g)], raw_hT[:, g % 2, :, :]).then_inc(s["hT_hi"], 1)

                def norm(section, a, at):
                    xhat_rows(a, 0)
                    xhat_rows(a, 1)
                    for g in range(G):
                        norm_copies(section, a, g, at)
                        if g + 2 < G:
                            xhat_rows(a, g + 2)
                        if section == "ln" and g > 0:
                            copy_q(section, a, 0, g - 1, 0, 0)

                def copy_q(section, a, i, t, head, pair):
                    src, freed = wait_full_apart(act, section, a, i, ("q", t))
                    at = a * (NH * HCOLS) + pair * (2 * HCOLS) + head * HCOLS
                    nc.scalar.activation(qT[:, head, quarter(t % G)], src[:, :], ACT.Identity, bias=hcols[:, bass.ds(at, 1)]).then_inc(freed, 1)

                def exps(n, t):
                    act.wait_ge(s["max_ready"], n + 2)
                    act.wait_ge(s["pT_ready"], n if t > 0 else n + 1)
                    for b in range(NB):
                        nc.scalar.activation(probs[:, t % 2, b * P:(b + 1) * P], scores[t % 2][:, b * P:(b + 1) * P], ACT.Exp,
                                             bias=negmax[:, t % 2, b:b + 1], scale=SCALE3, accum_out=sums[:, t % 2, b:b + 1])
                    nc.scalar.activation(learned[:, t % 2, :], negmax[:, t % 2, :], ACT.Exp).then_inc(s["exp_done"], 1)

                def copy_pT(n):
                    act.wait_ge(s["pT_ready"], n + 2)
                    act.wait_ge(s["o_ready"], n + 1)
                    nc.scalar.copy(probsT[:, :], pT_psum[:, :]).then_inc(s["pT_copied"], 1)

                def copy_o(a, i, n, t):
                    head = t // G
                    at = a * (NH * HCOLS) + i * (2 * HCOLS) + head * HCOLS + 3
                    act.wait_ge(s["o_ready"], n + 2)
                    act.sem_inc(s["wait_passed"], 1)
                    nc.scalar.activation(oT[:, HI, head, quarter(t % G)], o_psum[:, :], ACT.Identity, bias=hcols[:, bass.ds(at, 1)]).then_inc(s["o_hi"], 1)

                def pair(a, i, last):
                    section, loop = pair_section(last), 0 if last else i
                    for t in range(STEPS):
                        n = a * ATT_UNITS + i * STEPS + t
                        if t > 0:
                            copy_o(a, i, n - 1, t - 1)
                        exps(n, t)
                        pair_index = a * PAIRS + i
                        if t == 0:
                            split_hi("raw_qk0_loaded", pair_index * 16 + 32, qk_parts(0), raw_qk[:, 0, :])
                        elif t == 1:
                            split_hi("raw_o_loaded", pair_index * 16 + 16, o_parts, raw_o[:, :])
                        elif t == G:
                            split_hi("raw_v_loaded", pair_index * 32 + 64, v_parts, raw_v[:, :])
                        elif t == G + 1:
                            split_hi("raw_qk1_loaded", pair_index * 16 + 32, qk_parts(1), raw_qk[:, 1, :])
                        if t < G:
                            copy_q(section, a, loop, t, 1, i)
                        elif not last:
                            copy_q(section, a, loop, t, 0, i + 1)
                        copy_pT(n)
                    copy_o(a, i, n, STEPS - 1)

                with act.Fori(0, 2) as a:
                    norm("ln", a, a * 4 + COLS["lnA_s"][0])
                    copy_q("ln", a, 0, G - 1, 0, 0)
                    with act.Fori(0, PAIRS - 1) as i:
                        pair(a, i, False)
                    pair(a, PAIRS - 1, True)
                act.wait_ge(s["raw_up_loaded"], 16)
                wait_full(act, "last", 1, 0, ("k", STEPS - 1))
                nc.scalar.copy(w_up[:, HI, :, :].rearrange("p c n -> p (c n)"), raw_up).then_inc(s["hi_done"], 1)
                norm("mlp_ln", 2, COLS["lnM_s"][0])
                with act.Fori(0, G) as g:
                    for f in range(FC):
                        src, freed = wait_full(act, "mlp", 0, g, ("up", f))
                        at = COLS["mlp3_b"][0] + f
                        nc.scalar.activation(gelu[:, f, :], src[:, :], ACT.Gelu, bias=cols[:, at:at + 1]).then_inc(freed, 1)

            @block.vector
            def _(dve):
                seed(dve, [s["norm_step"], s["norm_ready"], s["xhat_dve"], s["max_step"], s["max_ready"],
                           s["rsum_step"], s["rsum_ready"], s["o_lo"], s["upT_hi"]] + free)

                def row_stats(b):
                    nc.vector.bn_stats(stats[:, b, :], X[:, b, :]).then_inc(s["norm_step"], 1)

                def copy_k(section, a, i, t, head, pair):
                    src, freed = wait_full(dve, section, a, i, ("k", t))
                    at = a * (NH * HCOLS) + pair * (2 * HCOLS) + head * HCOLS
                    nc.vector.tensor_scalar(kT[:, head, quarter(t % G)], src[:, :], hcols[:, bass.ds(at + 1, 1)], hcols[:, bass.ds(at + 2, 1)],
                                            ALU.add, ALU.subtract).then_inc(freed, 1)

                def copy_v(section, a, i, t):
                    for j in range(2):
                        src, freed = wait_full(dve, section, a, i, ("v", t, j))
                        b = t * NB + 2 * j
                        nc.vector.tensor_tensor(v[:, :, b:b + 2, :].rearrange("p h b k -> p b h k"),
                                                src[:, :].rearrange("p (b h k) -> p b h k", b=2, h=2),
                                                vrow[:, :].rearrange("p (h k) -> p h k", h=2).unsqueeze(1).broadcast_to([P, 2, 2, P]), ALU.add).then_inc(freed, 1)

                def front(n, t):
                    dve.wait_ge(s["scores_ready"], n + 2)
                    nc.vector.tensor_reduce(rawmax[:, t % 2, :], scores[t % 2][:, :].rearrange("p (b k) -> p b k", b=NB),
                                            axis=AX.X, op=ALU.max, negate=True).then_inc(s["max_step"], 1)
                    dve.wait_ge(s["max_step"], n + 2)
                    nc.vector.tensor_scalar(negmax[:, t % 2, :], rawmax[:, t % 2, :], 0.0, SCALE3, ALU.min, ALU.mult).then_inc(s["max_ready"], 1)

                def rsum(n, t):
                    dve.wait_ge(s["exp_done"], n + 2)
                    dve.wait_ge(s["probs_ready"], n if t > 0 else n + 1)
                    nc.vector.tensor_tensor(totals[:, t % 2, :], sums[:, t % 2, :], learned[:, t % 2, :], ALU.add).then_inc(s["rsum_step"], 1)
                    dve.wait_ge(s["rsum_step"], n + 2)
                    nc.vector.reciprocal(rsums[:, t % 2, :], totals[:, t % 2, :]).then_inc(s["rsum_ready"], 1)

                def o_low(a, i, n, t):
                    head = t // G
                    at = a * (NH * HCOLS) + i * (2 * HCOLS) + head * HCOLS + 3
                    dve.wait_ge(s["o_hi"], n + 2)
                    nc.vector.scalar_tensor_tensor(out=oT[:, LO, head, quarter(t % G)], in0=o_psum[:, :], scalar=hcols[:, bass.ds(at, 1)],
                                                   in1=oT[:, HI, head, quarter(t % G)], op0=ALU.add, op1=ALU.subtract).then_inc(s["o_lo"], 1)

                def add_out(section, a, i, q):
                    for j in range(2):
                        src, freed = wait_full(dve, section, a, i, ("out", q, j))
                        x = X[:, NB * q + 2 * j:NB * q + 2 * j + 2, :]
                        nc.vector.tensor_tensor(x, src[:, :].rearrange("p (b n) -> p b n", b=2), x, ALU.add).then_inc(freed, 1)
                    if section == "last":
                        for j in range(2):
                            wait_copied(dve, section, a, i, ("out", q, j))
                        for b in range(NB * q, NB * q + NB):
                            row_stats(b)

                def pair(a, i, last):
                    section, loop = pair_section(last), 0 if last else i
                    for t in range(STEPS):
                        n = a * ATT_UNITS + i * STEPS + t
                        if t > 0:
                            front(n, t)
                            o_low(a, i, n - 1, t - 1)
                        rsum(n, t)
                        if t < G:
                            copy_k(section, a, loop, t, 1, i)
                            if t == 0:
                                dve.wait_ge(s["vrow_ready"], a * PAIRS + i + 2)
                            copy_v(section, a, loop, t)
                        else:
                            if not last:
                                copy_k(section, a, loop, t, 0, i + 1)
                            else:
                                copy_k(section, a, loop, t, 0, PAIRS)
                        if last and t == G:
                            dve.wait_ge(s["xb_ready"], a * G + G + 1)
                        if t > G:
                            add_out(section, a, loop, t - G - 1)
                    o_low(a, i, n, STEPS - 1)
                    if not last:
                        front(n + 1, 0)
                    add_out(section, a, loop, G - 1)

                def norm(section, a, at):
                    count = [B]
                    base = a * NORM_STEPS3 + 1

                    def step(ins):
                        count[0] += 1
                        ins.then_inc(s["norm_step"], 1)

                    dve.wait_ge(s["norm_step"], base + count[0])
                    dve.sem_inc(s["wait_passed"], 1)
                    for b in range(B):
                        step(nc.vector.bn_aggr(mv[:, b, :], stats[:, b, :]))
                    dve.wait_ge(s["norm_step"], base + count[0])
                    step(nc.vector.tensor_scalar(var[:, :], mv[:, :, 1], 1e-5, None, ALU.add))
                    dve.wait_ge(s["norm_step"], base + count[0])
                    step(nc.vector.tensor_single_scalar(guess[:, :], var[:, :].bitcast(I32), 1, ALU.logical_shift_right))
                    dve.wait_ge(s["norm_step"], base + count[0])
                    step(nc.vector.tensor_scalar(guess[:, :], guess[:, :], -1.0, RSQRT_MAGIC, ALU.mult, ALU.add))
                    y = guess[:, :].bitcast(F32)
                    for i in range(NEWTON_STEPS):
                        dve.wait_ge(s["norm_step"], base + count[0])
                        step(nc.vector.scalar_tensor_tensor(out=newton[:, :], in0=y, scalar=-0.5, in1=y, op0=ALU.mult, op1=ALU.mult))
                        dve.wait_ge(s["norm_step"], base + count[0])
                        step(nc.vector.tensor_tensor(newton[:, :], newton[:, :], var[:, :], ALU.mult))
                        dve.wait_ge(s["norm_step"], base + count[0])
                        ins = nc.vector.scalar_tensor_tensor(out=rstd[:, :], in0=newton[:, :], scalar=1.5, in1=y, op0=ALU.add, op1=ALU.mult)
                        if i == NEWTON_STEPS - 1:
                            ins.then_inc(s["norm_ready"], 1)
                        else:
                            step(ins)
                        y = rstd[:, :]
                    dve.wait_ge(s["norm_ready"], a * 2 + 2)
                    nc.vector.scalar_tensor_tensor(out=shift[:, :], in0=mv[:, :, 0], scalar=-1.0, in1=rstd[:, :], op0=ALU.mult, op1=ALU.mult).then_inc(s["norm_ready"], 1)
                    assert count[0] == NORM_STEPS3
                    xhat_rows(0)
                    xhat_rows(1)
                    for g in range(G):
                        if g >= 2:
                            dve.wait_ge(s["hT_ready"], a * G + g)
                        src, freed = wait_full(dve, section, a, 0, ("ln", g, 0))
                        nc.vector.tensor_scalar(raw_hT[:, g % 2, 0, :], src[:, :], cols[:, bass.ds(at, 1)], cols[:, bass.ds(at + 2, 1)], ALU.mult, ALU.add).then_inc(freed, 1)
                        if g + 2 < G:
                            xhat_rows(g + 2)

                def xhat_rows(g):
                    for b in (NB * g, NB * g + 2):
                        nc.vector.tensor_scalar(xhat[:, b, :], X[:, b, :], mv[:, b, 0:1], rstd[:, b:b + 1], ALU.subtract, ALU.mult).then_inc(s["xhat_dve"], 1)

                for g in range(G):
                    dve.wait_ge(x_loaded[g], 16)
                    for b in range(NB * g, NB * g + NB):
                        row_stats(b)
                for g in range(G):
                    dve.wait_ge(s["ctxT_hi"], g + 1)
                    nc.vector.tensor_tensor(ctxT[:, LO, :, quarter(g)], raw_ctxT[:, :, quarter(g)], ctxT[:, HI, :, quarter(g)], ALU.subtract).then_inc(s["ctxT_ready"], 1)
                dve.wait_ge(s["vectors_loaded"], 32)
                for t in range(G):
                    copy_k("start", 0, 0, t, 0, 0)
                dve.wait_ge(s["ctxT_ready"], G)
                with dve.Fori(0, 2) as a:
                    norm("ln", a, a * 4 + COLS["lnA_s"][0])
                    dve.wait_ge(s["hT_ready"], a * G + G + 1)
                    front(a * ATT_UNITS, 0)
                    with dve.Fori(0, PAIRS - 1) as i:
                        pair(a, i, False)
                    pair(a, PAIRS - 1, True)
                norm("mlp_ln", 2, COLS["lnM_s"][0])
                down = [w_down[:, part, :, :].rearrange("p f n -> p (f n)") for part in (HI, LO)]
                dve.wait_ge(s["raw_down_loaded"], 16)
                nc.vector.tensor_copy(down[HI], raw_down).then_inc(s["w_down_hi"], 1)
                dve.wait_ge(s["w_down_hi"], 1)
                nc.vector.tensor_tensor(down[LO], raw_down, down[HI], ALU.subtract).then_inc(s["w_down_ready"], 1)
                with dve.Fori(0, G) as g:
                    for f in range(FC):
                        wait_copied(dve, "mlp", 0, g, ("up", f))
                        nc.vector.tensor_copy(upT[:, HI, f, :], gelu[:, f, :]).then_inc(s["upT_hi"], 1)
                    dve.wait_ge(s["xb_ready"], 2 * G + g + 2)
                    for j in range(2):
                        src, freed = wait_full(dve, "mlp", 0, g, ("down", j))
                        x = X[:, bass.ds(g * NB + 2 * j, 2), :]
                        nc.vector.tensor_tensor(x, src[:, :].rearrange("p (b n) -> p b n", b=2), x, ALU.add).then_inc(freed, 1)

            @block.tensor
            def _(pe):
                seed(pe, [s["scores_ready"], s["pT_ready"], s["o_ready"]] + full)

                def split_matmul(out, stationary, moving):
                    terms = [(a, b, c) for c in range(KC) for a, b in PASSES]
                    for i, (a, b, c) in enumerate(terms):
                        last = nc.tensor.matmul(out, stationary(a, c), moving(b, c), start=(i == 0), stop=(i == len(terms) - 1))
                    return last

                def transposed(section, a, g):
                    for c in range(KC):
                        out, filled = wait_free(pe, section, a, 0, ("ln", g, c))
                        if c == 0:
                            pe.wait_ge(s["xhat_dve"], a * (B // 2) + 2 * g + 3)
                            pe.wait_ge(s["xhat_act"], a * (B // 2) + 2 * g + 3)
                        for b in range(NB):
                            last = nc.tensor.transpose(out[:, b * P:(b + 1) * P], xhat[:, g * NB + b, c * P:(c + 1) * P], ident[:, :])
                        last.then_inc(filled, 1)

                def queries(section, a, i, t, head):
                    out, filled = wait_free(pe, section, a, i, ("q", t))
                    split_matmul(out[:, :], lambda part, c: w_qk[:, head, part, c * P:(c + 1) * P],
                                 lambda part, c: hT[:, part, c, quarter(t % G)]).then_inc(filled, 1)

                def keys(section, a, i, t, head):
                    out, filled = wait_free(pe, section, a, i, ("k", t))
                    split_matmul(out[:, :], lambda part, c: w_qk[:, head, part, (KC + c) * P:(KC + c + 1) * P],
                                 lambda part, c: ctxT[:, part, c, quarter(t % G)]).then_inc(filled, 1)

                def values(section, a, i, t):
                    for half in range(2):
                        out, filled = wait_free(pe, section, a, i, ("v", t, half))
                        for j in range(2):
                            b = t * NB + 2 * half + j
                            last = split_matmul(out[:, j * 2 * P:(j + 1) * 2 * P], lambda part, c: ctxT[:, part, c, b * P:(b + 1) * P],
                                                lambda part, c: w_v[:, part, c * 2 * P:(c + 1) * 2 * P])
                        last.then_inc(filled, 1)

                def score(t):
                    head = t // G
                    for j in range(NB):
                        b = (t % G) * NB + j
                        last = nc.tensor.matmul(scores[t % 2][:, j * P:(j + 1) * P], qT[:, head, b * P:(b + 1) * P], kT[:, head, b * P:(b + 1) * P], start=True, stop=True)
                    last.then_inc(s["scores_ready"], 1)

                def weigh_values(n, t, a, section, loop):
                    head = t // G
                    pe.wait_ge(s["pT_copied"], n + 2)
                    if head == 0:
                        for half in range(2):
                            wait_copied(pe, section, a, loop, ("v", t, half))
                    pe.wait_ge(s["o_lo"], n + 1)
                    for j in range(NB):
                        last = nc.tensor.matmul(o_psum[:, j * P:(j + 1) * P], v[:, head, (t % G) * NB + j, :], probsT[:, j * P:(j + 1) * P], start=True, stop=True)
                    last.then_inc(s["o_ready"], 1)

                def output(section, a, loop, q, half):
                    out, filled = wait_free(pe, section, a, loop, ("out", q, half))
                    for j in range(2):
                        b = q * NB + 2 * half + j
                        last = split_matmul(out[:, j * D:(j + 1) * D], lambda part, head: oT[:, part, head, b * P:(b + 1) * P],
                                            lambda part, head: w_o[:, part, head * D:(head + 1) * D])
                    last.then_inc(filled, 1)

                def pair(a, i, last_pair):
                    section, loop = pair_section(last_pair), 0 if last_pair else i
                    weights = a * PAIRS + i + 2
                    for t in range(STEPS):
                        n = a * ATT_UNITS + i * STEPS + t
                        if t > 0:
                            if t >= G:
                                for name in ("q", "k"):
                                    wait_copied(pe, section, a, loop, (name, t - G))
                            pe.wait_ge(s["exp_done"], n)
                            score(t)
                            weigh_values(n - 1, t - 1, a, section, loop)
                        if t == 0:
                            pe.wait_ge(s["qk1_ready"], weights)
                        elif t == G:
                            pe.wait_ge(s["qk0_ready"], weights + 1)
                        if not (last_pair and t >= G):
                            queries(section, a, loop, t, 1 - t // G)
                        keys(section, a, loop, t, 1 - t // G)
                        if t == 0:
                            pe.wait_ge(s["wv_ready"], weights)
                        if t < G:
                            values(section, a, loop, t)
                        elif t > G:
                            if t == G + 1:
                                pe.wait_ge(s["wo_ready"], weights)
                            pe.wait_ge(s["o_lo"], n + 1)
                            output(section, a, loop, t - G - 1, 0)
                            if t < STEPS - 1:
                                output(section, a, loop, t - G - 1, 1)
                        pe.wait_ge(s["probs_ready"], n + 2)
                        pe.wait_ge(s["pT_copied"], n + 1)
                        for j in range(NB):
                            last = nc.tensor.transpose(pT_psum[:, j * P:(j + 1) * P], probs[:, t % 2, j * P:(j + 1) * P], ident[:, :])
                        last.then_inc(s["pT_ready"], 1)
                    output(section, a, loop, G - 2, 1)
                    weigh_values(n, t, a, section, loop)
                    if not last_pair:
                        for t in range(G, STEPS):
                            for name in ("q", "k"):
                                wait_copied(pe, section, a, loop, (name, t))
                        pe.wait_ge(s["exp_done"], n + 1)
                        score(0)
                    pe.wait_ge(s["o_lo"], n + 2)
                    for half in range(2):
                        output(section, a, loop, G - 1, half)

                pe.wait_ge(s["qk0_ready"], 2)
                for t in range(G):
                    pe.wait_ge(s["ctxT_ready"], t + 1)
                    keys("start", 0, 0, t, 0)
                with pe.Fori(0, 2) as a:
                    for g in range(2):
                        transposed("ln", a, g)
                    for g in range(G):
                        pe.wait_ge(s["hT_ready"], a * G + g + 2)
                        queries("ln", a, 0, g, 0)
                        if g + 2 < G:
                            transposed("ln", a, g + 2)
                    for g in range(G):
                        wait_copied(pe, "ln", a, 0, ("q", g))
                    pe.wait_ge(s["exp_done"], a * ATT_UNITS + 1)
                    score(0)
                    with pe.Fori(0, PAIRS - 1) as i:
                        pair(a, i, False)
                    pair(a, PAIRS - 1, True)
                for g in range(G):
                    transposed("mlp_ln", 2, g)
                pe.wait_ge(s["w_up_ready"], 1)
                pe.wait_ge(s["hT_ready"], 3 * G + 1)
                with pe.Fori(0, G) as g:
                    for f in range(FC):
                        out, filled = wait_free(pe, "mlp", 0, g, ("up", f))
                        split_matmul(out[:, :], lambda part, c: w_up[:, part, c, f * P:(f + 1) * P],
                                     lambda part, c: hT[:, part, c, bass.ds(g * R, R)]).then_inc(filled, 1)
                    pe.wait_ge(s["w_down_ready"], 1)
                    for i in range(2):
                        out, filled = wait_free(pe, "mlp", 0, g, ("down", i))
                        for j in range(2):
                            b = 2 * i + j
                            for f in range(FC):
                                if b == 0:
                                    pe.wait_ge(s["upT_ready"], g * FC + f + 2)
                                for k, (up, down) in enumerate(PASSES):
                                    last = nc.tensor.matmul(out[:, j * D:(j + 1) * D], upT[:, up, f, b * P:(b + 1) * P], w_down[:, down, f, :],
                                                            start=(f == 0 and k == 0), stop=(f == FC - 1 and k == len(PASSES) - 1))
                        last.then_inc(filled, 1)


def chunked(w):
    k, n = w.shape
    return w.reshape(k // P, P, n).transpose(1, 0, 2).reshape(P, -1)


def columns(v):
    return v.reshape(-1, P).T


def by_pair(*matrices):
    stacked = np.stack([m.reshape(KC, P, PAIRS, 2, W3) for m in matrices])
    return stacked.transpose(3, 2, 4, 0, 1, 5).reshape(PAIRS, P, 2, -1)


def laid_out(x, ctx_2048, mask_1x1xSxS2_fc1, mask_Bx1xSxS2_ff1, mask_BxS2_ik0, **w):
    def padded(a, axis):
        widths = [(0, 0)] * a.ndim
        widths[axis] = (0, P - a.shape[axis])
        return np.pad(a, widths)

    l0, l1, l2, l3 = ("L0_xattn_", "L1_xattn_", "L2_xattn_", "L3_xattn_")
    qkv, b_qkv = w[l1 + "w_qkv"], w[l1 + "b_qkv"]
    kv, b_kv = w[l1 + "w_kv"], w[l1 + "b_kv"]
    lat_kv, b_lat_kv = w[l2 + "kv_w"], w[l2 + "kv_b"]
    weights = {
        "wq0": padded(w[l0 + "Wq"].T, 1), "wk0": padded(w[l0 + "Wk"].T, 1), "wv0": w[l0 + "Wv"].T,
        "self_q": qkv[:, 0:D], "self_k": qkv[:, D:2 * D], "self_v": qkv[:, 2 * D:3 * D], "self_o": w[l1 + "w_ao"],
        "cross_k": kv[:, 0:D], "cross_v": kv[:, D:2 * D], "cross_q": w[l1 + "w_q"], "cross_o": w[l1 + "w_co"],
        "mlp1_up": w[l1 + "w1"], "mlp1_down": w[l1 + "w2"],
        "lat_q": w[l2 + "q_w"], "lat_k": lat_kv[:, 0::2], "lat_v": lat_kv[:, 1::2], "lat_o": w[l2 + "out_w"],
        "mlp2_up": w[l2 + "mlp_w1"], "mlp2_down": w[l2 + "mlp_w2"],
    }
    vectors = {
        "bq0": padded(w[l0 + "bq"], 0), "bk0": padded(w[l0 + "bk"], 0), "bv0": w[l0 + "bv"],
        "ln1_s": w[l1 + "ln1_s"], "ln1_b": w[l1 + "ln1_b"], "ln2_s": w[l1 + "ln2_s"], "ln2_b": w[l1 + "ln2_b"],
        "ln3_s": w[l1 + "ln3_s"], "ln3_b": w[l1 + "ln3_b"],
        "self_bq": b_qkv[0:D], "self_bk": b_qkv[D:2 * D], "self_bv": b_qkv[2 * D:3 * D],
        "cross_bq": w[l1 + "b_q"], "cross_bk": b_kv[0:D], "cross_bv": b_kv[D:2 * D], "mlp1_b": w[l1 + "b1"],
        "lat_bq": w[l2 + "q_b"], "lat_bk": b_lat_kv[0::2], "lat_bv": b_lat_kv[1::2], "rms_w": w[l2 + "postnorm_w"],
        "mlp2_b": w[l2 + "mlp_b1"],
        "lnA_s": w[l3 + "ln1_scale"], "lnA_b": w[l3 + "ln1_offset"], "lnB_s": w[l3 + "ln2_scale"], "lnB_b": w[l3 + "ln2_offset"],
        "lnM_s": w[l3 + "ln_mlp_scale"], "lnM_b": w[l3 + "ln_mlp_offset"], "mlp3_b": w[l3 + "b_fc1"],
    }
    head_mask = np.repeat(np.eye(HPC, dtype=np.float32), HD, axis=0)
    return {
        "x": x, "ctx": ctx_2048,
        "ctxT": np.ascontiguousarray(ctx_2048.reshape(B, P, KC, P).transpose(3, 2, 0, 1)),
        "mask_self": mask_1x1xSxS2_fc1[0, 0], "mask_cross": mask_Bx1xSxS2_ff1[:, 0], "mask_lat": mask_BxS2_ik0,
        "ident": np.eye(P, dtype=np.float32),
        "cols": np.concatenate([columns(vectors[n]) if n in vectors else head_mask for n in COLS], axis=1),
        "weights_a": np.concatenate([chunked(weights[n]) for n, _, _ in WEIGHTS_A], axis=1),
        "rows_a": np.stack([w[l1 + "b_ao"], w[l1 + "b_co"], w[l1 + "b2"], w[l2 + "out_b"], w[l2 + "mlp_b2"]]),
        "rows_b": np.stack([w[l3 + "bo1"], w[l3 + "bo2"], w[l3 + "b_fc2"]]),
        "w_qk": np.concatenate([by_pair(w[l3 + f"wq{a}"], w[l3 + f"wk{a}"]) for a in (1, 2)]),
        "w_v": np.concatenate([w[l3 + f"wv{a}"].reshape(KC, P, PAIRS, 2 * W3).transpose(2, 1, 0, 3).reshape(PAIRS, P, -1) for a in (1, 2)]),
        "w_o": np.concatenate([w[l3 + f"wo{a}"].reshape(PAIRS, 2, P, D).transpose(0, 2, 1, 3).reshape(PAIRS, P, 2 * D) for a in (1, 2)]),
        "hcols": np.pad(np.concatenate([np.stack([w[l3 + f"{n}{a}"].reshape(NH, P) for n in ("bq", "bk", "bias_k", "bias_v")], axis=1)
                                        for a in (1, 2)]).reshape(2 * NH * HCOLS, P).T, ((0, 0), (0, HCOLS))),
        "vrows": np.stack([np.concatenate([w[l3 + f"{n}{a}"].reshape(PAIRS, 2 * W3) for a in (1, 2)]) for n in ("bv", "bias_v")],
                          axis=1).reshape(2 * PAIRS, -1),
        "w_up": chunked(w[l3 + "w_fc1"]), "w_down": chunked(w[l3 + "w_fc2"]),
    }


def build(nc, dram):
    with ExitStack() as ctx:
        consts = {
            "ident": ctx.enter_context(nc.sbuf_tensor("ident", [P, P], F32)),
            "cols": ctx.enter_context(nc.sbuf_tensor("cols", [P, NCOLS], F32)),
            "loaded": ctx.enter_context(nc.semaphore("consts_loaded")),
        }
        stages_0_to_2(nc, dram, consts)
        stage_3(nc, dram, consts)


def kernel(**inputs):
    import concourse.bacc as bacc
    from concourse.bass_utils import run_bass_kernel_spmd

    arrays = laid_out(**{name: np.asarray(a) for name, a in inputs.items()})
    arrays = {name: np.ascontiguousarray(a) for name, a in arrays.items()}
    nc = bacc.Bacc("TRN2", target_bir_lowering=False, num_devices=1)
    dram = {name: nc.dram_tensor(name + "_dram", a.shape, mybir.dt.from_np(a.dtype), kind="ExternalInput").ap()
            for name, a in arrays.items()}
    dram["mid"] = nc.dram_tensor("mid_dram", (P, B, D), F32, kind="Internal").ap()
    dram["out"] = nc.dram_tensor("out_dram", (B, P, D), F32, kind="ExternalOutput").ap()
    build(nc, dram)
    result = run_bass_kernel_spmd(nc, [{name + "_dram": a for name, a in arrays.items()}], core_ids=[0])
    return result.results[0]["out_dram"]
```

```python
import numpy as np

import concourse.bass as bass
from concourse import mybir
from contextlib import ExitStack

F32 = mybir.dt.float32
I32 = mybir.dt.int32
F32R = mybir.dt.float32r
ALU = mybir.AluOpType
ACT = mybir.ActivationFunctionType
AX = mybir.AxisListType

P = 128
B = 16
D = 256
KC = D // P
NB = 4
G = B // NB
R = NB * P
NH = 16
HD = D // NH
HPC = P // HD
F = 1024
FC = F // P
BANK = 512
L0K = 16
W3 = 128
PAIRS = NH // 2

COLS = {}
for _name, _n in [("bq0", 1), ("bk0", 1), ("bv0", 1),
                  ("ln1_s", 2), ("ln1_b", 2), ("ln2_s", 2), ("ln2_b", 2), ("ln3_s", 2), ("ln3_b", 2),
                  ("self_bq", 2), ("self_bk", 2), ("self_bv", 2),
                  ("cross_bq", 2), ("cross_bk", 2), ("cross_bv", 2), ("mlp1_b", FC),
                  ("lat_bq", 2), ("lat_bk", 2), ("lat_bv", 2), ("rms_w", 2), ("mlp2_b", FC),
                  ("lnA_s", 2), ("lnA_b", 2), ("lnB_s", 2), ("lnB_b", 2), ("lnM_s", 2), ("lnM_b", 2),
                  ("mlp3_b", FC), ("head_mask", HPC)]:
    COLS[_name] = (sum(n for _, n in COLS.values()), _n)
NCOLS = sum(n for _, n in COLS.values())

ROWS_A = ["self_bo", "cross_bo", "mlp1_bo", "lat_bo", "mlp2_bo"]
ROWS_B = ["a_bo", "b_bo", "mlp3_bo"]

WEIGHTS_A = [("wq0", 1, P), ("wk0", 1, P), ("wv0", 1, P),
             ("self_q", KC, D), ("self_k", KC, D), ("self_v", KC, D), ("self_o", KC, D),
             ("cross_k", KC, D), ("cross_v", KC, D), ("cross_q", KC, D), ("cross_o", KC, D),
             ("mlp1_up", KC, F), ("mlp1_down", FC, D),
             ("lat_q", KC, D), ("lat_k", KC, D), ("lat_v", KC, D), ("lat_o", KC, D),
             ("mlp2_up", KC, F), ("mlp2_down", FC, D)]

NEG = -1.0e30
RSQRT_MAGIC = 1597463007.0
UNITS = {"chan": NB, "self": 4 * NB, "cross": 4 * NB, "lat": 8 * NB}
FIRST_UNIT, NU = {}, 0
for _kind in ("self", "cross", "lat", "chan"):
    FIRST_UNIT[_kind] = NU
    NU += UNITS[_kind]
AHEAD = UNITS["chan"]
BLOCK_UNITS = {"chan": 1, "self": 2, "cross": 2, "lat": 4}
BLOCKS = KC * NB
SCORES_AHEAD = 3
WEIGH_AFTER = 2


def qkv_uses(name):
    return [(name + "_q", 0), (name + "_k", 0), (name + "_q", 1), (name + "_v", 0), (name + "_v", 1), (name + "_k", 1)]


CHAN_USES = [(name, i) for name in ("chan_q", "chan_k", "chan_v") for i in range(2)]
USES_A = ([("ln1", c) for c in range(KC)]
          + qkv_uses("self") + [("self_o", b) for b in range(NB)]
          + [("cross_k", c) for c in range(KC)] + [("cross_v", i) for i in range(2)]
          + [("ln2", c) for c in range(KC)] + [("cross_q", c) for c in range(KC)]
          + [("cross_o", b) for b in range(NB)]
          + [("ctx_k", c) for c in range(KC)] + [("ctx_v", i) for i in range(2)]
          + [("ln3", c) for c in range(KC)]
          + [("mlp1_up", f) for f in range(FC)] + [("mlp1_down", i) for i in range(2)]
          + [("lat", c) for c in range(KC)]
          + qkv_uses("lat") + [("lat_o", b) for b in range(NB)]
          + CHAN_USES
          + [("rms", c) for c in range(KC)]
          + [("mlp2_up", f) for f in range(FC)] + [("mlp2_down", i) for i in range(2)])
NBANKS_A = 2

NEWTON_STEPS = 3
NORM_STEPS = 2 * NB + 1 + 2 + 3 * NEWTON_STEPS
MASKED_UNITS = UNITS["self"] + UNITS["cross"]
DVE_STEPS_A = 4 * NORM_STEPS + 1


def seed(eng, sems):
    for sem in sems:
        eng.sem_inc(sem, 1)


class Banks:

    def __init__(self, uses, banks, first=0):
        self.at = {key: ((first + i) % banks, (first + i) // banks) for i, key in enumerate(uses)}
        assert len(self.at) == len(uses)
        self.per_loop = [sum(b == k for b, _ in self.at.values()) for k in range(banks)]

    def __getitem__(self, key):
        return self.at[key]


def stages_0_to_2(nc, dram, consts):
    ident, cols = consts["ident"], consts["cols"]

    def col(name, c=0):
        at, n = COLS[name]
        assert c < n
        return cols[:, at + c:at + c + 1]

    with ExitStack() as ctx:
        def sb(name, shape, dt=F32):
            return ctx.enter_context(nc.sbuf_tensor(name, shape, dt))

        def sem(name):
            return ctx.enter_context(nc.semaphore(name))

        total = sum(k * n for _, k, n in WEIGHTS_A)
        weights = sb("weights_a", [P, total])
        w, at = {}, 0
        for name, k, n in WEIGHTS_A:
            w[name] = weights[:, at:at + k * n].rearrange("p (k n) -> p k n", k=k)
            at += k * n
        split = [0, 3 * P, at]
        rows = sb("rows_a", [P, len(ROWS_A), D])
        mask_self = sb("mask_self", [P, P])
        madd_self = sb("madd_self", [P, P])
        mask_cross = sb("mask_cross", [P, NB, P])
        madd_cross = sb("madd_cross", [P, NB, P])
        mask_lat = sb("mask_lat", [P, NB, P], I32)
        madd_lat = sb("madd_lat", [P, NB, 2 * P])

        x_in = sb("x_in", [P, NB, D])
        ctx_in = sb("ctx_in", [P, NB, D])
        ctxT = sb("ctxT", [P, KC, NB, P])
        X = sb("X", [P, NB, D])
        Xb = sb("Xb", [P, NB, D])
        xhat = sb("xhat", [P, NB, D])
        hT = sb("hT", [P, KC, R])
        qT = sb("qT", [P, KC, R])
        big = sb("big", [P, NH * R])
        qm = big[:, :].rearrange("p (h r) -> p h r", h=NH)
        upT = big[:, 0:FC * R].rearrange("p (f r) -> p f r", f=FC)
        q0T, k0T = [big[:, FC * R + i * NB * D:FC * R + (i + 1) * NB * D] for i in range(2)]
        v0T = big[:, FC * R + 2 * NB * D:FC * R + 3 * NB * D].rearrange("p (b m c) -> p b m c", b=NB, m=2)
        kT_self = sb("kT_self", [P, KC, R])
        v_self = sb("v_self", [P, NB, NH * 2 * HD])
        kT_lat = sb("kT_lat", [P, KC, NB, 2, P])
        v_lat = sb("v_lat", [P, 2, NB, NH * 2 * HD])
        masked = sb("masked", [P, 2, BANK])
        negated = sb("negated", [P, 3, BANK])
        probs = sb("probs", [P, 4, BANK])
        probsT = sb("probsT", [P, 2, BANK])
        oT = sb("oT", [P, KC, NB, P])
        negmax = sb("negmax", [P, 4, 4])
        sums = sb("sums", [P, 4, 4])
        rsums = sb("rsums", [P, 4, 4])
        stats = sb("stats", [P, NB, 6])
        mv = sb("mv", [P, NB, 2])
        var = sb("var", [P, NB])
        guess = sb("guess", [P, NB], I32)
        rstd = sb("rstd", [P, NB])
        newton = sb("newton", [P, NB])

        def bank(name):
            return ctx.enter_context(nc.psum_tensor(name, [P, BANK], F32))

        scores = [bank(f"scores{i}") for i in range(2)]
        pT_psum = [bank(f"pT_psum{i}") for i in range(2)]
        o_psum = [bank(f"o_psum{i}") for i in range(2)]
        general = [bank(f"general{i}") for i in range(NBANKS_A)]
        uses, first_uses = Banks(USES_A, NBANKS_A), Banks(CHAN_USES, NBANKS_A)

        s = {n: sem(n) for n in (
            "weights0_loaded", "weights_loaded", "rows_loaded", "mask_self_loaded", "x_loaded", "ctx_loaded",
            "ctxT_loaded", "mask_cross_loaded", "mask_lat_loaded", "mid_stored",
            "v_zeroed", "madd_self_ready", "madd_cross_ready", "madd_lat_ready",
            "scores_ready", "scores_free", "max_ready", "exp_done", "rsum_ready", "probs_ready",
            "pT_ready", "pT_copied", "pT_copied_dve", "pv_done", "o_copied",
            "xb_ready", "xhat_ready", "qm_dve", "qm_act", "qm_pool", "chan_done", "cross_done", "ctx_used", "dve_step", "wait_passed")}
        full = [sem(f"general_full{i}") for i in range(NBANKS_A)]
        free = [sem(f"general_free{i}") for i in range(NBANKS_A)]

        def bank_use(g, key):
            if isinstance(g, int):
                return first_uses[key]
            k, n = uses[key]
            return k, g * uses.per_loop[k] + (n + first_uses.per_loop[k])

        def wait_full(eng, g, key):
            k, n = bank_use(g, key)
            eng.wait_ge(full[k], n + 2)
            return general[k], free[k]

        def wait_free(eng, g, key):
            k, n = bank_use(g, key)
            eng.wait_ge(free[k], n + 1)
            return general[k], full[k]

        def wait_copied(eng, g, key):
            k, n = bank_use(g, key)
            eng.wait_ge(free[k], n + 2)

        def after_unit(g, n, back=0):
            value = g * NU + (n + AHEAD - back + 2)
            return max(value, 1) if isinstance(g, int) else value

        def wait_x(eng, g, after):
            if after == "chan":
                eng.wait_ge(s["chan_done"], g * NB + NB + 1)
            elif after.startswith("mlp"):
                for i in range(2):
                    wait_copied(eng, g, (after + "_down", i))
            else:
                for b in range(NB):
                    wait_copied(eng, g, (after + "_o", b))

        def unit_parts(kind, u):
            block, i = divmod(u, BLOCK_UNITS[kind])
            c, b = divmod(block, NB)
            return c, b, i, {"chan": 2, "self": 4, "cross": 4, "lat": 2}[kind]

        NTH = {"self": 0, "cross": 1, "lat": 2}

        def dve_copies(n):
            return 0 <= n < FIRST_UNIT["lat"] and n % 2 == 1

        def wait_pT_copied(eng, g, n):
            if dve_copies(n):
                eng.wait_ge(s["pT_copied_dve"], g * (MASKED_UNITS // 2) + n // 2 + 2)
            else:
                count = AHEAD + n + 1 if n < 0 else AHEAD + sum(not dve_copies(m) for m in range(n + 1))
                value = g * (NU - MASKED_UNITS // 2) + (count + 1)
                eng.wait_ge(s["pT_copied"], max(value, 1) if isinstance(g, int) else value)

        XHAT_AFTER = {"ln1": 4, "ln2": 8, "ln3": 12, "rms": 16}
        XB_AFTER = {"self": 1, "cross": 2, "mlp1": 3, "lat": 4, "mlp2": 5}
        ROW_OF = {"self": 0, "cross": 1, "mlp1": 2, "lat": 3, "mlp2": 4}

        with nc.Block() as block:

            @block.sync
            def _(sp):
                sp.dma_start(ident[:, :], dram["ident"]).then_inc(consts["loaded"], 16)
                sp.dma_start(cols[:, :], dram["cols"]).then_inc(consts["loaded"], 16)
                sp.dma_start(weights[:, 0:split[1]], dram["weights_a"][:, 0:split[1]]).then_inc(s["weights0_loaded"], 16)
                def load_x(g):
                    sp.dma_start(x_in[:, :, :], dram["x"][bass.ds(g * NB, NB), :, :].rearrange("b p n -> p b n")).then_inc(s["x_loaded"], 16)
                    sp.dma_start(ctx_in[:, :, :], dram["ctx"][bass.ds(g * NB, NB), :, :].rearrange("b p n -> p b n")).then_inc(s["ctx_loaded"], 16)

                def loads(g, following):
                    sp.wait_ge(s["chan_done"], g * NB + NB + 1)
                    load_x(following)
                    sp.wait_ge(s["cross_done"], g + 1)
                    sp.dma_start(mask_cross[:, :, :], dram["mask_cross"][bass.ds(g * NB, NB), :, :].rearrange("b p n -> p b n")).then_inc(s["mask_cross_loaded"], 16)
                    sp.wait_ge(s["ctx_used"], g + 1)
                    for c in range(KC):
                        sp.dma_start(ctxT[:, c, :, :], dram["ctxT"][:, c, bass.ds(g * NB, NB), :]).then_inc(s["ctxT_loaded"], 16)
                    sp.wait_ge(s["madd_lat_ready"], g + 1)
                    sp.dma_start(mask_lat[:, :, :], dram["mask_lat"][bass.ds(g * NB, NB), :].partition_broadcast(P)).then_inc(s["mask_lat_loaded"], 16)

                load_x(0)
                with sp.Fori(0, G - 1) as g:
                    loads(g, g + 1)
                loads(G - 1, 0)

            @block.gpsimd
            def _(pool):
                seed(pool, [s["probs_ready"], s["qm_pool"], s["xb_ready"], s["madd_self_ready"], s["madd_cross_ready"], s["madd_lat_ready"],
                            s["v_zeroed"]])
                nc.gpsimd.memset(v_self[:, :, :], 0.0).then_inc(s["v_zeroed"], 1)
                nc.gpsimd.memset(v_lat[:, :, :, :], 0.0).then_inc(s["v_zeroed"], 1)
                nc.gpsimd.memset(madd_lat[:, :, :], 0.0).then_inc(s["v_zeroed"], 1)
                pool.wait_ge(s["mask_self_loaded"], 16)
                nc.gpsimd.tensor_scalar(madd_self[:, :], mask_self[:, :], -1.0, 10000.0, ALU.add, ALU.mult).then_inc(s["madd_self_ready"], 1)
                def add_bias(g, name):
                    x_after = {"self": "chan", "cross": "self", "mlp1": "cross", "lat": "mlp1", "mlp2": "mlp1"}[name]
                    wait_x(pool, g, x_after)
                    if name == "mlp2":
                        pool.wait_ge(s["xhat_ready"], g * 16 + XHAT_AFTER["rms"] + 1)
                    nc.gpsimd.tensor_tensor(Xb[:, :, :], X[:, :, :],
                                            rows[:, ROW_OF[name]:ROW_OF[name] + 1, :].broadcast_to([P, NB, D]),
                                            ALU.add).then_inc(s["xb_ready"], 1)

                def normalise(g, kind):
                    for u in range(UNITS[kind]):
                        n = FIRST_UNIT[kind] + u
                        segs = unit_parts(kind, u)[3]
                        pr = probs[:, n % 4, :].rearrange("p (s k) -> p s k", s=segs)
                        pool.wait_ge(s["rsum_ready"], after_unit(g, n))
                        nc.gpsimd.tensor_tensor(pr, pr, rsums[:, n % 4, 0:segs].unsqueeze(2).broadcast_to([P, segs, BANK // segs]),
                                                ALU.mult).then_inc(s["probs_ready"], 1)
                        if kind != "chan" and u < HPC // 2:
                            mask_head(g, kind, HPC // 2 + u)

                def mask_head(g, kind, h):
                    wait_copied(pool, g, (kind + "_q", 1))
                    mask = COLS["head_mask"][0] + h
                    nc.gpsimd.tensor_tensor(qm[:, HPC + h, :], qT[:, 1, :], cols[:, mask:mask + 1].broadcast_to([P, R]), ALU.mult).then_inc(s["qm_pool"], 1)

                normalise(-1, "chan")
                with pool.Fori(0, G) as g:
                    pool.wait_ge(s["rows_loaded"], 16)
                    add_bias(g, "self")
                    pool.wait_ge(s["mask_cross_loaded"], g * 16 + 16)
                    pool.sem_inc(s["wait_passed"], 1)
                    nc.gpsimd.tensor_scalar(madd_cross[:, :, :], mask_cross[:, :, :], -1.0, 10000.0, ALU.add, ALU.mult).then_inc(s["madd_cross_ready"], 1)
                    normalise(g, "self")
                    add_bias(g, "cross")
                    normalise(g, "cross")
                    add_bias(g, "mlp1")
                    pool.wait_ge(s["v_zeroed"], 4)
                    pool.wait_ge(s["mask_lat_loaded"], g * 16 + 16)
                    pool.sem_inc(s["wait_passed"], 1)
                    nc.gpsimd.tensor_scalar(madd_lat[:, :, 0:P], mask_lat[:, :, :], 0.0, NEG, ALU.is_equal, ALU.mult).then_inc(s["madd_lat_ready"], 1)
                    add_bias(g, "lat")
                    normalise(g, "lat")
                    add_bias(g, "mlp2")
                    normalise(g, "chan")
                    wait_x(pool, g, "mlp2")
                    pool.dma_start(dram["mid"][:, bass.ds(g * NB, NB), :], Xb[:, :, :]).then_inc(s["mid_stored"], 16)
                    pool.wait_ge(s["mid_stored"], g * 16 + 16)

            @block.scalar
            def _(act):
                seed(act, [s["exp_done"], s["pT_copied"], s["o_copied"], s["qm_act"]])
                act.dma_start(weights[:, split[1]:split[2]], dram["weights_a"][:, split[1]:split[2]]).then_inc(s["weights_loaded"], 16)
                act.dma_start(mask_self[:, :], dram["mask_self"]).then_inc(s["mask_self_loaded"], 16)
                act.dma_start(rows[:, :, :], dram["rows_a"].partition_broadcast(P)).then_inc(s["rows_loaded"], 16)
                act.wait_ge(consts["loaded"], 32)
                def exps(g, kind, u):
                    n = FIRST_UNIT[kind] + u
                    segs = unit_parts(kind, u)[3]
                    width = BANK // segs
                    act.wait_ge(s["max_ready"], after_unit(g, n))
                    act.wait_ge(s["pT_ready"], after_unit(g, n, 4))
                    for i in range(segs):
                        src = scores[n % 2] if kind == "chan" else negated[:, n % 3, :]
                        last = nc.scalar.activation(probs[:, n % 4, i * width:(i + 1) * width], src[:, i * width:(i + 1) * width],
                                                    ACT.Exp, scale=1.0 if kind == "chan" else -1.0, bias=negmax[:, n % 4, i:i + 1], accum_out=sums[:, n % 4, i:i + 1])
                        if i == segs - 1:
                            last.then_inc(s["exp_done"], 1)

                def copy_pT(g, kind, u):
                    n = FIRST_UNIT[kind] + u
                    act.wait_ge(s["pT_ready"], after_unit(g, n))
                    act.wait_ge(s["pv_done"], after_unit(g, n, 2))
                    nc.scalar.copy(probsT[:, n % 2, :], pT_psum[n % 2][:, :]).then_inc(s["pT_copied"], 1)

                def copy_o(g, kind, block):
                    act.wait_ge(s["pv_done"], after_unit(g, FIRST_UNIT[kind] + (block + 1) * BLOCK_UNITS[kind] - 1))
                    c, b = divmod(block, NB)
                    nc.scalar.activation(oT[:, c, b, :], o_psum[block % 2][:, 0:P], ACT.Identity,
                                         bias=col(kind + "_bv", c)).then_inc(s["o_copied"], 1)

                def attention(g, kind, meanwhile={}):
                    n = UNITS[kind]
                    per = BLOCK_UNITS[kind]
                    for t in range(n + SCORES_AHEAD + WEIGH_AFTER + 1):
                        if 0 <= t - SCORES_AHEAD < n and not dve_copies(FIRST_UNIT[kind] + t - SCORES_AHEAD):
                            copy_pT(g, kind, t - SCORES_AHEAD)
                        if t < n:
                            exps(g, kind, t)
                        if t in meanwhile:
                            meanwhile[t]()
                        done = t - SCORES_AHEAD - WEIGH_AFTER
                        if kind != "chan" and 0 <= done < n and done % per == per - 1:
                            copy_o(g, kind, done // per)

                def norm_copy(g, name):
                    src, freed = wait_full(act, g, (name, 1))
                    if name == "lat":
                        ins = nc.scalar.copy(hT[:, 1, :], src[:, :])
                    elif name == "rms":
                        ins = nc.scalar.activation(hT[:, 1, :], src[:, :], ACT.Copy, scale=col("rms_w", 1))
                    else:
                        ins = nc.scalar.activation(hT[:, 1, :], src[:, :], ACT.Identity, scale=col(name + "_s", 1), bias=col(name + "_b", 1))
                    ins.then_inc(freed, 1)

                def keys(g, name, bias, out, split_b, chunks=range(KC)):
                    for c in chunks:
                        src, freed = wait_full(act, g, (name + "_k", c))
                        if split_b:
                            src = src[:, :].rearrange("p (b k) -> p b k", b=NB)
                        else:
                            src = src[:, :]
                        nc.scalar.activation(out[c], src, ACT.Identity, bias=col(bias + "_bk", c)).then_inc(freed, 1)

                def values(g, name, out, halves=range(2)):
                    for i in halves:
                        src, freed = wait_full(act, g, (name + "_v", i))
                        for j in range(2):
                            dst = out[:, 2 * i + j, :].rearrange("p (t w d) -> p t w d", w=4, d=HD)[:, :, 0:4:3, :]
                            ins = nc.scalar.copy(dst, src[:, j * D:(j + 1) * D].rearrange("p (t w d) -> p t w d", w=2, d=HD))
                        ins.then_inc(freed, 1)

                def mask_heads(g, kind):
                    wait_copied(act, g, (kind + "_q", 0))
                    for h in range(HPC // 2, HPC):
                        nc.scalar.activation(qm[:, h, :], qT[:, 0, :], ACT.Copy, scale=col("head_mask", h)).then_inc(s["qm_act"], 1)

                def gelus(g, name):
                    for f in range(FC):
                        src, freed = wait_full(act, g, (name + "_up", f))
                        nc.scalar.activation(upT[:, f, :], src[:, :], ACT.Gelu_apprx_tanh, bias=col(name + "_b", f)).then_inc(freed, 1)

                def chan_inputs(g):
                    for i in range(2):
                        src, freed = wait_full(act, g, ("chan_q", i))
                        nc.scalar.activation(q0T[:, i * BANK:(i + 1) * BANK], src[:, :], ACT.Identity, bias=col("bq0")).then_inc(freed, 1)
                    for i in range(2):
                        src, freed = wait_full(act, g, ("chan_k", i))
                        nc.scalar.activation(k0T[:, i * BANK:(i + 1) * BANK], src[:, :], ACT.Identity, bias=col("bk0")).then_inc(freed, 1)
                    for i in range(2):
                        src, freed = wait_full(act, g, ("chan_v", i))
                        nc.scalar.copy(v0T[:, 2 * i:2 * i + 2, :, :], src[:, :].rearrange("p (b m c) -> p b m c", b=2, m=2)).then_inc(freed, 1)

                chan_inputs(-1)
                attention(-1, "chan")
                with act.Fori(0, G) as g:
                    norm_copy(g, "ln1")
                    act.wait_ge(s["v_zeroed"], 3)
                    kT = [kT_self[:, c, :] for c in range(KC)]
                    keys(g, "self", "self", kT, False, [0])
                    mask_heads(g, "self")
                    attention(g, "self", {1: lambda: values(g, "self", v_self, [0]), 2: lambda: values(g, "self", v_self, [1]),
                                       3: lambda: keys(g, "self", "self", kT, False, [1])})
                    kT_ctx = [kT_lat[:, c, :, 0, :] for c in range(KC)]
                    keys(g, "cross", "cross", kT_ctx, True)
                    values(g, "cross", v_lat[:, 0, :, :])
                    norm_copy(g, "ln2")
                    mask_heads(g, "cross")
                    attention(g, "cross")
                    keys(g, "ctx", "lat", kT_ctx, True)
                    values(g, "ctx", v_lat[:, 0, :, :])
                    norm_copy(g, "ln3")
                    gelus(g, "mlp1")
                    norm_copy(g, "lat")
                    kT_own, v_own = [kT_lat[:, c, :, 1, :] for c in range(KC)], v_lat[:, 1, :, :]
                    keys(g, "lat", "lat", kT_own, True, [0])
                    mask_heads(g, "lat")
                    attention(g, "lat", {1: lambda: values(g, "lat", v_own, [0]), 2: lambda: values(g, "lat", v_own, [1]),
                                      3: lambda: keys(g, "lat", "lat", kT_own, True, [1])})
                    chan_inputs(g)
                    norm_copy(g, "rms")
                    gelus(g, "mlp2")
                    attention(g, "chan")

            @block.vector
            def _(dve):
                seed(dve, [s["pT_copied_dve"], s["max_ready"], s["rsum_ready"], s["chan_done"], s["cross_done"], s["scores_free"], s["qm_dve"],
                           s["xhat_ready"], s["dve_step"]] + free)
                dve.wait_ge(consts["loaded"], 32)
                steps = [0]

                def step(ins):
                    steps[0] += 1
                    ins.then_inc(s["dve_step"], 1)

                def wait_step(g, apart=False):
                    value = steps[0] if isinstance(g, int) else g * DVE_STEPS_A + steps[0]
                    if apart:
                        dve.wait_ge(s["dve_step"], value + 1)
                        dve.sem_inc(s["wait_passed"], 1)
                    else:
                        dve.wait_ge(s["dve_step"], value + 1)

                def front(g, kind, u):
                    n = FIRST_UNIT[kind] + u
                    c, b, i, segs = unit_parts(kind, u)
                    dve.wait_ge(s["scores_ready"], after_unit(g, n))
                    ready = scores[n % 2][:, :].rearrange("p (s k) -> p s k", s=segs)
                    if kind != "chan":
                        m = masked[:, n % 2, :].rearrange("p (s k) -> p s k", s=segs)
                        dve.wait_ge(s["exp_done"], after_unit(g, n, 3))
                    before = after_unit(g, n, 4)
                    if kind == "chan":
                        dve.wait_ge(s["exp_done"], before)
                        nc.vector.tensor_reduce(negmax[:, n % 4, 0:segs], ready, axis=AX.X, op=ALU.max, negate=True).then_inc(s["max_ready"], 1)
                        return
                    if kind == "lat":
                        add = madd_lat[:, b, :]
                        dve.wait_ge(s["exp_done"], before)
                        dve.sem_inc(s["wait_passed"], 1)
                    else:
                        mul, add = (mask_self[:, :].unsqueeze(1), madd_self[:, :]) if kind == "self" else (mask_cross[:, b:b + 1, :], madd_cross[:, b, :])
                        nc.vector.tensor_tensor(m, ready, mul.broadcast_to([P, segs, P]), ALU.mult).then_inc(s["scores_free"], 1)
                        dve.wait_ge(s["exp_done"], before)
                        dve.wait_ge(s["scores_free"], g * MASKED_UNITS + n + 1 - FIRST_UNIT["self"] + 1)
                        dve.sem_inc(s["wait_passed"], 1)
                        ready = m
                    for j in range(segs):
                        last = nc.vector.tensor_tensor_reduce(out=negated[:, n % 3, j * (BANK // segs):(j + 1) * (BANK // segs)],
                                                              in0=ready[:, j, :], in1=add, scale=-1.0, scalar=3.0e38, op0=ALU.add, op1=ALU.min,
                                                              accum_out=negmax[:, n % 4, j:j + 1])
                    last.then_inc(s["max_ready"], 1)

                def rsum(g, kind, u):
                    n = FIRST_UNIT[kind] + u
                    segs = unit_parts(kind, u)[3]
                    dve.wait_ge(s["exp_done"], after_unit(g, n))
                    dve.wait_ge(s["probs_ready"], after_unit(g, n, 4))
                    nc.vector.reciprocal(rsums[:, n % 4, 0:segs], sums[:, n % 4, 0:segs]).then_inc(s["rsum_ready"], 1)

                def copy_pT(g, kind, u):
                    n = FIRST_UNIT[kind] + u
                    dve.wait_ge(s["pT_ready"], after_unit(g, n))
                    dve.wait_ge(s["pv_done"], after_unit(g, n, 2))
                    nc.vector.tensor_copy(probsT[:, n % 2, :], pT_psum[n % 2][:, :]).then_inc(s["pT_copied_dve"], 1)

                def residual(g, kind, b):
                    src, freed = wait_full(dve, g, (kind + "_o", b))
                    dst = Xb if kind == "lat" else X
                    if b == 0:
                        dve.wait_ge(s["xb_ready"], g * 5 + XB_AFTER[kind] + 1)
                    nc.vector.tensor_tensor(dst[:, b, :], src[:, 0:D], Xb[:, b, :], ALU.add).then_inc(freed, 1)

                def chan_residual(g, b):
                    dve.wait_ge(s["pv_done"], after_unit(g, FIRST_UNIT["chan"] + b))
                    if b == 0 and not isinstance(g, int):
                        dve.wait_ge(s["xb_ready"], g * 5 + XB_AFTER["mlp2"] + 1)
                    nc.vector.scalar_tensor_tensor(out=X[:, b, :], in0=o_psum[b % 2][:, 0:D], scalar=col("bv0"), in1=x_in[:, b, :],
                                                   op0=ALU.add, op1=ALU.add).then_inc(s["chan_done"], 1)

                def attention(g, kind, meanwhile={}):
                    n = UNITS[kind]
                    per = BLOCK_UNITS[kind]
                    for t in range(n + SCORES_AHEAD + WEIGH_AFTER + 4):
                        if t < n:
                            front(g, kind, t)
                        if 0 <= t - SCORES_AHEAD < n and dve_copies(FIRST_UNIT[kind] + t - SCORES_AHEAD):
                            copy_pT(g, kind, t - SCORES_AHEAD)
                        if 0 <= t - 1 < n:
                            rsum(g, kind, t - 1)
                        if t in meanwhile:
                            meanwhile[t]()
                        done = t - SCORES_AHEAD - WEIGH_AFTER - (1 if kind == "chan" else 3)
                        if 0 <= done < n and done % per == per - 1 and (kind == "chan" or done // per >= NB):
                            b = done // per % NB
                            if kind == "chan":
                                chan_residual(g, b)
                                dve.wait_ge(s["chan_done"], (g + 1) * NB + b + 2)
                            else:
                                residual(g, kind, b)
                                wait_copied(dve, g, (kind + "_o", b))
                            step(nc.vector.bn_stats(stats[:, b, :], (Xb if kind == "lat" else X)[:, b, :]))

                def norm(g, name):
                    src = Xb if name == "rms" else X
                    wait_step(g, apart=True)
                    for b in range(NB):
                        step(nc.vector.bn_aggr(mv[:, b, :], stats[:, b, :]))
                    wait_step(g)
                    if name == "rms":
                        step(nc.vector.tensor_tensor(newton[:, :], mv[:, :, 0], mv[:, :, 0], ALU.mult))
                        wait_step(g)
                        step(nc.vector.scalar_tensor_tensor(out=var[:, :], in0=mv[:, :, 1], scalar=1e-6, in1=newton[:, :], op0=ALU.add, op1=ALU.add))
                    else:
                        step(nc.vector.tensor_scalar(var[:, :], mv[:, :, 1], 1e-5, None, ALU.add))
                    wait_step(g)
                    inverse_root(g)
                    for b in range(NB):
                        if name == "rms":
                            ins = nc.vector.tensor_scalar(xhat[:, b, :], src[:, b, :], rstd[:, b:b + 1], None, ALU.mult)
                        else:
                            ins = nc.vector.tensor_scalar(xhat[:, b, :], src[:, b, :], mv[:, b, 0:1], rstd[:, b:b + 1], ALU.subtract, ALU.mult)
                        ins.then_inc(s["xhat_ready"], 1)

                def inverse_root(g):
                    step(nc.vector.tensor_single_scalar(guess[:, :], var[:, :].bitcast(I32), 1, ALU.logical_shift_right))
                    wait_step(g)
                    step(nc.vector.tensor_scalar(guess[:, :], guess[:, :], -1.0, RSQRT_MAGIC, ALU.mult, ALU.add))
                    wait_step(g)
                    y = guess[:, :].bitcast(F32)
                    for i in range(NEWTON_STEPS):
                        step(nc.vector.scalar_tensor_tensor(out=newton[:, :], in0=y, scalar=-0.5, in1=y, op0=ALU.mult, op1=ALU.mult))
                        wait_step(g)
                        step(nc.vector.tensor_tensor(newton[:, :], newton[:, :], var[:, :], ALU.mult))
                        wait_step(g)
                        step(nc.vector.scalar_tensor_tensor(out=rstd[:, :], in0=newton[:, :], scalar=1.5, in1=y, op0=ALU.add, op1=ALU.mult))
                        wait_step(g)
                        y = rstd[:, :]

                def norm_copy(g, name):
                    src, freed = wait_full(dve, g, (name, 0))
                    if name == "lat":
                        ins = nc.vector.tensor_copy(hT[:, 0, :], src[:, :])
                    elif name == "rms":
                        ins = nc.vector.tensor_scalar(hT[:, 0, :], src[:, :], col("rms_w", 0), None, ALU.mult)
                    else:
                        ins = nc.vector.tensor_scalar(hT[:, 0, :], src[:, :], col(name + "_s", 0), col(name + "_b", 0), ALU.mult, ALU.add)
                    ins.then_inc(freed, 1)

                def queries(g, nth, kind, c):
                    scale = 1.0 / HD if kind == "lat" else HD ** -0.5
                    src, freed = wait_full(dve, g, (kind + "_q", c))
                    half = HPC // 2
                    dve.wait_ge(s["qm_dve"], (g * 3 + nth) * HPC + c * half + 1)
                    dve.wait_ge(s["qm_pool" if c else "qm_act"], (g * 3 + nth) * half + 1)
                    nc.vector.tensor_scalar(qT[:, c, :], src[:, :], col(kind + "_bq", c), scale, ALU.add, ALU.mult).then_inc(freed, 1)

                def mask_heads(g, kind, c, heads):
                    wait_copied(dve, g, (kind + "_q", c))
                    for h in heads:
                        nc.vector.tensor_scalar(qm[:, c * HPC + h, :], qT[:, c, :], col("head_mask", h), None, ALU.mult).then_inc(s["qm_dve"], 1)

                def first_queries(g, nth, kind):
                    queries(g, nth, kind, 0)
                    mask_heads(g, kind, 0, range(HPC // 2))

                def other_queries(g, nth, kind):
                    steps = {2 + h: lambda h=h: mask_heads(g, kind, 1, [h]) for h in range(HPC // 2)}
                    return {(1 if kind == "cross" else 0): lambda: queries(g, nth, kind, 1), **steps}

                def mlp_residual(g, name, halves):
                    dst = Xb if name == "mlp2" else X
                    dve.wait_ge(s["xb_ready"], g * 5 + XB_AFTER[name] + 1)
                    for i in halves:
                        src, freed = wait_full(dve, g, (name + "_down", i))
                        nc.vector.tensor_tensor(dst[:, 2 * i:2 * i + 2, :], src[:, :].rearrange("p (b n) -> p b n", b=2),
                                                Xb[:, 2 * i:2 * i + 2, :], ALU.add).then_inc(freed, 1)

                attention(-1, "chan")
                norm(-1, "ln1")
                with dve.Fori(0, G) as g:
                    norm_copy(g, "ln1")
                    first_queries(g, 0, "self")
                    dve.wait_ge(s["madd_self_ready"], 2)
                    attention(g, "self", other_queries(g, 0, "self"))
                    norm(g, "ln2")
                    norm_copy(g, "ln2")
                    first_queries(g, 1, "cross")
                    dve.wait_ge(s["madd_cross_ready"], g + 2)
                    attention(g, "cross", other_queries(g, 1, "cross"))
                    norm(g, "ln3")
                    dve.sem_inc(s["cross_done"], 1)
                    norm_copy(g, "ln3")
                    mlp_residual(g, "mlp1", range(2))
                    norm_copy(g, "lat")
                    first_queries(g, 2, "lat")
                    dve.wait_ge(s["madd_lat_ready"], g + 2)
                    attention(g, "lat", other_queries(g, 2, "lat"))
                    norm(g, "rms")
                    norm_copy(g, "rms")
                    attention(g, "chan", {5: lambda: mlp_residual(g, "mlp2", [0])})
                    norm(g, "ln1")
                    mlp_residual(g, "mlp2", [1])
                    assert steps[0] == NORM_STEPS + DVE_STEPS_A, steps

            @block.tensor
            def _(pe):
                seed(pe, [s["scores_ready"], s["pT_ready"], s["pv_done"], s["ctx_used"]] + full)
                pe.wait_ge(consts["loaded"], 32)
                pe.wait_ge(s["weights0_loaded"], 16)
                def transposed(g, name):
                    src = X if name == "lat" else xhat
                    for c in range(KC):
                        out, filled = wait_free(pe, g, (name, c))
                        for b in range(NB):
                            if name == "lat":
                                if c == b == 0:
                                    wait_x(pe, g, "mlp1")
                            elif c == 0:
                                pe.wait_ge(s["xhat_ready"], g * 16 + XHAT_AFTER[name] - NB + b + 2)
                            last = nc.tensor.transpose(out[:, b * P:(b + 1) * P], src[:, b, c * P:(c + 1) * P], ident[:, :])
                        last.then_inc(filled, 1)

                def project(g, key, weight, chunk, rhs):
                    out, filled = wait_free(pe, g, key)
                    for c in range(KC):
                        last = nc.tensor.matmul(out[:, :], w[weight][:, c, chunk * P:(chunk + 1) * P], rhs[c], start=(c == 0), stop=(c == KC - 1))
                    last.then_inc(filled, 1)

                def project_rows(g, key, weight, i, lhs):
                    out, filled = wait_free(pe, g, key)
                    for j in range(2):
                        for c in range(KC):
                            last = nc.tensor.matmul(out[:, j * D:(j + 1) * D], lhs(c, 2 * i + j), w[weight][:, c, :], start=(c == 0), stop=(c == KC - 1))
                    last.then_inc(filled, 1)

                def scores_of(g, kind, u):
                    n = FIRST_UNIT[kind] + u
                    c, b, i, segs = unit_parts(kind, u)
                    old = n - 2
                    if old < 0 or old >= FIRST_UNIT["chan"]:
                        pe.wait_ge(s["exp_done"], after_unit(g, old))
                    elif old < FIRST_UNIT["lat"]:
                        pe.wait_ge(s["scores_free"], g * MASKED_UNITS + old + 2)
                    else:
                        pe.wait_ge(s["max_ready"], after_unit(g, old))
                    out = scores[n % 2]
                    if kind != "chan" and b == i == 0:
                        wait_copied(pe, g, (kind + "_k", c))
                    for j in range(segs):
                        if kind != "chan" and b == 0:
                            half, in_chunk = HPC // 2, segs * i + j
                            if in_chunk < half:
                                pe.wait_ge(s["qm_dve"], (g * 3 + NTH[kind]) * HPC + c * half + in_chunk + 2)
                            else:
                                pe.wait_ge(s["qm_pool" if c else "qm_act"], (g * 3 + NTH[kind]) * half + in_chunk - half + 2)
                        if kind == "chan":
                            last = nc.tensor.matmul(out[:, j * D:(j + 1) * D], q0T[:, b * D + j * P:b * D + (j + 1) * P], k0T[:, b * D:(b + 1) * D], start=True, stop=True)
                        elif kind == "lat":
                            h = c * HPC + 2 * i + j
                            last = nc.tensor.matmul(out[:, j * D:(j + 1) * D], qm[:, h, b * P:(b + 1) * P],
                                                    kT_lat[:, c, b, :, :], start=True, stop=True)
                        else:
                            h = c * HPC + 4 * i + j
                            key = kT_self[:, c, b * P:(b + 1) * P] if kind == "self" else kT_lat[:, c, b, 0, :]
                            last = nc.tensor.matmul(out[:, j * P:(j + 1) * P], qm[:, h, b * P:(b + 1) * P], key, start=True, stop=True)
                    last.then_inc(s["scores_ready"], 1)

                def transpose_probs(g, kind, u):
                    n = FIRST_UNIT[kind] + u
                    pe.wait_ge(s["probs_ready"], after_unit(g, n))
                    wait_pT_copied(pe, g, n - 2)
                    for j in range(4):
                        at = (j % 2) * 2 + j // 2 if kind == "chan" else j
                        last = nc.tensor.transpose(pT_psum[n % 2][:, at * P:(at + 1) * P], probs[:, n % 4, j * P:(j + 1) * P], ident[:, :])
                    last.then_inc(s["pT_ready"], 1)

                def weigh_values(g, kind, u):
                    n = FIRST_UNIT[kind] + u
                    c, b, i, segs = unit_parts(kind, u)
                    wait_pT_copied(pe, g, n)
                    block = c * NB + b
                    if i == 0:
                        if kind == "chan":
                            if b >= 2:
                                pe.wait_ge(s["chan_done"], (g + 1) * NB + b)
                            else:
                                pe.wait_ge(s["o_copied"], (g + 1) * 3 * BLOCKS + 1)
                        elif kind == "self" and block < 2:
                            pe.wait_ge(s["chan_done"], g * NB + NB - 1 + block + 1)
                        else:
                            pe.wait_ge(s["o_copied"], g * 3 * BLOCKS + BLOCKS * NTH[kind] + block)
                        if kind != "chan" and block == 0:
                            for half in range(2):
                                wait_copied(pe, g, (kind + "_v", half))
                    pT = probsT[:, n % 2, :]
                    out = o_psum[block % 2]
                    if kind == "chan":
                        for m in range(2):
                            last = nc.tensor.matmul(out[:, 0:D], v0T[:, b, m, :], pT[:, m * D:(m + 1) * D], start=(m == 0), stop=(m == 1))
                    elif kind == "lat":
                        for j in range(2):
                            h = c * HPC + 2 * i + j
                            for m in range(2):
                                last = nc.tensor.matmul(out[32 * i:32 * i + 32, 0:P], v_lat[:, m, b, 32 * h:32 * h + 32],
                                                        pT[:, (2 * j + m) * P:(2 * j + m + 1) * P], start=(j == 0 and m == 0), stop=(j == 1 and m == 1))
                    else:
                        for j in range(4):
                            h = c * HPC + 4 * i + j
                            row = 32 * (h // 2 % 4)
                            v = v_self[:, b, 32 * h:32 * h + 32] if kind == "self" else v_lat[:, 0, b, 32 * h:32 * h + 32]
                            last = nc.tensor.matmul(out[row:row + 32, 0:P], v, pT[:, j * P:(j + 1) * P], start=(j % 2 == 0), stop=(j % 2 == 1))
                    last.then_inc(s["pv_done"], 1)

                def output(g, kind, b):
                    pe.wait_ge(s["o_copied"], g * 3 * BLOCKS + BLOCKS * NTH[kind] + NB + b + 2)
                    out, filled = wait_free(pe, g, (kind + "_o", b))
                    for c in range(KC):
                        last = nc.tensor.matmul(out[:, 0:D], oT[:, c, b, :], w[kind + "_o"][:, c, :], start=(c == 0), stop=(c == KC - 1))
                    last.then_inc(filled, 1)

                def attention(g, kind, meanwhile={}):
                    n = UNITS[kind]
                    per = BLOCK_UNITS[kind]
                    for t in range(n + SCORES_AHEAD + WEIGH_AFTER + 3):
                        if t < n:
                            scores_of(g, kind, t)
                        if t in meanwhile:
                            meanwhile[t]()
                        if 0 <= t - SCORES_AHEAD - WEIGH_AFTER < n:
                            weigh_values(g, kind, t - SCORES_AHEAD - WEIGH_AFTER)
                        if 0 <= t - SCORES_AHEAD < n:
                            transpose_probs(g, kind, t - SCORES_AHEAD)
                        done = t - SCORES_AHEAD - WEIGH_AFTER - 2
                        if kind != "chan" and NB * per <= done < n and done % per == per - 1:
                            output(g, kind, done // per - NB)

                def mlp_up(g, name):
                    for f in range(FC):
                        project(g, (name + "_up", f), name + "_up", f, [hT[:, c, :] for c in range(KC)])

                def mlp_down(g, name, b):
                    k, _ = uses[(name + "_down", b // 2)]
                    if b % 2 == 0:
                        wait_free(pe, g, (name + "_down", b // 2))
                    for f in range(FC):
                        if b == 0:
                            wait_copied(pe, g, (name + "_up", f))
                        last = nc.tensor.matmul(general[k][:, b % 2 * D:(b % 2 + 1) * D], upT[:, f, b * P:(b + 1) * P], w[name + "_down"][:, f, :], start=(f == 0), stop=(f == FC - 1))
                    if b % 2 == 1:
                        last.then_inc(full[k], 1)

                hT_chunks = [hT[:, c, :] for c in range(KC)]
                ctxT_chunks = [ctxT[:, c, :, :] for c in range(KC)]

                def hT_rows(c, b):
                    return hT[:, c, b * P:(b + 1) * P]

                def ctxT_rows(c, b):
                    return ctxT[:, c, b, :]

                def own_attention(g, name):
                    project(g, (name + "_q", 0), name + "_q", 0, hT_chunks)
                    project(g, (name + "_k", 0), name + "_k", 0, hT_chunks)
                    attention(g, name, {0: lambda: project(g, (name + "_q", 1), name + "_q", 1, hT_chunks),
                                     1: lambda: project_rows(g, (name + "_v", 0), name + "_v", 0, hT_rows),
                                     2: lambda: project_rows(g, (name + "_v", 1), name + "_v", 1, hT_rows),
                                     3: lambda: project(g, (name + "_k", 1), name + "_k", 1, hT_chunks)})

                def chan_inputs(g):
                    pe.wait_ge(s["x_loaded"], g * 16 + 32)
                    for i in range(2):
                        out, filled = wait_free(pe, g, ("chan_q", i))
                        nc.tensor.matmul(out[:, :], w["wq0"][:, 0, :], x_in[:, 2 * i:2 * i + 2, :], start=True, stop=True).then_inc(filled, 1)
                    pe.wait_ge(s["ctx_loaded"], g * 16 + 32)
                    for i in range(2):
                        out, filled = wait_free(pe, g, ("chan_k", i))
                        nc.tensor.matmul(out[:, :], w["wk0"][:, 0, :], ctx_in[:, 2 * i:2 * i + 2, :], start=True, stop=True).then_inc(filled, 1)
                    for i in range(2):
                        out, filled = wait_free(pe, g, ("chan_v", i))
                        for j in range(4):
                            b, m = 2 * i + j // 2, j % 2
                            last = nc.tensor.matmul(out[:, j * P:(j + 1) * P], ctx_in[:, b, m * P:(m + 1) * P], w["wv0"][:, 0, :], start=True, stop=True)
                        last.then_inc(filled, 1)
                    for i in range(2):
                        wait_copied(pe, g, ("chan_v", i))

                chan_inputs(-1)
                attention(-1, "chan")
                with pe.Fori(0, G) as g:

                    pe.wait_ge(s["weights_loaded"], 16)
                    transposed(g, "ln1")
                    for c in range(KC):
                        wait_copied(pe, g, ("ln1", c))
                    own_attention(g, "self")

                    pe.wait_ge(s["ctxT_loaded"], g * 32 + 32)
                    for c in range(KC):
                        project(g, ("cross_k", c), "cross_k", c, ctxT_chunks)
                    for i in range(2):
                        project_rows(g, ("cross_v", i), "cross_v", i, ctxT_rows)
                    transposed(g, "ln2")
                    for c in range(KC):
                        wait_copied(pe, g, ("ln2", c))
                    project(g, ("cross_q", 0), "cross_q", 0, hT_chunks)
                    attention(g, "cross", {1: lambda: project(g, ("cross_q", 1), "cross_q", 1, hT_chunks)})

                    for c in range(KC):
                        project(g, ("ctx_k", c), "lat_k", c, ctxT_chunks)
                    for i in range(2):
                        project_rows(g, ("ctx_v", i), "lat_v", i, ctxT_rows)
                    for i in range(2):
                        wait_copied(pe, g, ("ctx_v", i))
                    pe.sem_inc(s["ctx_used"], 1)
                    transposed(g, "ln3")
                    for c in range(KC):
                        wait_copied(pe, g, ("ln3", c))
                    mlp_up(g, "mlp1")
                    for b in range(NB):
                        mlp_down(g, "mlp1", b)

                    transposed(g, "lat")
                    for c in range(KC):
                        wait_copied(pe, g, ("lat", c))
                    own_attention(g, "lat")
                    chan_inputs(g)
                    transposed(g, "rms")
                    for c in range(KC):
                        wait_copied(pe, g, ("rms", c))
                    mlp_up(g, "mlp2")
                    attention(g, "chan", {t: lambda b=b: mlp_down(g, "mlp2", b) for b, t in enumerate((1, 3, 5, 9))})


STEPS = 2 * G
ATT_UNITS = PAIRS * STEPS
SCALE3 = W3 ** -0.5
HCOLS = 4
NGEN = 4
LATE = 3
NORM_STEPS3 = 2 * B + 2 + 3 * NEWTON_STEPS

HI, LO = 0, 1
PASSES = [(HI, HI), (LO, HI), (HI, LO)]


def pair_work(last):
    values = [[("v", t, 0), ("v", t, 1)] for t in range(G)]
    outputs = [[("out", t, 0), ("out", t, 1)] for t in range(G)]
    if last:
        return [[*values[0], ("q", 0)], [*values[1], ("k", 0)], [*values[2], ("q", 1)], [*values[3], ("k", 1)],
                [("q", 2), ("k", 2), ("q", 3)], [("k", 3), *outputs[0][:1]], [outputs[0][1], outputs[1][0]], [outputs[1][1], outputs[2][0]]]
    return [[("q", 0), ("k", 0), *values[0]], [("q", 1), ("k", 1), *values[1]], [("q", 2), ("k", 2), *values[2]], [("q", 3), *values[3]],
            [("k", 3), ("q", 4), ("k", 4)], [("q", 5), ("k", 5), *outputs[0]], [("q", 6), ("k", 6), *outputs[1]],
            [("q", 7), ("k", 7), *outputs[2][:1]]]


def pair_uses(last):
    return sum(pair_work(last), []) + [("out", G - 2, 1), ("out", G - 1, 0), ("out", G - 1, 1)]


LN_USES = [("ln", g, c) for g in range(2) for c in range(KC)] + [("k", 0), ("k", 1)]
for _g in range(G):
    LN_USES.append(("q", _g))
    if _g + 2 < G:
        LN_USES += [("ln", _g + 2, c) for c in range(KC)] + [("k", _g + 2)]
SECTIONS = {"ln": Banks(LN_USES, NGEN), "pair": Banks(pair_uses(False), NGEN), "last": Banks(pair_uses(True), NGEN),
            "mlp_ln": Banks([("ln", g, c) for g in range(G) for c in range(KC)], NGEN),
            "mlp": Banks([("up", f) for f in range(FC)] + [("down", i) for i in range(2)], NGEN)}


def bank_count(section, a, i, key):
    k, n = SECTIONS[section][key]
    per = {name: SECTIONS[name].per_loop[k] for name in SECTIONS}
    attention = per["ln"] + (PAIRS - 1) * per["pair"] + per["last"]
    if section in ("mlp_ln", "mlp"):
        n += 2 * attention
        return k, n if section == "mlp_ln" else i * per["mlp"] + (n + per["mlp_ln"])
    n += {"ln": 0, "pair": per["ln"], "last": per["ln"] + (PAIRS - 1) * per["pair"]}[section]
    return k, a * attention + i * per[section] + n


def stage_3(nc, dram, consts):
    ident, cols = consts["ident"], consts["cols"]

    with ExitStack() as ctx:
        def sb(name, shape, dt=F32):
            return ctx.enter_context(nc.sbuf_tensor(name, shape, dt))

        def sem(name):
            return ctx.enter_context(nc.semaphore(name))

        X = sb("X3", [P, B, D])
        hT = sb("hT3", [P, 2, KC, B * P], F32R)
        ctxT = sb("ctxT3", [P, 2, KC, B * P], F32R)
        qT = sb("qT3", [P, 2, B * P])
        kT = sb("kT3", [P, 2, B * P])
        v = sb("v3", [P, 2, B, P])
        oT = sb("oT3", [P, 2, 2, B * P], F32R)
        probs = sb("probs3", [P, 2, BANK])
        probsT = sb("probsT3", [P, BANK])
        rawmax = sb("rawmax3", [P, 2, NB])
        negmax = sb("negmax3", [P, 2, NB])
        sums = sb("sums3", [P, 2, NB])
        learned = sb("learned3", [P, 2, NB])
        totals = sb("totals3", [P, 2, NB])
        rsums = sb("rsums3", [P, 2, NB])
        raw_qk = sb("raw_qk3", [P, 2, 2 * KC * P])
        raw_v = sb("raw_v3", [P, KC * 2 * P])
        raw_o = sb("raw_o3", [P, 2 * D])
        w_qk = sb("w_qk3", [P, 2, 2, 2 * KC * P], F32R)
        w_v = sb("w_v3", [P, 2, KC * 2 * P], F32R)
        w_o = sb("w_o3", [P, 2, 2 * D], F32R)
        raw_vrows = sb("raw_vrows3", [P, 2, 2 * P])
        vrow = sb("vrow3", [P, 2 * P])
        hcols = sb("hcols3", [P, 2 * NH * HCOLS])
        rows = sb("rows_b", [P, len(ROWS_B), D])
        stats = sb("stats3", [P, B, 6])
        mv = sb("mv3", [P, B, 2])
        var = sb("var3", [P, B])
        guess = sb("guess3", [P, B], I32)
        rstd = sb("rstd3", [P, B])
        shift = sb("shift3", [P, B])
        newton = sb("newton3", [P, B])

        xhat = qT[:, :, :].rearrange("p h r -> p (h r)").rearrange("p (b n) -> p b n", b=B)
        raw_hT = kT[:, 1, :].rearrange("p (i c r) -> p i c r", i=2, c=KC)
        raw_ctxT = v[:, :, :, :].rearrange("p h b k -> p h (b k)")
        raw_up = v[:, 0, :, :].rearrange("p b k -> p (b k)")
        raw_down = v[:, 1, :, :].rearrange("p b k -> p (b k)")
        w_up = ctxT[:, :, 0, :].rearrange("p s (c n) -> p s c n", c=KC)
        w_down = ctxT[:, :, 1, :].rearrange("p s (f n) -> p s f n", f=FC)
        gelu = qT[:, :, :].rearrange("p h r -> p (h r)").rearrange("p (f r) -> p f r", f=FC)
        upT = oT[:, :, :, :].rearrange("p s h r -> p s (h r)").rearrange("p s (f r) -> p s f r", f=FC)

        def bank(name):
            return ctx.enter_context(nc.psum_tensor(name, [P, BANK], F32))

        scores = [bank(f"scores3_{i}") for i in range(2)]
        pT_psum = bank("pT_psum3")
        o_psum = bank("o_psum3")
        general = [bank(f"general3_{i}") for i in range(NGEN)]

        s = {n: sem(n + "3") for n in (
            "raw_qk0_loaded", "raw_qk1_loaded", "raw_v_loaded", "raw_o_loaded", "raw_up_loaded", "raw_down_loaded",
            "vectors_loaded", "stored",
            "hi_done", "vrow_ready", "qk0_ready", "qk1_ready", "wv_ready", "wo_ready", "w_up_ready", "w_down_hi", "w_down_ready",
            "ctxT_hi", "ctxT_ready", "xb_ready", "norm_step", "norm_ready", "xhat_dve", "xhat_act",
            "hT_hi", "hT_ready",
            "scores_ready", "max_step", "max_ready", "exp_done", "rsum_step", "rsum_ready", "probs_ready", "pT_ready", "pT_copied",
            "o_ready", "o_hi", "o_lo", "upT_hi", "upT_ready", "upT_late", "wait_passed")}
        x_loaded = [sem(f"x_loaded3_{g}") for g in range(G)]
        ctxT_loaded = [sem(f"ctxT_loaded3_{g}") for g in range(G)]
        full = [sem(f"general_full3_{i}") for i in range(NGEN)]
        free = [sem(f"general_free3_{i}") for i in range(NGEN)]

        def wait_full(eng, *at):
            k, n = bank_count(*at)
            eng.wait_ge(full[k], n + 2)
            return general[k], free[k]

        def wait_full_apart(eng, *at):
            k, n = bank_count(*at)
            eng.wait_ge(full[k], n + 2)
            eng.sem_inc(s["wait_passed"], 1)
            return general[k], free[k]

        def wait_free(eng, *at):
            k, n = bank_count(*at)
            eng.wait_ge(free[k], n + 1)
            return general[k], full[k]

        def wait_copied(eng, *at):
            k, n = bank_count(*at)
            eng.wait_ge(free[k], n + 2)

        def pair_section(last):
            return "last" if last else "pair"

        def quarter(g):
            return slice(g * R, (g + 1) * R)

        def qk_parts(head):
            return lambda part: w_qk[:, head, part, :]

        def v_parts(part):
            return w_v[:, part, :]

        def o_parts(part):
            return w_o[:, part, :]

        with nc.Block() as block:

            @block.sync
            def _(sp):
                def load_qk(pair, head):
                    sp.dma_start(raw_qk[:, head, :], dram["w_qk"][bass.ds(pair, 1), :, head, :].rearrange("a p n -> p (a n)")).then_inc(s[f"raw_qk{head}_loaded"], 16)

                def load_v(pair):
                    sp.dma_start(raw_v[:, :], dram["w_v"][bass.ds(pair, 1), :, :].rearrange("a p n -> p (a n)")).then_inc(s["raw_v_loaded"], 16)
                    sp.dma_start(raw_vrows[:, :, :].rearrange("p j n -> p (j n)"), dram["vrows"][bass.ds(pair, 1), :].rearrange("a n -> (a n)").partition_broadcast(P)).then_inc(s["raw_v_loaded"], 16)

                def load_o(pair):
                    sp.dma_start(raw_o[:, :], dram["w_o"][bass.ds(pair, 1), :, :].rearrange("a p n -> p (a n)")).then_inc(s["raw_o_loaded"], 16)

                load_qk(0, 0)
                for g in range(0, G, 2):
                    sp.dma_start(X[:, NB * g:NB * g + NB, :], dram["mid"][:, NB * g:NB * g + NB, :]).then_inc(x_loaded[g], 16)
                load_qk(0, 1)
                load_v(0)
                load_o(0)

                def next_weights(pair, following, more):
                    sp.wait_ge(s["qk0_ready"], pair + 2)
                    load_qk(following, 0)
                    sp.wait_ge(s["wv_ready"], pair + 2)
                    sp.wait_ge(s["vrow_ready"], pair + 2)
                    load_v(following)
                    sp.wait_ge(s["qk1_ready"], pair + 2)
                    load_qk(following, 1)
                    if more:
                        sp.wait_ge(s["wo_ready"], pair + 2)
                        load_o(following)

                with sp.Fori(0, 2 * PAIRS - 1) as i:
                    next_weights(i, i + 1, True)
                next_weights(2 * PAIRS - 1, 0, False)
                sp.wait_ge(s["o_ready"], 2 * ATT_UNITS - STEPS + G + 1)
                sp.dma_start(raw_up, dram["w_up"]).then_inc(s["raw_up_loaded"], 16)
                sp.wait_ge(s["o_ready"], 2 * ATT_UNITS + 1)
                sp.dma_start(raw_down, dram["w_down"]).then_inc(s["raw_down_loaded"], 16)

            @block.gpsimd
            def _(pool):
                seed(pool, [s["vrow_ready"], s["qk0_ready"], s["qk1_ready"], s["wv_ready"], s["wo_ready"],
                            s["xb_ready"], s["probs_ready"], s["hT_ready"], s["upT_ready"]])

                def split_lo(parts, raw, his, ready):
                    pool.wait_ge(s["hi_done"], his + 1)
                    nc.gpsimd.tensor_tensor(parts(LO), raw, parts(HI), ALU.subtract).then_inc(s[ready], 1)

                def value_rows(loads):
                    pool.wait_ge(s["raw_v_loaded"], loads)
                    nc.gpsimd.tensor_tensor(vrow[:, :], raw_vrows[:, 0, :], raw_vrows[:, 1, :], ALU.subtract).then_inc(s["vrow_ready"], 1)

                split_lo(qk_parts(0), raw_qk[:, 0, :], 1, "qk0_ready")
                value_rows(32)
                split_lo(v_parts, raw_v[:, :], 2, "wv_ready")
                split_lo(qk_parts(1), raw_qk[:, 1, :], 3, "qk1_ready")

                def split_h(a, g):
                    pool.wait_ge(s["hT_hi"], a * G + g + 2)
                    nc.gpsimd.tensor_tensor(hT[:, LO, :, quarter(g)], raw_hT[:, g % 2, :, :], hT[:, HI, :, quarter(g)], ALU.subtract).then_inc(s["hT_ready"], 1)

                def pair(a, i, last):
                    pair_index = a * PAIRS + i
                    his = pair_index * 4 + 3
                    for t in range(STEPS):
                        n = a * ATT_UNITS + i * STEPS + t
                        pr = probs[:, t % 2, :].rearrange("p (b k) -> p b k", b=NB)
                        pool.wait_ge(s["rsum_ready"], n + 2)
                        nc.gpsimd.tensor_tensor(pr, pr, rsums[:, t % 2, :].unsqueeze(2).broadcast_to([P, NB, P]), ALU.mult).then_inc(s["probs_ready"], 1)
                        if t == 0:
                            split_lo(qk_parts(0), raw_qk[:, 0, :], his + 1, "qk0_ready")
                        elif t == 1:
                            split_lo(o_parts, raw_o[:, :], his + 2, "wo_ready")
                        elif t == G:
                            value_rows(pair_index * 32 + 64)
                            split_lo(v_parts, raw_v[:, :], his + 3, "wv_ready")
                        elif t == G + 2:
                            split_lo(qk_parts(1), raw_qk[:, 1, :], his + 4, "qk1_ready")
                        if last and t < G:
                            for j in range(2):
                                wait_copied(pool, "pair", a, PAIRS - 2, ("out", t, j))
                            pool.sem_inc(s["wait_passed"], 1)
                            x = X[:, NB * t:NB * t + NB, :]
                            nc.gpsimd.tensor_tensor(x, x, rows[:, bass.ds(a, 1), :].broadcast_to([P, NB, D]), ALU.add).then_inc(s["xb_ready"], 1)

                with pool.Fori(0, 2) as a:
                    for g in range(G):
                        split_h(a, g)
                    with pool.Fori(0, PAIRS - 1) as i:
                        pair(a, i, False)
                    pair(a, PAIRS - 1, True)
                pool.wait_ge(s["hi_done"], 2 * PAIRS * 4 + 5)
                nc.gpsimd.tensor_tensor(w_up[:, LO, :, :].rearrange("p c n -> p (c n)"), raw_up, w_up[:, HI, :, :].rearrange("p c n -> p (c n)"), ALU.subtract).then_inc(s["w_up_ready"], 1)
                for g in range(G):
                    split_h(2, g)
                with pool.Fori(0, G) as g:
                    for f in range(FC - LATE):
                        pool.wait_ge(s["upT_hi"], g * FC + f + 2)
                        nc.gpsimd.tensor_tensor(upT[:, LO, f, :], gelu[:, f, :], upT[:, HI, f, :], ALU.subtract).then_inc(s["upT_ready"], 1)
                    x = X[:, bass.ds(g * NB, NB), :]
                    nc.gpsimd.tensor_tensor(x, x, rows[:, 2:3, :].broadcast_to([P, NB, D]), ALU.add).then_inc(s["xb_ready"], 1)
                    for j in range(2):
                        wait_copied(pool, "mlp", 0, g, ("down", j))
                        x = bass.ds(g * NB + 2 * j, 2)
                        pool.dma_start(dram["out"][x, :, :].rearrange("b p n -> p b n"), X[:, x, :]).then_inc(s["stored"], 16)
                pool.wait_ge(s["stored"], 2 * 16 * G)

            @block.scalar
            def _(act):
                seed(act, [s["exp_done"], s["pT_copied"], s["o_hi"], s["hi_done"], s["xhat_act"], s["hT_hi"]])
                for g in range(1, G, 2):
                    act.dma_start(X[:, NB * g:NB * g + NB, :], dram["mid"][:, NB * g:NB * g + NB, :]).then_inc(x_loaded[g], 16)
                for g in range(G):
                    act.dma_start(raw_ctxT[:, :, quarter(g)], dram["ctxT"][:, :, NB * g:NB * g + NB, :].rearrange("p c b k -> p c (b k)")).then_inc(ctxT_loaded[g], 16)
                act.dma_start(hcols[:, :], dram["hcols"]).then_inc(s["vectors_loaded"], 16)
                act.dma_start(rows[:, :, :], dram["rows_b"].partition_broadcast(P)).then_inc(s["vectors_loaded"], 16)

                def split_hi(name, loads, parts, raw):
                    act.wait_ge(s[name], loads)
                    nc.scalar.copy(parts(HI), raw).then_inc(s["hi_done"], 1)

                split_hi("raw_qk0_loaded", 16, qk_parts(0), raw_qk[:, 0, :])
                for g in range(G):
                    act.wait_ge(ctxT_loaded[g], 16)
                    nc.scalar.copy(ctxT[:, HI, :, quarter(g)], raw_ctxT[:, :, quarter(g)]).then_inc(s["ctxT_hi"], 1)
                split_hi("raw_v_loaded", 32, v_parts, raw_v[:, :])
                split_hi("raw_qk1_loaded", 16, qk_parts(1), raw_qk[:, 1, :])
                act.wait_ge(s["vectors_loaded"], 32)

                def xhat_rows(a, g):
                    act.wait_ge(s["norm_ready"], a * 2 + 3)
                    act.sem_inc(s["wait_passed"], 1)
                    for b in (NB * g + 1, NB * g + 3):
                        nc.scalar.activation(xhat[:, b, :], X[:, b, :], ACT.Identity, scale=rstd[:, b:b + 1], bias=shift[:, b:b + 1]).then_inc(s["xhat_act"], 1)

                def norm_copies(section, a, g, at):
                    if g >= 2:
                        act.wait_ge(s["hT_ready"], a * G + g)
                    src, freed = wait_full_apart(act, section, a, 0, ("ln", g, 1))
                    nc.scalar.activation(raw_hT[:, g % 2, 1, :], src[:, :], ACT.Identity, scale=cols[:, bass.ds(at + 1, 1)], bias=cols[:, bass.ds(at + 3, 1)]).then_inc(freed, 1)
                    for c in range(KC):
                        wait_copied(act, section, a, 0, ("ln", g, c))
                    nc.scalar.copy(hT[:, HI, :, quarter(g)], raw_hT[:, g % 2, :, :]).then_inc(s["hT_hi"], 1)

                def norm(section, a, at):
                    xhat_rows(a, 0)
                    xhat_rows(a, 1)
                    for g in range(G):
                        norm_copies(section, a, g, at)
                        if g + 2 < G:
                            xhat_rows(a, g + 2)
                        if section == "ln" and g > 0:
                            copy_q(section, a, 0, g - 1, 0, 0)

                def copy_q(section, a, i, t, head, pair):
                    src, freed = wait_full_apart(act, section, a, i, ("q", t))
                    at = a * (NH * HCOLS) + pair * (2 * HCOLS) + head * HCOLS
                    nc.scalar.activation(qT[:, head, quarter(t % G)], src[:, :], ACT.Identity, bias=hcols[:, bass.ds(at, 1)]).then_inc(freed, 1)

                def exps(n, t):
                    act.wait_ge(s["max_ready"], n + 2)
                    act.wait_ge(s["pT_ready"], n if t > 0 else n + 1)
                    for b in range(NB):
                        nc.scalar.activation(probs[:, t % 2, b * P:(b + 1) * P], scores[t % 2][:, b * P:(b + 1) * P], ACT.Exp,
                                             bias=negmax[:, t % 2, b:b + 1], scale=SCALE3, accum_out=sums[:, t % 2, b:b + 1])
                    nc.scalar.activation(learned[:, t % 2, :], negmax[:, t % 2, :], ACT.Exp).then_inc(s["exp_done"], 1)

                def copy_pT(n):
                    act.wait_ge(s["pT_ready"], n + 2)
                    act.wait_ge(s["o_ready"], n + 1)
                    nc.scalar.copy(probsT[:, :], pT_psum[:, :]).then_inc(s["pT_copied"], 1)

                def copy_o(a, i, n, t):
                    head = t // G
                    at = a * (NH * HCOLS) + i * (2 * HCOLS) + head * HCOLS + 3
                    act.wait_ge(s["o_ready"], n + 2)
                    act.sem_inc(s["wait_passed"], 1)
                    nc.scalar.activation(oT[:, HI, head, quarter(t % G)], o_psum[:, :], ACT.Identity, bias=hcols[:, bass.ds(at, 1)]).then_inc(s["o_hi"], 1)

                def pair(a, i, last):
                    section, loop = pair_section(last), 0 if last else i
                    for t in range(STEPS):
                        n = a * ATT_UNITS + i * STEPS + t
                        if t > 0:
                            copy_o(a, i, n - 1, t - 1)
                        exps(n, t)
                        pair_index = a * PAIRS + i
                        if t == 0:
                            split_hi("raw_qk0_loaded", pair_index * 16 + 32, qk_parts(0), raw_qk[:, 0, :])
                        elif t == 1:
                            split_hi("raw_o_loaded", pair_index * 16 + 16, o_parts, raw_o[:, :])
                        elif t == G:
                            split_hi("raw_v_loaded", pair_index * 32 + 64, v_parts, raw_v[:, :])
                        elif t == G + 2:
                            split_hi("raw_qk1_loaded", pair_index * 16 + 32, qk_parts(1), raw_qk[:, 1, :])
                        for key in pair_work(last)[t]:
                            if key[0] == "q" and key[1] < G:
                                copy_q(section, a, loop, key[1], 1, i)
                            elif key[0] == "q":
                                copy_q(section, a, loop, key[1], 0, i + 1)
                        copy_pT(n)
                    copy_o(a, i, n, STEPS - 1)

                with act.Fori(0, 2) as a:
                    norm("ln", a, a * 4 + COLS["lnA_s"][0])
                    copy_q("ln", a, 0, G - 1, 0, 0)
                    with act.Fori(0, PAIRS - 1) as i:
                        pair(a, i, False)
                    pair(a, PAIRS - 1, True)
                act.wait_ge(s["raw_up_loaded"], 16)
                wait_full(act, "last", 1, 0, ("v", G - 1, 1))
                nc.scalar.copy(w_up[:, HI, :, :].rearrange("p c n -> p (c n)"), raw_up).then_inc(s["hi_done"], 1)
                norm("mlp_ln", 2, COLS["lnM_s"][0])
                with act.Fori(0, G) as g:
                    for f in range(FC):
                        src, freed = wait_full(act, "mlp", 0, g, ("up", f))
                        at = COLS["mlp3_b"][0] + f
                        nc.scalar.activation(gelu[:, f, :], src[:, :], ACT.Gelu, bias=cols[:, at:at + 1]).then_inc(freed, 1)

            @block.vector
            def _(dve):
                seed(dve, [s["norm_step"], s["norm_ready"], s["xhat_dve"], s["max_step"], s["max_ready"],
                           s["rsum_step"], s["rsum_ready"], s["o_lo"], s["upT_hi"], s["upT_late"]] + free)

                def row_stats(b):
                    nc.vector.bn_stats(stats[:, b, :], X[:, b, :]).then_inc(s["norm_step"], 1)

                def copy_k(section, a, i, t, head, pair):
                    src, freed = wait_full(dve, section, a, i, ("k", t))
                    at = a * (NH * HCOLS) + pair * (2 * HCOLS) + head * HCOLS
                    nc.vector.tensor_scalar(kT[:, head, quarter(t % G)], src[:, :], hcols[:, bass.ds(at + 1, 1)], hcols[:, bass.ds(at + 2, 1)],
                                            ALU.add, ALU.subtract).then_inc(freed, 1)

                def copy_v(section, a, i, t, j):
                    src, freed = wait_full(dve, section, a, i, ("v", t, j))
                    b = t * NB + 2 * j
                    nc.vector.tensor_tensor(v[:, :, b:b + 2, :].rearrange("p h b k -> p b h k"),
                                            src[:, :].rearrange("p (b h k) -> p b h k", b=2, h=2),
                                            vrow[:, :].rearrange("p (h k) -> p h k", h=2).unsqueeze(1).broadcast_to([P, 2, 2, P]), ALU.add).then_inc(freed, 1)

                def front(n, t):
                    dve.wait_ge(s["scores_ready"], n + 2)
                    nc.vector.tensor_reduce(rawmax[:, t % 2, :], scores[t % 2][:, :].rearrange("p (b k) -> p b k", b=NB),
                                            axis=AX.X, op=ALU.max, negate=True).then_inc(s["max_step"], 1)
                    dve.wait_ge(s["max_step"], n + 2)
                    nc.vector.tensor_scalar(negmax[:, t % 2, :], rawmax[:, t % 2, :], 0.0, SCALE3, ALU.min, ALU.mult).then_inc(s["max_ready"], 1)

                def rsum(n, t):
                    dve.wait_ge(s["exp_done"], n + 2)
                    dve.wait_ge(s["probs_ready"], n if t > 0 else n + 1)
                    nc.vector.tensor_tensor(totals[:, t % 2, :], sums[:, t % 2, :], learned[:, t % 2, :], ALU.add).then_inc(s["rsum_step"], 1)
                    dve.wait_ge(s["rsum_step"], n + 2)
                    nc.vector.reciprocal(rsums[:, t % 2, :], totals[:, t % 2, :]).then_inc(s["rsum_ready"], 1)

                def o_low(a, i, n, t):
                    head = t // G
                    at = a * (NH * HCOLS) + i * (2 * HCOLS) + head * HCOLS + 3
                    dve.wait_ge(s["o_hi"], n + 2)
                    nc.vector.scalar_tensor_tensor(out=oT[:, LO, head, quarter(t % G)], in0=o_psum[:, :], scalar=hcols[:, bass.ds(at, 1)],
                                                   in1=oT[:, HI, head, quarter(t % G)], op0=ALU.add, op1=ALU.subtract).then_inc(s["o_lo"], 1)

                def add_out(section, a, i, q, j):
                    src, freed = wait_full(dve, section, a, i, ("out", q, j))
                    x = X[:, NB * q + 2 * j:NB * q + 2 * j + 2, :]
                    nc.vector.tensor_tensor(x, src[:, :].rearrange("p (b n) -> p b n", b=2), x, ALU.add).then_inc(freed, 1)
                    if section == "last":
                        wait_copied(dve, section, a, i, ("out", q, j))
                        for b in (NB * q + 2 * j, NB * q + 2 * j + 1):
                            row_stats(b)

                def pair(a, i, last):
                    section, loop = pair_section(last), 0 if last else i
                    for t in range(STEPS):
                        n = a * ATT_UNITS + i * STEPS + t
                        if t > 0:
                            front(n, t)
                            o_low(a, i, n - 1, t - 1)
                        rsum(n, t)
                        if t == 0:
                            dve.wait_ge(s["vrow_ready"], a * PAIRS + i + 2)
                        if last and t == G:
                            dve.wait_ge(s["xb_ready"], a * G + G + 1)
                        for key in pair_work(last)[t]:
                            if key[0] == "k" and key[1] < G:
                                copy_k(section, a, loop, key[1], 1, i)
                            elif key[0] == "k":
                                copy_k(section, a, loop, key[1], 0, i + 1)
                            elif key[0] == "v":
                                copy_v(section, a, loop, key[1], key[2])
                            elif key[0] == "out":
                                add_out(section, a, loop, key[1], key[2])
                    add_out(section, a, loop, G - 2, 1)
                    o_low(a, i, n, STEPS - 1)
                    if not last:
                        front(n + 1, 0)
                    for j in range(2):
                        add_out(section, a, loop, G - 1, j)

                def norm_factors(a):
                    count = [B]
                    base = a * NORM_STEPS3 + 1

                    def step(ins):
                        count[0] += 1
                        ins.then_inc(s["norm_step"], 1)

                    dve.wait_ge(s["norm_step"], base + count[0])
                    dve.sem_inc(s["wait_passed"], 1)
                    for b in range(B):
                        step(nc.vector.bn_aggr(mv[:, b, :], stats[:, b, :]))
                    dve.wait_ge(s["norm_step"], base + count[0])
                    step(nc.vector.tensor_scalar(var[:, :], mv[:, :, 1], 1e-5, None, ALU.add))
                    dve.wait_ge(s["norm_step"], base + count[0])
                    step(nc.vector.tensor_single_scalar(guess[:, :], var[:, :].bitcast(I32), 1, ALU.logical_shift_right))
                    dve.wait_ge(s["norm_step"], base + count[0])
                    step(nc.vector.tensor_scalar(guess[:, :], guess[:, :], -1.0, RSQRT_MAGIC, ALU.mult, ALU.add))
                    y = guess[:, :].bitcast(F32)
                    for i in range(NEWTON_STEPS):
                        dve.wait_ge(s["norm_step"], base + count[0])
                        step(nc.vector.scalar_tensor_tensor(out=newton[:, :], in0=y, scalar=-0.5, in1=y, op0=ALU.mult, op1=ALU.mult))
                        dve.wait_ge(s["norm_step"], base + count[0])
                        step(nc.vector.tensor_tensor(newton[:, :], newton[:, :], var[:, :], ALU.mult))
                        dve.wait_ge(s["norm_step"], base + count[0])
                        ins = nc.vector.scalar_tensor_tensor(out=rstd[:, :], in0=newton[:, :], scalar=1.5, in1=y, op0=ALU.add, op1=ALU.mult)
                        if i == NEWTON_STEPS - 1:
                            ins.then_inc(s["norm_ready"], 1)
                        else:
                            step(ins)
                        y = rstd[:, :]
                    dve.wait_ge(s["norm_ready"], a * 2 + 2)
                    nc.vector.scalar_tensor_tensor(out=shift[:, :], in0=mv[:, :, 0], scalar=-1.0, in1=rstd[:, :], op0=ALU.mult, op1=ALU.mult).then_inc(s["norm_ready"], 1)
                    assert count[0] == NORM_STEPS3

                def norm(section, a, at):
                    dve.wait_ge(s["norm_ready"], a * 2 + 3)
                    xhat_rows(0)
                    xhat_rows(1)
                    for g in range(G):
                        if g >= 2:
                            dve.wait_ge(s["hT_ready"], a * G + g)
                        src, freed = wait_full(dve, section, a, 0, ("ln", g, 0))
                        nc.vector.tensor_scalar(raw_hT[:, g % 2, 0, :], src[:, :], cols[:, bass.ds(at, 1)], cols[:, bass.ds(at + 2, 1)], ALU.mult, ALU.add).then_inc(freed, 1)
                        if g + 2 < G:
                            xhat_rows(g + 2)
                        if section == "ln" and g > 0:
                            for t in ((0, 1) if g == 1 else (g,)):
                                copy_k(section, a, 0, t, 0, 0)

                def xhat_rows(g):
                    for b in (NB * g, NB * g + 2):
                        nc.vector.tensor_scalar(xhat[:, b, :], X[:, b, :], mv[:, b, 0:1], rstd[:, b:b + 1], ALU.subtract, ALU.mult).then_inc(s["xhat_dve"], 1)

                for g in range(G):
                    dve.wait_ge(x_loaded[g], 16)
                    for b in range(NB * g, NB * g + NB):
                        row_stats(b)
                norm_factors(0)
                for g in range(G):
                    dve.wait_ge(s["ctxT_hi"], g + 1)
                    nc.vector.tensor_tensor(ctxT[:, LO, :, quarter(g)], raw_ctxT[:, :, quarter(g)], ctxT[:, HI, :, quarter(g)], ALU.subtract).then_inc(s["ctxT_ready"], 1)
                dve.wait_ge(s["vectors_loaded"], 32)
                dve.wait_ge(s["ctxT_ready"], G)
                with dve.Fori(0, 2) as a:
                    norm("ln", a, a * 4 + COLS["lnA_s"][0])
                    dve.wait_ge(s["hT_ready"], a * G + G + 1)
                    front(a * ATT_UNITS, 0)
                    with dve.Fori(0, PAIRS - 1) as i:
                        pair(a, i, False)
                    pair(a, PAIRS - 1, True)
                    norm_factors(a + 1)
                norm("mlp_ln", 2, COLS["lnM_s"][0])
                down = [w_down[:, part, :, :].rearrange("p f n -> p (f n)") for part in (HI, LO)]
                dve.wait_ge(s["raw_down_loaded"], 16)
                nc.vector.tensor_copy(down[HI], raw_down).then_inc(s["w_down_hi"], 1)
                dve.wait_ge(s["w_down_hi"], 1)
                nc.vector.tensor_tensor(down[LO], raw_down, down[HI], ALU.subtract).then_inc(s["w_down_ready"], 1)
                with dve.Fori(0, G) as g:
                    for f in range(FC):
                        wait_copied(dve, "mlp", 0, g, ("up", f))
                        nc.vector.tensor_copy(upT[:, HI, f, :], gelu[:, f, :]).then_inc(s["upT_hi"], 1)
                        if f >= FC - LATE:
                            dve.wait_ge(s["upT_hi"], g * FC + f + 2)
                            nc.vector.tensor_tensor(upT[:, LO, f, :], gelu[:, f, :], upT[:, HI, f, :], ALU.subtract).then_inc(s["upT_late"], 1)
                    dve.wait_ge(s["xb_ready"], 2 * G + g + 2)
                    for j in range(2):
                        src, freed = wait_full(dve, "mlp", 0, g, ("down", j))
                        x = X[:, bass.ds(g * NB + 2 * j, 2), :]
                        nc.vector.tensor_tensor(x, src[:, :].rearrange("p (b n) -> p b n", b=2), x, ALU.add).then_inc(freed, 1)

            @block.tensor
            def _(pe):
                seed(pe, [s["scores_ready"], s["pT_ready"], s["o_ready"]] + full)

                def split_matmul(out, stationary, moving):
                    terms = [(a, b, c) for c in range(KC) for a, b in PASSES]
                    for i, (a, b, c) in enumerate(terms):
                        last = nc.tensor.matmul(out, stationary(a, c), moving(b, c), start=(i == 0), stop=(i == len(terms) - 1))
                    return last

                def transposed(section, a, g):
                    for c in range(KC):
                        out, filled = wait_free(pe, section, a, 0, ("ln", g, c))
                        if c == 0:
                            pe.wait_ge(s["xhat_dve"], a * (B // 2) + 2 * g + 3)
                            pe.wait_ge(s["xhat_act"], a * (B // 2) + 2 * g + 3)
                        for b in range(NB):
                            last = nc.tensor.transpose(out[:, b * P:(b + 1) * P], xhat[:, g * NB + b, c * P:(c + 1) * P], ident[:, :])
                        last.then_inc(filled, 1)

                def queries(section, a, i, t, head):
                    out, filled = wait_free(pe, section, a, i, ("q", t))
                    split_matmul(out[:, :], lambda part, c: w_qk[:, head, part, c * P:(c + 1) * P],
                                 lambda part, c: hT[:, part, c, quarter(t % G)]).then_inc(filled, 1)

                def keys(section, a, i, t, head):
                    out, filled = wait_free(pe, section, a, i, ("k", t))
                    split_matmul(out[:, :], lambda part, c: w_qk[:, head, part, (KC + c) * P:(KC + c + 1) * P],
                                 lambda part, c: ctxT[:, part, c, quarter(t % G)]).then_inc(filled, 1)

                def values(section, a, i, t, half):
                    out, filled = wait_free(pe, section, a, i, ("v", t, half))
                    for j in range(2):
                        b = t * NB + 2 * half + j
                        last = split_matmul(out[:, j * 2 * P:(j + 1) * 2 * P], lambda part, c: ctxT[:, part, c, b * P:(b + 1) * P],
                                            lambda part, c: w_v[:, part, c * 2 * P:(c + 1) * 2 * P])
                    last.then_inc(filled, 1)

                def score(t):
                    head = t // G
                    for j in range(NB):
                        b = (t % G) * NB + j
                        last = nc.tensor.matmul(scores[t % 2][:, j * P:(j + 1) * P], qT[:, head, b * P:(b + 1) * P], kT[:, head, b * P:(b + 1) * P], start=True, stop=True)
                    last.then_inc(s["scores_ready"], 1)

                def weigh_values(n, t, a, section, loop):
                    head = t // G
                    pe.wait_ge(s["pT_copied"], n + 2)
                    if head == 0:
                        for half in range(2):
                            wait_copied(pe, section, a, loop, ("v", t, half))
                    pe.wait_ge(s["o_lo"], n + 1)
                    for j in range(NB):
                        last = nc.tensor.matmul(o_psum[:, j * P:(j + 1) * P], v[:, head, (t % G) * NB + j, :], probsT[:, j * P:(j + 1) * P], start=True, stop=True)
                    last.then_inc(s["o_ready"], 1)

                def output(section, a, loop, q, half):
                    out, filled = wait_free(pe, section, a, loop, ("out", q, half))
                    for j in range(2):
                        b = q * NB + 2 * half + j
                        last = split_matmul(out[:, j * D:(j + 1) * D], lambda part, head: oT[:, part, head, b * P:(b + 1) * P],
                                            lambda part, head: w_o[:, part, head * D:(head + 1) * D])
                    last.then_inc(filled, 1)

                def pair(a, i, last_pair):
                    section, loop = pair_section(last_pair), 0 if last_pair else i
                    weights = a * PAIRS + i + 2
                    for t in range(STEPS):
                        n = a * ATT_UNITS + i * STEPS + t
                        if t > 0:
                            if t >= G:
                                for name in ("q", "k"):
                                    wait_copied(pe, section, a, loop, (name, t - G))
                            pe.wait_ge(s["exp_done"], n)
                            score(t)
                            weigh_values(n - 1, t - 1, a, section, loop)
                        if t == 0:
                            pe.wait_ge(s["qk1_ready"], weights)
                            pe.wait_ge(s["wv_ready"], weights)
                        elif t == G and not last_pair:
                            pe.wait_ge(s["qk0_ready"], weights + 1)
                        elif t == G + 1:
                            pe.wait_ge(s["wo_ready"], weights)
                        for key in pair_work(last_pair)[t]:
                            if key[0] == "q":
                                queries(section, a, loop, key[1], 1 - key[1] // G)
                            elif key[0] == "k":
                                keys(section, a, loop, key[1], 1 - key[1] // G)
                            elif key[0] == "v":
                                values(section, a, loop, key[1], key[2])
                            else:
                                if key[2] == 0:
                                    pe.wait_ge(s["o_lo"], n + 1)
                                output(section, a, loop, key[1], key[2])
                        pe.wait_ge(s["probs_ready"], n + 2)
                        pe.wait_ge(s["pT_copied"], n + 1)
                        for j in range(NB):
                            last = nc.tensor.transpose(pT_psum[:, j * P:(j + 1) * P], probs[:, t % 2, j * P:(j + 1) * P], ident[:, :])
                        last.then_inc(s["pT_ready"], 1)
                    output(section, a, loop, G - 2, 1)
                    weigh_values(n, t, a, section, loop)
                    if not last_pair:
                        for t in range(G, STEPS):
                            for name in ("q", "k"):
                                wait_copied(pe, section, a, loop, (name, t))
                        pe.wait_ge(s["exp_done"], n + 1)
                        score(0)
                    pe.wait_ge(s["o_lo"], n + 2)
                    for half in range(2):
                        output(section, a, loop, G - 1, half)

                pe.wait_ge(s["ctxT_ready"], G)
                with pe.Fori(0, 2) as a:
                    for g in range(2):
                        transposed("ln", a, g)
                    pe.wait_ge(s["qk0_ready"], a * PAIRS + 2)
                    for g in range(2):
                        keys("ln", a, 0, g, 0)
                    for g in range(G):
                        pe.wait_ge(s["hT_ready"], a * G + g + 2)
                        queries("ln", a, 0, g, 0)
                        if g + 2 < G:
                            transposed("ln", a, g + 2)
                            keys("ln", a, 0, g + 2, 0)
                    for name, g in (("q", G - 2), ("q", G - 1), ("k", G - 1), ("ln", G - 1)):
                        wait_copied(pe, "ln", a, 0, (name, g, 1) if name == "ln" else (name, g))
                    pe.wait_ge(s["exp_done"], a * ATT_UNITS + 1)
                    score(0)
                    with pe.Fori(0, PAIRS - 1) as i:
                        pair(a, i, False)
                    pair(a, PAIRS - 1, True)
                for g in range(G):
                    transposed("mlp_ln", 2, g)
                pe.wait_ge(s["w_up_ready"], 1)
                with pe.Fori(0, G) as g:
                    pe.wait_ge(s["hT_ready"], g + (2 * G + 2))
                    for f in range(FC):
                        out, filled = wait_free(pe, "mlp", 0, g, ("up", f))
                        split_matmul(out[:, :], lambda part, c: w_up[:, part, c, f * P:(f + 1) * P],
                                     lambda part, c: hT[:, part, c, bass.ds(g * R, R)]).then_inc(filled, 1)
                    pe.wait_ge(s["w_down_ready"], 1)
                    for i in range(2):
                        out, filled = wait_free(pe, "mlp", 0, g, ("down", i))
                        for j in range(2):
                            b = 2 * i + j
                            for f in range(FC):
                                if b == 0:
                                    if f < FC - LATE:
                                        pe.wait_ge(s["upT_ready"], g * (FC - LATE) + f + 2)
                                    else:
                                        pe.wait_ge(s["upT_late"], g * LATE + (f - (FC - LATE) + 2))
                                for k, (up, down) in enumerate(PASSES):
                                    last = nc.tensor.matmul(out[:, j * D:(j + 1) * D], upT[:, up, f, b * P:(b + 1) * P], w_down[:, down, f, :],
                                                            start=(f == 0 and k == 0), stop=(f == FC - 1 and k == len(PASSES) - 1))
                        last.then_inc(filled, 1)


def chunked(w):
    k, n = w.shape
    return w.reshape(k // P, P, n).transpose(1, 0, 2).reshape(P, -1)


def columns(v):
    return v.reshape(-1, P).T


def by_pair(*matrices):
    stacked = np.stack([m.reshape(KC, P, PAIRS, 2, W3) for m in matrices])
    return stacked.transpose(3, 2, 4, 0, 1, 5).reshape(PAIRS, P, 2, -1)


def laid_out(x, ctx_2048, mask_1x1xSxS2_fc1, mask_Bx1xSxS2_ff1, mask_BxS2_ik0, **w):
    def padded(a, axis):
        widths = [(0, 0)] * a.ndim
        widths[axis] = (0, P - a.shape[axis])
        return np.pad(a, widths)

    l0, l1, l2, l3 = ("L0_xattn_", "L1_xattn_", "L2_xattn_", "L3_xattn_")
    qkv, b_qkv = w[l1 + "w_qkv"], w[l1 + "b_qkv"]
    kv, b_kv = w[l1 + "w_kv"], w[l1 + "b_kv"]
    lat_kv, b_lat_kv = w[l2 + "kv_w"], w[l2 + "kv_b"]
    weights = {
        "wq0": padded(w[l0 + "Wq"].T, 1), "wk0": padded(w[l0 + "Wk"].T, 1), "wv0": w[l0 + "Wv"].T,
        "self_q": qkv[:, 0:D], "self_k": qkv[:, D:2 * D], "self_v": qkv[:, 2 * D:3 * D], "self_o": w[l1 + "w_ao"],
        "cross_k": kv[:, 0:D], "cross_v": kv[:, D:2 * D], "cross_q": w[l1 + "w_q"], "cross_o": w[l1 + "w_co"],
        "mlp1_up": w[l1 + "w1"], "mlp1_down": w[l1 + "w2"],
        "lat_q": w[l2 + "q_w"], "lat_k": lat_kv[:, 0::2], "lat_v": lat_kv[:, 1::2], "lat_o": w[l2 + "out_w"],
        "mlp2_up": w[l2 + "mlp_w1"], "mlp2_down": w[l2 + "mlp_w2"],
    }
    vectors = {
        "bq0": padded(w[l0 + "bq"], 0), "bk0": padded(w[l0 + "bk"], 0), "bv0": w[l0 + "bv"],
        "ln1_s": w[l1 + "ln1_s"], "ln1_b": w[l1 + "ln1_b"], "ln2_s": w[l1 + "ln2_s"], "ln2_b": w[l1 + "ln2_b"],
        "ln3_s": w[l1 + "ln3_s"], "ln3_b": w[l1 + "ln3_b"],
        "self_bq": b_qkv[0:D], "self_bk": b_qkv[D:2 * D], "self_bv": b_qkv[2 * D:3 * D],
        "cross_bq": w[l1 + "b_q"], "cross_bk": b_kv[0:D], "cross_bv": b_kv[D:2 * D], "mlp1_b": w[l1 + "b1"],
        "lat_bq": w[l2 + "q_b"], "lat_bk": b_lat_kv[0::2], "lat_bv": b_lat_kv[1::2], "rms_w": w[l2 + "postnorm_w"],
        "mlp2_b": w[l2 + "mlp_b1"],
        "lnA_s": w[l3 + "ln1_scale"], "lnA_b": w[l3 + "ln1_offset"], "lnB_s": w[l3 + "ln2_scale"], "lnB_b": w[l3 + "ln2_offset"],
        "lnM_s": w[l3 + "ln_mlp_scale"], "lnM_b": w[l3 + "ln_mlp_offset"], "mlp3_b": w[l3 + "b_fc1"],
    }
    head_mask = np.repeat(np.eye(HPC, dtype=np.float32), HD, axis=0)
    return {
        "x": x, "ctx": ctx_2048,
        "ctxT": np.ascontiguousarray(ctx_2048.reshape(B, P, KC, P).transpose(3, 2, 0, 1)),
        "mask_self": mask_1x1xSxS2_fc1[0, 0], "mask_cross": mask_Bx1xSxS2_ff1[:, 0], "mask_lat": mask_BxS2_ik0,
        "ident": np.eye(P, dtype=np.float32),
        "cols": np.concatenate([columns(vectors[n]) if n in vectors else head_mask for n in COLS], axis=1),
        "weights_a": np.concatenate([chunked(weights[n]) for n, _, _ in WEIGHTS_A], axis=1),
        "rows_a": np.stack([w[l1 + "b_ao"], w[l1 + "b_co"], w[l1 + "b2"], w[l2 + "out_b"], w[l2 + "mlp_b2"]]),
        "rows_b": np.stack([w[l3 + "bo1"], w[l3 + "bo2"], w[l3 + "b_fc2"]]),
        "w_qk": np.concatenate([by_pair(w[l3 + f"wq{a}"], w[l3 + f"wk{a}"]) for a in (1, 2)]),
        "w_v": np.concatenate([w[l3 + f"wv{a}"].reshape(KC, P, PAIRS, 2 * W3).transpose(2, 1, 0, 3).reshape(PAIRS, P, -1) for a in (1, 2)]),
        "w_o": np.concatenate([w[l3 + f"wo{a}"].reshape(PAIRS, 2, P, D).transpose(0, 2, 1, 3).reshape(PAIRS, P, 2 * D) for a in (1, 2)]),
        "hcols": np.concatenate([np.stack([w[l3 + f"{n}{a}"].reshape(NH, P) for n in ("bq", "bk", "bias_k", "bias_v")], axis=1)
                                 for a in (1, 2)]).reshape(2 * NH * HCOLS, P).T,
        "vrows": np.stack([np.concatenate([w[l3 + f"{n}{a}"].reshape(PAIRS, 2 * W3) for a in (1, 2)]) for n in ("bv", "bias_v")],
                          axis=1).reshape(2 * PAIRS, -1),
        "w_up": chunked(w[l3 + "w_fc1"]), "w_down": chunked(w[l3 + "w_fc2"]),
    }


def build(nc, dram):
    with ExitStack() as ctx:
        consts = {
            "ident": ctx.enter_context(nc.sbuf_tensor("ident", [P, P], F32)),
            "cols": ctx.enter_context(nc.sbuf_tensor("cols", [P, NCOLS], F32)),
            "loaded": ctx.enter_context(nc.semaphore("consts_loaded")),
        }
        stages_0_to_2(nc, dram, consts)
        stage_3(nc, dram, consts)


def kernel(**inputs):
    import concourse.bacc as bacc
    from concourse.bass_utils import run_bass_kernel_spmd

    arrays = laid_out(**{name: np.asarray(a) for name, a in inputs.items()})
    arrays = {name: np.ascontiguousarray(a) for name, a in arrays.items()}
    nc = bacc.Bacc("TRN2", target_bir_lowering=False, num_devices=1)
    dram = {name: nc.dram_tensor(name + "_dram", a.shape, mybir.dt.from_np(a.dtype), kind="ExternalInput").ap()
            for name, a in arrays.items()}
    dram["mid"] = nc.dram_tensor("mid_dram", (P, B, D), F32, kind="Internal").ap()
    dram["out"] = nc.dram_tensor("out_dram", (B, P, D), F32, kind="ExternalOutput").ap()
    build(nc, dram)
    result = run_bass_kernel_spmd(nc, [{name + "_dram": a for name, a in arrays.items()}], core_ids=[0])
    return result.results[0]["out_dram"]
```
